# Optimizing a Trainium2 kernel written in Bass

```python
import numpy as np
import jax
import jax.numpy as jnp

def _softmax(x, axis=-1):
    return jax.nn.softmax(x, axis=axis)

def _gelu(x):
    return jax.nn.gelu(x, approximate=True)

def _silu(x):
    return jax.nn.silu(x)

def _sigmoid(x):
    return jax.nn.sigmoid(x)

def _layernorm(x, axis=-1, eps=1e-05):
    m = jnp.mean(x, axis=axis, keepdims=True)
    v = jnp.var(x, axis=axis, keepdims=True)
    return (x - m) / jnp.sqrt(v + eps)

def _scatter_add(tgt, idx, src, axis=0):
    return tgt.at[idx].add(src)

def _segment_sum(src, seg, n):
    return jax.ops.segment_sum(src, seg, n)
kernel_name = 'mk_decoder_postln_d2_seqx_r4_9b6bd0'

def setup_inputs(seed: int=0):
    np.random.seed(seed)
    _w = jnp.asarray

    def _rec_inputs():
        import jax
        import jax.numpy as jnp
        _rk = jax.random.key(seed)
        x = -0.0003929 + 0.9999 * jax.random.normal(jax.random.fold_in(_rk, 1), (16, 112, 1024), jnp.float32)
        _lenS = 112 - jax.random.randint(jax.random.fold_in(_rk, 7), (16,), 0, max(1, 112 // 4) + 1, jnp.int32)
        _lenS2 = 375 - jax.random.randint(jax.random.fold_in(_rk, 8), (16,), 0, max(1, 375 // 4) + 1, jnp.int32)
        _ctx_1024P = jax.random.normal(jax.random.fold_in(_rk, 11), (16, 16, 256), jnp.float32)
        _ctx_1024c = jax.random.dirichlet(jax.random.fold_in(_rk, 511), 0.3 * jnp.ones((16,), jnp.float32), (16, 375))
        _ctx_1024t = jnp.einsum('bsk,bkd->bsd', _ctx_1024c, _ctx_1024P)
        _ctx_1024t = _ctx_1024t * jax.lax.rsqrt(jnp.mean(jnp.square(_ctx_1024t)) + 1e-12) * 0.953939
        ctx_1024 = -1.39393e-06 + 0.999914 * (_ctx_1024t + 0.3 * jax.random.normal(jax.random.fold_in(_rk, 611), (16, 375, 256), jnp.float32))
        _validS = jnp.arange(112)[None, :] < _lenS[:, None]
        _validS2 = jnp.arange(375)[None, :] < _lenS2[:, None]
        _causal = jnp.tril(jnp.ones((112, 112), dtype=bool))
        mask_SxS2_ff0 = jnp.where(jnp.ones((112, 375), dtype=bool), 0.0, -1000000000.0).astype(jnp.float32)
        return (x, ctx_1024, mask_SxS2_ff0)
    x, ctx_1024, mask_SxS2_ff0 = _rec_inputs()

    def _L0_attn_setup():
        import jax, jax.numpy as jnp
        import numpy as np
        BH = 32
        BW = 32
        key = jax.random.key(seed)
        k1, k2, k3, k4 = jax.random.split(key, 4)
        B, S, K, N = (2, 512, 1024, 1024)
        data = jax.random.normal(k1, (B, S, K), dtype=jnp.float32)
        weight = jax.random.normal(k2, (N, K), dtype=jnp.float32) * 0.02
        bias = jax.random.normal(k3, (N,), dtype=jnp.float32) * 0.02
        Nb, Kb = (N // BH, K // BW)
        block_on = jax.random.uniform(k4, (Nb, Kb)) < 0.3
        mask = jnp.repeat(jnp.repeat(block_on, BH, axis=0), BW, axis=1).astype(jnp.int32)
        return {'data': data, 'mask': mask, 'weight': weight, 'bias': bias}
    _L0_attn_all = _L0_attn_setup()
    _L0_attn_in = {k: v for k, v in _L0_attn_all.items() if k in ('mask', 'weight', 'bias')}
    del _L0_attn_all

    def _L0_xattn_setup():
        import math
        import jax, jax.numpy as jnp
        import numpy as np
        N_HEADS = 32
        N_KV_HEADS = 8
        N_REP = N_HEADS // N_KV_HEADS
        HEAD_DIM = 1024 // N_HEADS
        key = jax.random.key(seed)
        kq, kk, kv = jax.random.split(key, 3)
        B, S, T = (2, 512, 512)
        q = jax.random.normal(kq, (B, S, N_HEADS * HEAD_DIM), dtype=jnp.float32)
        k = jax.random.normal(kk, (B, T, N_KV_HEADS * HEAD_DIM), dtype=jnp.float32)
        v = jax.random.normal(kv, (B, T, N_KV_HEADS * HEAD_DIM), dtype=jnp.float32)
        mask = jnp.zeros((S, T), dtype=jnp.float32)
        return {'q': q, 'k': k, 'v': v, 'start_pos': 0, 'mask': mask}
    _L0_xattn_all = _L0_xattn_setup()
    _L0_xattn_in = {k: v for k, v in _L0_xattn_all.items() if k in ()}
    del _L0_xattn_all

    def _L0_ffn_setup():
        import jax, jax.numpy as jnp
        import numpy as np
        HID, BOT, RDIM, NSLOT, K, VB = (1024, 64, 48, 256, 8, 64)
        TAU_LOW, TAU_HIGH, EARLY_EXIT = (0.5, 2.0, 0.05)

        def _uncertainty(h, Wu1, bu1, Wu2, bu2):
            var = jnp.var(h, axis=-1)
            log_var = jnp.log1p(var)
            norm_var = log_var / (jnp.mean(log_var) + 1e-06)
            learned = (jax.nn.gelu(h @ Wu1.T + bu1) @ Wu2.T + bu2)[..., 0]
            return jnp.clip(norm_var * 0.5 + jax.nn.sigmoid(learned) * 2.5, 0.0, 5.0)
        key = jax.random.key(seed)
        ks = jax.random.split(key, 12)
        B, S = (2, 512)
        return {'hidden_states': jax.random.normal(ks[0], (B, S, HID), dtype=jnp.float32), 'Wq': jax.random.normal(ks[1], (BOT, HID), dtype=jnp.float32) / np.sqrt(HID), 'Wr': jax.random.normal(ks[2], (RDIM, BOT), dtype=jnp.float32) / np.sqrt(BOT), 'aux_keys': jax.random.normal(ks[3], (NSLOT, BOT), dtype=jnp.float32) * 0.01, 'aux_values': jax.random.normal(ks[4], (NSLOT, HID), dtype=jnp.float32) * 0.02, 'Wvd': jax.random.normal(ks[5], (VB, HID), dtype=jnp.float32) * 0.1 / np.sqrt(HID), 'Wvu': jax.random.normal(ks[6], (HID, VB), dtype=jnp.float32) * 0.1 / np.sqrt(VB), 'Wu1': jax.random.normal(ks[7], (HID // 4, HID), dtype=jnp.float32) / np.sqrt(HID), 'bu1': jnp.zeros((HID // 4,), dtype=jnp.float32), 'Wu2': jax.random.normal(ks[8], (1, HID // 4), dtype=jnp.float32) * 0.01, 'bu2': jnp.zeros((1,), dtype=jnp.float32), 'gate_w1': jnp.float32(0.5), 'gate_bias': jnp.float32(-1.0), 'log_rel': jnp.zeros((NSLOT,), dtype=jnp.float32)}
    _L0_ffn_all = _L0_ffn_setup()
    _L0_ffn_in = {k: v for k, v in _L0_ffn_all.items() if k in ('Wq', 'Wr', 'aux_keys', 'aux_values', 'Wvd', 'Wvu', 'Wu1', 'bu1', 'Wu2', 'bu2', 'gate_w1', 'gate_bias', 'log_rel')}
    del _L0_ffn_all

    def _L1_attn_setup():
        import jax, jax.numpy as jnp
        import numpy as np
        SEQ, BATCH, HIDDEN = (512, 1, 1024)
        NUM_HEADS, NUM_KV_HEADS, HEAD_DIM = (32, 8, 128)
        Q_PER_GROUP = NUM_HEADS // NUM_KV_HEADS
        TOTAL_PROJ = NUM_KV_HEADS * (Q_PER_GROUP + 2) * HEAD_DIM
        key = jax.random.key(seed)
        k1, k2, k3 = jax.random.split(key, 3)
        tokens = jax.random.normal(k1, (SEQ, BATCH, HIDDEN), dtype=jnp.float32)
        weight_qkv = jax.random.normal(k2, (TOTAL_PROJ, HIDDEN), dtype=jnp.float32) * (2.0 / (TOTAL_PROJ + HIDDEN)) ** 0.5
        weight_proj = jax.random.normal(k3, (HIDDEN, NUM_HEADS * HEAD_DIM), dtype=jnp.float32) * (2.0 / (HIDDEN + NUM_HEADS * HEAD_DIM)) ** 0.5
        return {'tokens': tokens, 'weight_qkv': weight_qkv, 'weight_proj': weight_proj}
    _L1_attn_all = _L1_attn_setup()
    _L1_attn_in = {k: v for k, v in _L1_attn_all.items() if k in ('weight_qkv', 'weight_proj')}
    del _L1_attn_all

    def _L1_xattn_setup():
        import math
        import jax, jax.numpy as jnp
        import numpy as np
        N_HEADS = 32
        N_KV_HEADS = 8
        N_REP = N_HEADS // N_KV_HEADS
        HEAD_DIM = 1024 // N_HEADS
        key = jax.random.key(seed)
        kq, kk, kv = jax.random.split(key, 3)
        B, S, T = (2, 512, 512)
        q = jax.random.normal(kq, (B, S, N_HEADS * HEAD_DIM), dtype=jnp.float32)
        k = jax.random.normal(kk, (B, T, N_KV_HEADS * HEAD_DIM), dtype=jnp.float32)
        v = jax.random.normal(kv, (B, T, N_KV_HEADS * HEAD_DIM), dtype=jnp.float32)
        mask = jnp.zeros((S, T), dtype=jnp.float32)
        return {'q': q, 'k': k, 'v': v, 'start_pos': 0, 'mask': mask}
    _L1_xattn_all = _L1_xattn_setup()
    _L1_xattn_in = {k: v for k, v in _L1_xattn_all.items() if k in ()}
    del _L1_xattn_all

    def _L1_ffn_setup():
        import jax, jax.numpy as jnp
        import numpy as np
        IN_F = 1024
        OUT_F = 1024
        RANK = 8
        NUM_EXPERTS = 64
        TOP_K = 16
        ROUTER_DIM = 16
        ALPHA = 32
        SCALING = ALPHA / TOP_K
        BOTTLENECK = NUM_EXPERTS * RANK
        key = jax.random.key(seed)
        ks = jax.random.split(key, 5)
        x = jax.random.normal(ks[0], (4, 1024, IN_F), dtype=jnp.float32)
        bound_a = float(np.sqrt(6.0 / IN_F))
        A_w = jax.random.uniform(ks[1], (BOTTLENECK, IN_F), jnp.float32, -bound_a, bound_a)
        B_w = jax.random.normal(ks[2], (OUT_F, BOTTLENECK), dtype=jnp.float32) * 0.02
        Wq_w = jax.random.normal(ks[3], (ROUTER_DIM, IN_F), dtype=jnp.float32) * 0.02
        keys = jax.random.normal(ks[4], (NUM_EXPERTS, ROUTER_DIM), dtype=jnp.float32) * 0.01
        return {'x': x, 'A_w': A_w, 'B_w': B_w, 'Wq_w': Wq_w, 'keys': keys}
    _L1_ffn_all = _L1_ffn_setup()
    _L1_ffn_in = {k: v for k, v in _L1_ffn_all.items() if k in ('A_w', 'B_w', 'Wq_w', 'keys')}
    del _L1_ffn_all
    return {'x': x, 'ctx_1024': ctx_1024, 'mask_SxS2_ff0': mask_SxS2_ff0, 'L0_attn_mask': _L0_attn_in['mask'], 'L0_attn_weight': _L0_attn_in['weight'], 'L0_attn_bias': _L0_attn_in['bias'], 'L0_ffn_Wq': _L0_ffn_in['Wq'], 'L0_ffn_Wr': _L0_ffn_in['Wr'], 'L0_ffn_aux_keys': _L0_ffn_in['aux_keys'], 'L0_ffn_aux_values': _L0_ffn_in['aux_values'], 'L0_ffn_Wvd': _L0_ffn_in['Wvd'], 'L0_ffn_Wvu': _L0_ffn_in['Wvu'], 'L0_ffn_Wu1': _L0_ffn_in['Wu1'], 'L0_ffn_bu1': _L0_ffn_in['bu1'], 'L0_ffn_Wu2': _L0_ffn_in['Wu2'], 'L0_ffn_bu2': _L0_ffn_in['bu2'], 'L0_ffn_gate_w1': _L0_ffn_in['gate_w1'], 'L0_ffn_gate_bias': _L0_ffn_in['gate_bias'], 'L0_ffn_log_rel': _L0_ffn_in['log_rel'], 'L1_attn_weight_qkv': _L1_attn_in['weight_qkv'], 'L1_attn_weight_proj': _L1_attn_in['weight_proj'], 'L1_ffn_A_w': _L1_ffn_in['A_w'], 'L1_ffn_B_w': _L1_ffn_in['B_w'], 'L1_ffn_Wq_w': _L1_ffn_in['Wq_w'], 'L1_ffn_keys': _L1_ffn_in['keys']}

def reference(x, ctx_1024, mask_SxS2_ff0, L0_attn_mask, L0_attn_weight, L0_attn_bias, L0_ffn_Wq, L0_ffn_Wr, L0_ffn_aux_keys, L0_ffn_aux_values, L0_ffn_Wvd, L0_ffn_Wvu, L0_ffn_Wu1, L0_ffn_bu1, L0_ffn_Wu2, L0_ffn_bu2, L0_ffn_gate_w1, L0_ffn_gate_bias, L0_ffn_log_rel, L1_attn_weight_qkv, L1_attn_weight_proj, L1_ffn_A_w, L1_ffn_B_w, L1_ffn_Wq_w, L1_ffn_keys):
    import jax
    import jax.numpy as jnp

    def _L0_attn_ref(data, mask, weight, bias):
        import jax, jax.numpy as jnp
        import numpy as np
        BH = 32
        BW = 32
        N, K = weight.shape
        Nb, Kb = (N // BH, K // BW)
        bm = mask.reshape(Nb, BH, Kb, BW).sum(axis=(1, 3)) > 0
        wb = weight.reshape(Nb, BH, Kb, BW) * bm[:, None, :, None].astype(weight.dtype)
        w = wb.reshape(N, K)
        out = jnp.einsum('bsk,nk->bsn', data, w) + bias
        return out

    def _L0_xattn_ref(q, k, v, start_pos, mask):
        import math
        import jax, jax.numpy as jnp
        import numpy as np
        N_HEADS = 32
        N_KV_HEADS = 8
        N_REP = N_HEADS // N_KV_HEADS
        HEAD_DIM = 1024 // N_HEADS
        b, s, _ = q.shape
        t = k.shape[1]
        xq = q.reshape(b, s, N_KV_HEADS, N_REP, HEAD_DIM)
        xk = k.reshape(b, t, N_KV_HEADS, HEAD_DIM)
        xv = v.reshape(b, t, N_KV_HEADS, HEAD_DIM)
        scores = jnp.einsum('bsgrd,btgd->bgrst', xq, xk) / math.sqrt(HEAD_DIM)
        scores = scores + mask
        probs = jax.nn.softmax(scores.astype(jnp.float32), axis=-1).astype(q.dtype)
        out = jnp.einsum('bgrst,btgd->bsgrd', probs, xv)
        return out.reshape(b, s, N_HEADS * HEAD_DIM)

    def _L0_ffn_ref(hidden_states, Wq, Wr, aux_keys, aux_values, Wvd, Wvu, Wu1, bu1, Wu2, bu2, gate_w1, gate_bias, log_rel):
        import jax, jax.numpy as jnp
        import numpy as np
        HID, BOT, RDIM, NSLOT, K, VB = (1024, 64, 48, 256, 8, 64)
        TAU_LOW, TAU_HIGH, EARLY_EXIT = (0.5, 2.0, 0.05)

        def _uncertainty(h, Wu1, bu1, Wu2, bu2):
            var = jnp.var(h, axis=-1)
            log_var = jnp.log1p(var)
            norm_var = log_var / (jnp.mean(log_var) + 1e-06)
            learned = (jax.nn.gelu(h @ Wu1.T + bu1) @ Wu2.T + bu2)[..., 0]
            return jnp.clip(norm_var * 0.5 + jax.nn.sigmoid(learned) * 2.5, 0.0, 5.0)
        query = hidden_states @ Wq.T
        rq = query @ Wr.T
        rk = aux_keys @ Wr.T
        router_scores = jnp.einsum('bsr,nr->bsn', rq, rk) / np.sqrt(RDIM) + log_rel
        top_scores, top_idx = jax.lax.top_k(router_scores, K)
        sel_keys = aux_keys[top_idx]
        attn = jnp.einsum('bsd,bskd->bsk', query, sel_keys) / np.sqrt(BOT) + log_rel[top_idx]
        w = jax.nn.softmax(attn, axis=-1)
        sel_vals = aux_values[top_idx]
        aux_out = jnp.einsum('bsk,bskh->bsh', w, sel_vals)
        aux_out = aux_out @ Wvd.T @ Wvu.T
        u = _uncertainty(hidden_states, Wu1, bu1, Wu2, bu2)
        u_norm = jnp.clip((u - TAU_LOW) / (TAU_HIGH - TAU_LOW), 0.0, 1.0)
        gate = jax.nn.sigmoid(gate_w1 * u_norm + gate_bias)
        gate = jnp.where(gate < EARLY_EXIT, 0.0, gate)
        return hidden_states + gate[..., None] * aux_out

    def _L1_attn_ref(tokens, weight_qkv, weight_proj):
        import jax, jax.numpy as jnp
        import numpy as np
        SEQ, BATCH, HIDDEN = (512, 1, 1024)
        NUM_HEADS, NUM_KV_HEADS, HEAD_DIM = (32, 8, 128)
        Q_PER_GROUP = NUM_HEADS // NUM_KV_HEADS
        TOTAL_PROJ = NUM_KV_HEADS * (Q_PER_GROUP + 2) * HEAD_DIM
        S, B, H = tokens.shape
        scale = 1.0 / HEAD_DIM ** 0.5
        qkv = jnp.einsum('sbh,ph->sbp', tokens, weight_qkv)
        qkv = qkv.reshape(S, B, NUM_KV_HEADS, Q_PER_GROUP + 2, HEAD_DIM)
        q = qkv[:, :, :, :Q_PER_GROUP, :].reshape(S, B, NUM_HEADS, HEAD_DIM)
        k = qkv[:, :, :, Q_PER_GROUP, :]
        v = qkv[:, :, :, Q_PER_GROUP + 1, :]
        k = jnp.repeat(k, Q_PER_GROUP, axis=2)
        v = jnp.repeat(v, Q_PER_GROUP, axis=2)
        q = q.transpose(1, 2, 0, 3)
        k = k.transpose(1, 2, 0, 3)
        v = v.transpose(1, 2, 0, 3)
        scores = jnp.einsum('bhsd,bhtd->bhst', q, k) * scale
        causal = jnp.tril(jnp.ones((S, S), dtype=bool))
        scores = jnp.where(causal, scores, jnp.finfo(scores.dtype).min)
        attn = jax.nn.softmax(scores, axis=-1)
        out = jnp.einsum('bhst,bhtd->bhsd', attn, v)
        out = out.transpose(2, 0, 1, 3).reshape(S, B, NUM_HEADS * HEAD_DIM)
        return jnp.einsum('sbe,he->sbh', out, weight_proj)

    def _L1_xattn_ref(q, k, v, start_pos, mask):
        import math
        import jax, jax.numpy as jnp
        import numpy as np
        N_HEADS = 32
        N_KV_HEADS = 8
        N_REP = N_HEADS // N_KV_HEADS
        HEAD_DIM = 1024 // N_HEADS
        b, s, _ = q.shape
        t = k.shape[1]
        xq = q.reshape(b, s, N_KV_HEADS, N_REP, HEAD_DIM)
        xk = k.reshape(b, t, N_KV_HEADS, HEAD_DIM)
        xv = v.reshape(b, t, N_KV_HEADS, HEAD_DIM)
        scores = jnp.einsum('bsgrd,btgd->bgrst', xq, xk) / math.sqrt(HEAD_DIM)
        scores = scores + mask
        probs = jax.nn.softmax(scores.astype(jnp.float32), axis=-1).astype(q.dtype)
        out = jnp.einsum('bgrst,btgd->bsgrd', probs, xv)
        return out.reshape(b, s, N_HEADS * HEAD_DIM)

    def _L1_ffn_ref(x, A_w, B_w, Wq_w, keys):
        import jax, jax.numpy as jnp
        import numpy as np
        IN_F = 1024
        OUT_F = 1024
        RANK = 8
        NUM_EXPERTS = 64
        TOP_K = 16
        ROUTER_DIM = 16
        ALPHA = 32
        SCALING = ALPHA / TOP_K
        BOTTLENECK = NUM_EXPERTS * RANK
        q = jnp.einsum('bsd,rd->bsr', x, Wq_w)
        scores = jnp.einsum('bsr,er->bse', q, keys)
        top_vals, top_idx = jax.lax.top_k(scores, TOP_K)
        top_w = jax.nn.softmax(top_vals, axis=-1)
        gate = jnp.sum(jax.nn.one_hot(top_idx, NUM_EXPERTS, dtype=top_w.dtype) * top_w[..., None], axis=-2)
        z = jnp.einsum('bsd,nd->bsn', x, A_w)
        z = z.reshape(*z.shape[:-1], NUM_EXPERTS, RANK)
        z_gated = (z * gate[..., None]).reshape(*z.shape[:-2], BOTTLENECK)
        out = jnp.einsum('bsn,on->bso', z_gated, B_w) * SCALING
        return out
    x = _layernorm(x + _L0_attn_ref(x, L0_attn_mask, L0_attn_weight, L0_attn_bias), axis=-1)
    x = _layernorm(x + _L0_xattn_ref(x, ctx_1024, ctx_1024, 0, mask_SxS2_ff0), axis=-1)
    x = _layernorm(x + _L0_ffn_ref(x, L0_ffn_Wq, L0_ffn_Wr, L0_ffn_aux_keys, L0_ffn_aux_values, L0_ffn_Wvd, L0_ffn_Wvu, L0_ffn_Wu1, L0_ffn_bu1, L0_ffn_Wu2, L0_ffn_bu2, L0_ffn_gate_w1, L0_ffn_gate_bias, L0_ffn_log_rel), axis=-1)
    x = _layernorm(x + _L1_attn_ref(x, L1_attn_weight_qkv, L1_attn_weight_proj), axis=-1)
    x = _layernorm(x + _L1_xattn_ref(x, ctx_1024, ctx_1024, 0, mask_SxS2_ff0), axis=-1)
    x = _layernorm(x + _L1_ffn_ref(x, L1_ffn_A_w, L1_ffn_B_w, L1_ffn_Wq_w, L1_ffn_keys), axis=-1)
    return x

_drawn_inputs = setup_inputs


def setup_inputs(seed=0):
    import zlib

    import numpy as np

    out = dict(_drawn_inputs(seed))
    spreads = {'mask_SxS2_ff0': (0.0, 0.547), 'L0_ffn_bu1': (0.0, 2.0), 'L0_ffn_log_rel': (0.0, 2.0)}
    factors = {'L0_attn_bias': 3.27,
     'L0_ffn_Wq': 63.358,
     'L0_ffn_Wr': 64.0,
     'L0_ffn_aux_keys': 63.297,
     'L0_ffn_aux_values': 62.309,
     'L0_ffn_Wvd': 62.982,
     'L0_ffn_Wvu': 61.387,
     'L0_ffn_Wu1': 64.0,
     'L0_ffn_Wu2': 64.0}
    for name, (base, spread) in spreads.items():
        noise = np.random.default_rng([zlib.crc32(name.encode()), seed]).standard_normal(out[name].shape)
        drawn = base * np.exp(spread * noise) if base else spread * noise
        out[name] = jnp.asarray(drawn.astype(out[name].dtype))
    for name, factor in factors.items():
        out[name] = (out[name] * factor).astype(out[name].dtype)
    return out
```

```python
from contextlib import ExitStack

import numpy as np
import concourse.bass as bass
from concourse import mybir

F32 = mybir.dt.float32
F32R = mybir.dt.float32r
I32 = mybir.dt.int32
ALU = mybir.AluOpType
ACT = mybir.ActivationFunctionType
AX = mybir.AxisListType

P = 128
B, S, D = 16, 112, 1024
T, C = 375, 256
KT = D // P
HD = 32
NG, NR = 8, 4
NH = NG * NR
TC, TJ = 125, 3
TP = T + 1
EPS = 1e-5
BOT, SLOTS, UH = 64, 256, 256
ROW = 1096
COL_Z, COL_LEARNED, COL_VAR = D, D + BOT, D + BOT + 1
NE, RANK = 64, 8
BN = NE * RANK
HUGE = 3.0e38


class Counts:

    def __init__(self, eng):
        self.eng, self.counts = eng, {}

    def next(self, sem, n=1):
        total = self.counts.get(sem.name, (sem, 0))[1] + n
        self.counts[sem.name] = (sem, total)
        return total

    def take_off(self):
        for sem, total in self.counts.values():
            self.eng.sem_inc(sem, -total)
        self.counts = {}


def split_passes(hi_a, lo_a, hi_b, lo_b):
    return ((hi_a, hi_b), (hi_a, lo_b), (lo_a, hi_b))


def split_context(nc, ctxT, ks, sem):
    NB = 4
    with ExitStack() as ctx:
        raw = ctx.enter_context(nc.sbuf_tensor("ctx_raw", [P, 2, NB, T], F32))
        scaled = ctx.enter_context(nc.sbuf_tensor("ctx_scaled", [P, 2, NB, T], F32))
        hi = ctx.enter_context(nc.sbuf_tensor("ctx_hi", [P, 2, NB, T], F32R))
        lo = ctx.enter_context(nc.sbuf_tensor("ctx_lo", [P, 2, NB, T], F32R))
        loaded, scaled_ok, hi_ok, lo_ok, stored = (
            sem(f"split_{n}") for n in ("loaded", "scaled", "hi", "lo", "stored"))
        block = ctx.enter_context(nc.Block())
        src = ctxT.rearrange("(h p) b t -> p h b t", p=P)
        dst = [ks[part].rearrange("(h p) b t -> p h b t", p=P) for part in range(2)]

        @block.sync
        def _(sp):
            with sp.Fori(0, B // NB) as i:
                w = Counts(sp)
                for h in range(2):
                    sp.dma_start(raw[:, h], src[:, h, bass.ds(i * NB, NB), :]).then_inc(loaded, 16)
                sp.wait_ge(hi_ok, w.next(hi_ok))
                for h in range(2):
                    sp.dma_start(dst[0][:, h, bass.ds(i * NB, NB), :], hi[:, h].bitcast(F32)).then_inc(stored, 16)
                sp.wait_ge(lo_ok, w.next(lo_ok))
                for h in range(2):
                    sp.dma_start(dst[1][:, h, bass.ds(i * NB, NB), :], lo[:, h].bitcast(F32)).then_inc(stored, 16)
                sp.wait_ge(stored, w.next(stored, 64))
                w.take_off()

        @block.scalar
        def _(act):
            with act.Fori(0, B // NB) as i:
                w = Counts(act)
                act.wait_ge(loaded, w.next(loaded, 32))
                nc.scalar.mul(scaled[:], raw[:], -float(HD) ** -0.5).then_inc(scaled_ok, 1)
                w.take_off()

        @block.vector
        def _(dve):
            with dve.Fori(0, B // NB) as i:
                w = Counts(dve)
                dve.wait_ge(scaled_ok, w.next(scaled_ok))
                nc.vector.tensor_copy(hi[:], scaled[:]).then_inc(hi_ok, 1)
                dve.drain()
                nc.vector.tensor_tensor(lo[:], scaled[:], hi[:].bitcast(F32), ALU.subtract).then_inc(lo_ok, 1)
                w.take_off()


def token_stage(nc, layer, io, sem):
    first = layer == 0
    with ExitStack() as ctx:
        def sb(name, shape, dt=F32):
            return ctx.enter_context(nc.sbuf_tensor(f"L{layer}_{name}", shape, dt))

        def s(name):
            return sem(f"L{layer}_{name}")

        wide = ctx.enter_context(nc.psum_tensor(f"L{layer}_wide", [P, 2, 512], F32))
        scores = ctx.enter_context(nc.psum_tensor(f"L{layer}_scores", [P, 3, 512], F32))
        turned = ctx.enter_context(nc.psum_tensor(f"L{layer}_turned", [P, 2, 512], F32))

        ident = sb("ident", [P, P])
        nmask = sb("nmask", [P, T])
        xcur = sb("xcur", [P, D])
        row = sb("row", [P, ROW])
        attn = sb("attn", [P, D])
        tT_hi = sb("tT_hi", [P, KT, S], F32R)
        tT_lo = sb("tT_lo", [P, KT, S], F32R)
        qrep = sb("qrep", [P, NG, NR, S], F32R)
        krep = sb("krep", [P, NG, TP], F32R)
        val = sb("val", [TC, TJ, C])
        masked = sb("masked", [P, 3, T])
        probs = sb("probs", [P, 4, T])
        probsT = sb("probsT", [TC, 8, TJ, S])
        oT = sb("oT", [P, 8, S])
        least = sb("least", [P, NH])
        rsum = sb("rsum", [P, NH])
        rinv = sb("rinv", [P, NH])
        st = sb("st", [P, 12])
        mv = sb("mv", [P, 2])
        veps = sb("veps", [P, 1])
        rstd = sb("rstd", [P, 1])
        half = sb("half", [P, 1])

        ld_x, ld_xt, x_free, xt_free = s("ld_x"), s("ld_xt"), s("x_free"), s("xt_free")
        ld_k, ld_v, ld_q, k_free, v_free = s("ld_k"), s("ld_v"), s("ld_q"), s("k_free"), s("v_free")
        split_x, xb_ok, xb_used = s("split_x"), s("xb_ok"), s("xb_used")
        lin_ok, x_ok = s("lin"), s("x_ok")
        turn_ok, hi_ok, lo_ok, q_ok = s("turn"), s("hi"), s("lo"), s("q_ok")
        score_ok, least_ok, prob_ok = s("score"), s("least"), s("prob")
        turned_v, turned_s, copied_v, copied_s = s("turned_v"), s("turned_s"), s("copied_v"), s("copied_s")
        pv_s, pv_v, oT_s, oT_v = s("pv_s"), s("pv_v"), s("oT_s"), s("oT_v")
        attn_ok, x2_ok, var_ok, rstd_ok = s("attn"), s("x2"), s("var"), s("rstd")
        stored, tail_free = s("stored"), s("tail_free")

        if first:
            gate_h_ok, gelu_arg_ok, least_pen_ok, qaug_ok, queryT_ok = (s("gate_h_ok"), s("gelu_arg_ok"), s("least_pen_ok"), s("qaug_ok"), s("queryT_ok"))
            ra_ok, route_ok, row_ok, slotT_ok, slot_exp_ok = (s("ra_ok"), s("route_ok"), s("row_ok"), s("slotT_ok"), s("slot_exp_ok"))
            slot_w_ok, tanh_ok, wT_ok, z_ok = (s("slot_w_ok"), s("tanh_ok"), s("wT_ok"), s("z_ok"))
            w0_hi, w0_lo = sb("w0_hi", [P, KT, D], F32R), sb("w0_lo", [P, KT, D], F32R)
            xt = sb("xt", [P, KT, S])
            x_hi, x_lo = sb("x_hi", [P, KT, S], F32R), sb("x_lo", [P, KT, S], F32R)
            xb = sb("xb", [P, D])
            bias = sb("bias", [P, D])
            wu_hi, wu_lo = sb("wu_hi", [P, KT, UH], F32R), sb("wu_lo", [P, KT, UH], F32R)
            wq_hi, wq_lo = sb("wq_hi", [P, KT, BOT], F32R), sb("wq_lo", [P, KT, BOT], F32R)
            route = sb("route", [BOT + 1, 2 * SLOTS])
            u_val = sb("u_val", [P, 2, BOT])
            bu1, wu2, bu2 = sb("bu1", [P, UH]), sb("wu2", [P, UH]), sb("bu2", [P, 1])
            qaug = sb("qaug", [BOT + 1, S])
            ra = sb("ra", [P, 2 * SLOTS])
            top8 = sb("top8", [P, 8])
            left = sb("left", [P, SLOTS])
            pen = sb("pen", [P, SLOTS])
            slot_w = sb("slot_w", [P, SLOTS])
            sm = sb("sm", [P, 4])
            wT = sb("wT", [P, 2, S])
            ua, ub, uc = sb("ua", [P, UH]), sb("ub", [P, UH]), sb("uc", [P, UH])
        else:
            bottleneck_ok, egate_ok, gatedT_ok, gated_ok, out_ok = (s("bottleneck_ok"), s("egate_ok"), s("gatedT_ok"), s("gated_ok"), s("out_ok"))
            res_ok, rscore_ok, top_ok, z_hi_ok, z_lo_ok = (s("res_ok"), s("rscore_ok"), s("top_ok"), s("z_hi_ok"), s("z_lo_ok"))
            a_hi, a_lo = sb("a_hi", [P, KT, BN], F32R), sb("a_lo", [P, KT, BN], F32R)
            r_hi, r_lo = sb("r_hi", [P, KT, NE], F32R), sb("r_lo", [P, KT, NE], F32R)
            b_hi, b_lo = sb("b_hi", [P, 4, D], F32R), sb("b_lo", [P, 4, D], F32R)
            sc = sb("sc", [P, NE])
            sc1, sc2 = sb("sc1", [P, NE]), sb("sc2", [P, NE])
            top8, top16 = sb("top8", [P, 8]), sb("top16", [P, 8])
            egate = sb("egate", [P, NE])
            sel = sb("sel", [P, NE])
            sm = sb("sm", [P, 4])
            zg = sb("zg", [P, BN])
            z_hi, z_lo = sb("z_hi", [P, 4, S], F32R), sb("z_lo", [P, 4, S], F32R)
            res = sb("res", [P, D])

        once = ExitStack()

        def tmp(name, shape, dt=F32):
            return once.enter_context(nc.sbuf_tensor(f"L{layer}_once_{name}", shape, dt))

        NST = 2 if first else 4
        stage = tmp("stage", [P, NST, D])
        part_of = []
        if first:
            bmask = tmp("bmask", [P, 2, D], I32)
            brow = tmp("brow", [P, KT * 32])
            bm = tmp("bm", [P, KT, 32])
            blocks = tmp("blocks", [P, P])
            wr, wrT, keysT = tmp("wr", [48, BOT]), tmp("wrT", [BOT, 48]), tmp("keysT", [BOT, SLOTS])
            valT, wvdT = tmp("valT", [P, KT, SLOTS]), tmp("wvdT", [P, KT, BOT])
            rkT = tmp("rkT", [48, SLOTS])
            for k in range(KT):
                rows_k = slice(P * k, P * k + P)
                part_of.append((io["w0T"][rows_k], D, k, w0_hi[:, k, :], w0_lo[:, k, :]))
                part_of.append((io["wu1T"][rows_k], UH, None, wu_hi[:, k, :], wu_lo[:, k, :]))
                part_of.append((io["wqT"][rows_k], BOT, None, wq_hi[:, k, :], wq_lo[:, k, :]))
            small = [(blocks[:], io["blocks"]),
                     (wr[:], io["wr"]), (wrT[:], io["wrT"]), (keysT[:], io["keysT"]),
                     (valT[:], io["valuesT"].rearrange("(k p) n -> p k n", p=P)),
                     (wvdT[:], io["wvdT"].rearrange("(k p) n -> p k n", p=P)),
                     (route[BOT:BOT + 1, :], io["log_rel"]), (bias[:], io["b0"]), (bu1[:], io["bu1"]),
                     (wu2[:], io["wu2"]), (bu2[:], io["bu2"])]
        else:
            rq, rkeysT = tmp("rq", [16, D]), tmp("rkeysT", [16, NE])
            for k in range(KT):
                part_of.append((io["awT"][P * k:P * k + P], BN, None, a_hi[:, k, :], a_lo[:, k, :]))
            for k in range(4):
                part_of.append((io["bwT"][P * k:P * k + P], D, None, b_hi[:, k, :], b_lo[:, k, :]))
            small = [(rq[:], io["rq"]), (rkeysT[:], io["rkeysT"])]
        small += [(ident[:], io["ident"]), (nmask[0:S, :], io["mask"])]
        small_in, chunk_done, prep_pe, prep_dve = s("small_in"), s("chunk_done"), s("prep_pe"), s("prep_dve")
        chunk_in = [s(f"chunk_in{i}") for i in range(NST)]
        bmask_in, brow_ok = [s("bmask_in0"), s("bmask_in1")], s("brow_ok")
        prep = once.enter_context(nc.Block())

        @prep.sync
        def _(sp):
            for dst, src in small:
                sp.dma_start(dst, src).then_inc(small_in, 16)
            if first:
                for k in range(KT):
                    if k >= 2:
                        sp.wait_ge(brow_ok, k - 1)
                    sp.dma_start(bmask[:, k % 2, :], io["bmaskT"][P * k:P * k + P]).then_inc(bmask_in[k % 2], 16)
            for i, (src, cols, _, _, _) in enumerate(part_of):
                if i >= NST:
                    sp.wait_ge(chunk_done, i - NST + 1)
                sp.dma_start(stage[:, i % NST, 0:cols], src).then_inc(chunk_in[i % NST], 16)

        @prep.tensor
        def _(pe):
            pe.wait_ge(small_in, 16 * len(small))
            if first:
                pe.wait_ge(brow_ok, KT)
                pe.matmul(wide[:, 0, 0:KT * 32], blocks[:], brow[:], start=True, stop=True)
                pe.matmul(wide[0:48, 1, 0:SLOTS], wrT[:], keysT[:], start=True, stop=True)
                for j in range(2):
                    for k in range(KT):
                        mm = pe.matmul(scores[:, j, 0:BOT], valT[:, k, P * j:P * j + P], wvdT[:, k, :],
                                       start=(k == 0), stop=(k == KT - 1))
                mm.then_inc(prep_pe, 1)
                pe.wait_ge(prep_dve, 1)
                pe.matmul(scores[0:BOT, 2, 0:SLOTS], wr[:], rkT[:], start=True, stop=True).then_inc(prep_pe, 1)
            else:
                for k in range(KT):
                    mm = pe.matmul(wide[:, 0, NE * k:NE * k + NE], rq[:, P * k:P * k + P], rkeysT[:],
                                   start=True, stop=True)
                mm.then_inc(prep_pe, 1)

        @prep.vector
        def _(dve):
            v = nc.vector
            v.memset(half[:], -0.5)
            v.memset(row[:, COL_VAR + 1:ROW], 0.0)
            v.memset(krep[:, :, T:TP].bitcast(F32), 0.0)
            dve.wait_ge(small_in, 16 * len(small))
            v.tensor_scalar(nmask[0:S, :], nmask[0:S, :], -1.0, None, ALU.mult)
            if first:
                v.memset(qaug[BOT:BOT + 1, :], 1.0)
                for k in range(KT):
                    dve.wait_ge(bmask_in[k % 2], 16 * (k // 2 + 1))
                    v.tensor_reduce(brow[:, 32 * k:32 * k + 32],
                                    bmask[:, k % 2, :].rearrange("p (n j) -> p n j", j=32), AX.X, ALU.add).then_inc(brow_ok, 1)
                v.tensor_scalar(route[0:BOT, SLOTS:2 * SLOTS], keysT[:], BOT ** -0.5, None, ALU.mult)
                dve.wait_ge(prep_pe, 1)
                v.tensor_copy(rkT[:], wide[0:48, 1, 0:SLOTS]).then_inc(prep_dve, 1)
                v.tensor_scalar(bm[:], wide[:, 0, 0:KT * 32].rearrange("p (k n) -> p k n", k=KT), 0.0, None, ALU.is_gt)
                for j in range(2):
                    v.tensor_copy(u_val[:, j, :], scores[:, j, 0:BOT])
                dve.wait_ge(prep_pe, 2)
                v.tensor_scalar(route[0:BOT, 0:SLOTS], scores[0:BOT, 2, 0:SLOTS], 48 ** -0.5, None, ALU.mult)
            else:
                dve.wait_ge(prep_pe, 1)
                psum = wide[:, 0, :].rearrange("p (k e) -> p k e", k=KT)
                v.tensor_copy(r_hi[:], psum)
                dve.drain()
                v.tensor_tensor(r_lo[:], psum, r_hi[:].bitcast(F32), ALU.subtract)
            dve.drain()
            for i, (_, cols, k, hi, lo) in enumerate(part_of):
                raw = stage[:, i % NST, 0:cols]
                dve.wait_ge(chunk_in[i % NST], 16 * (i // NST + 1))
                if k is not None:
                    v.tensor_tensor(raw.rearrange("p (n j) -> p n j", j=32), raw.rearrange("p (n j) -> p n j", j=32),
                                    bm[:, k, :].unsqueeze(2).broadcast_to([P, 32, 32]), ALU.mult)
                    dve.drain()
                v.tensor_copy(hi, raw)
                dve.drain()
                v.tensor_tensor(lo, raw, hi.bitcast(F32), ALU.subtract).then_inc(chunk_done, 1)

        once.close()

        def slot_ffn_vector(dve, w):
            v = nc.vector
            for h in range(2):
                v.bn_stats(st[0:S, 6 * h:6 * h + 6], row[0:S, 512 * h:512 * h + 512])
            dve.drain()
            v.bn_aggr(mv[0:S, :], st[0:S, :])
            dve.wait_ge(gate_h_ok, w.next(gate_h_ok))
            v.tensor_tensor(ua[0:S, :], wide[0:S, 0, 0:UH], bu1[0:S, :], ALU.add)
            dve.drain()
            v.tensor_copy(row[0:S, COL_VAR:COL_VAR + 1], mv[0:S, 1:2])
            v.tensor_tensor(ub[0:S, :], ua[0:S, :], ua[0:S, :], ALU.mult)
            dve.drain()
            v.tensor_scalar(ub[0:S, :], ub[0:S, :], 0.044715, 1.0, ALU.mult, ALU.add)
            dve.drain()
            v.tensor_tensor(ub[0:S, :], ub[0:S, :], ua[0:S, :], ALU.mult).then_inc(gelu_arg_ok, 1)
            dve.wait_ge(ra_ok, w.next(ra_ok))
            v.max(top8[0:S, :], ra[0:S, 0:SLOTS])
            dve.drain()
            v.match_replace(out=left[0:S, :], in_to_replace=top8[0:S, :], in_values=ra[0:S, 0:SLOTS], imm_value=-HUGE)
            dve.drain()
            v.tensor_tensor(left[0:S, :], left[0:S, :], ra[0:S, 0:SLOTS], ALU.not_equal)
            dve.drain()
            v.tensor_scalar(left[0:S, :], left[0:S, :], HUGE, -HUGE, ALU.mult, ALU.add)
            dve.drain()
            v.tensor_tensor_reduce(out=pen[0:S, :], in0=ra[0:S, SLOTS:2 * SLOTS], in1=left[0:S, :], scale=1.0,
                                   scalar=-HUGE, op0=ALU.add, op1=ALU.max, accum_out=sm[0:S, 0:1])
            dve.drain()
            v.tensor_scalar(sm[0:S, 1:2], sm[0:S, 0:1], -1.0, None, ALU.mult).then_inc(least_pen_ok, 1)
            dve.wait_ge(tanh_ok, w.next(tanh_ok))
            v.tensor_scalar(uc[0:S, :], uc[0:S, :], 1.0, 0.5, ALU.add, ALU.mult)
            dve.drain()
            v.tensor_tensor(uc[0:S, :], uc[0:S, :], ua[0:S, :], ALU.mult)
            dve.drain()
            v.tensor_tensor(uc[0:S, :], uc[0:S, :], wu2[0:S, :], ALU.mult)
            dve.drain()
            v.tensor_reduce(sm[0:S, 3:4], uc[0:S, :], AX.X, ALU.add)
            dve.wait_ge(slot_exp_ok, w.next(slot_exp_ok))
            v.reciprocal(sm[0:S, 2:3], sm[0:S, 2:3])
            dve.drain()
            v.tensor_tensor(row[0:S, COL_LEARNED:COL_LEARNED + 1], sm[0:S, 3:4], bu2[0:S, :], ALU.add)
            v.tensor_scalar(slot_w[0:S, :], slot_w[0:S, :], sm[0:S, 2:3], None, ALU.mult).then_inc(slot_w_ok, 1)
            dve.wait_ge(z_ok, w.next(z_ok))
            v.tensor_copy(row[0:S, COL_Z:COL_Z + BOT], scores[0:S, 1, 0:BOT])
            dve.drain().then_inc(row_ok, 1)

        def routed_ffn_vector(dve, w):
            v = nc.vector
            dve.wait_ge(rscore_ok, w.next(rscore_ok))
            v.tensor_copy(sc[0:S, :], wide[0:S, 1, 0:NE])
            dve.drain()
            v.max(top8[0:S, :], sc[0:S, :])
            dve.drain()
            v.tensor_scalar(sm[0:S, 1:2], top8[0:S, 0:1], -1.0, None, ALU.mult).then_inc(top_ok, 1)
            v.match_replace(out=sc1[0:S, :], in_to_replace=top8[0:S, :], in_values=sc[0:S, :], imm_value=-HUGE)
            dve.drain()
            v.max(top16[0:S, :], sc1[0:S, :])
            dve.drain()
            v.match_replace(out=sc2[0:S, :], in_to_replace=top16[0:S, :], in_values=sc1[0:S, :], imm_value=-HUGE)
            dve.drain()
            v.tensor_tensor(sel[0:S, :], sc2[0:S, :], sc[0:S, :], ALU.not_equal)
            dve.drain()
            dve.wait_ge(egate_ok, w.next(egate_ok))
            v.tensor_tensor(sel[0:S, :], sel[0:S, :], egate[0:S, :], ALU.mult)
            dve.drain()
            v.tensor_reduce(sm[0:S, 2:3], sel[0:S, :], AX.X, ALU.add)
            dve.drain()
            v.reciprocal(sm[0:S, 2:3], sm[0:S, 2:3])
            dve.drain()
            v.tensor_scalar(sel[0:S, :], sel[0:S, :], sm[0:S, 2:3], None, ALU.mult)
            dve.drain()
            dve.wait_ge(bottleneck_ok, w.next(bottleneck_ok))
            v.tensor_tensor(zg[0:S, :].rearrange("p (e k) -> p e k", k=RANK),
                            wide[0:S, 0, :].rearrange("p (e k) -> p e k", k=RANK),
                            sel[0:S, :].unsqueeze(2).broadcast_to([S, NE, RANK]), ALU.mult).then_inc(gated_ok, 1)
            dve.wait_ge(z_hi_ok, w.next(z_hi_ok))
            v.tensor_tensor(z_lo[:, :, :], turned[:, 0, 0:4 * S].rearrange("p (j s) -> p j s", s=S),
                            z_hi[:, :, :].bitcast(F32), ALU.subtract).then_inc(z_lo_ok, 1)
            for h in range(2):
                dve.wait_ge(out_ok, w.next(out_ok))
                v.scalar_tensor_tensor(out=res[0:S, 512 * h:512 * h + 512], in0=wide[0:S, h, :], scalar=2.0,
                                       in1=row[0:S, 512 * h:512 * h + 512], op0=ALU.mult, op1=ALU.add)
            dve.drain().then_inc(tail_free, 1)
            norm(dve, w, res, res, res_ok)

        block = ctx.enter_context(nc.Block())

        @block.sync
        def _(sp):
            ks = io["ks"]
            with sp.Fori(0, B) as b:
                w = Counts(sp)
                if first:
                    sp.wait_ge(xt_free, w.next(xt_free))
                    sp.dma_start(xt[:], io["xT"].rearrange("(k p) b s -> p k b s", p=P)[:, :, b, :]).then_inc(ld_xt, 16)
                    sp.wait_ge(x_free, w.next(x_free))
                    sp.dma_start(xb[0:S, :], io["x"][b]).then_inc(ld_x, 16)
                else:
                    sp.wait_ge(x_free, w.next(x_free))
                    sp.dma_start(xcur[0:S, :], io["x4"][b]).then_inc(ld_x, 16)
                sp.wait_ge(k_free, w.next(k_free))
                for c in range(4):
                    src = ks[c % 2].rearrange("(g d) b t -> d g b t", d=HD)[:, :, b, :]
                    sp.dma_start(krep[HD * c:HD * c + HD, :, 0:T].bitcast(F32), src).then_inc(ld_k, 16)
                sp.wait_ge(v_free, w.next(v_free))
                sp.dma_start(val[:], io["ctx"].rearrange("b (j t) c -> b t j c", t=TC)[b]).then_inc(ld_v, 16)
                sp.wait_ge(q_ok, w.next(q_ok, 2))
                for c in range(4):
                    part = tT_hi if c < 2 else tT_lo
                    for r in range(NR):
                        sp.dma_start(qrep[HD * c:HD * c + HD, :, r, :].bitcast(F32),
                                     part[HD * r:HD * r + HD, :, :].bitcast(F32)).then_inc(ld_q, 16)
                w.take_off()

        @block.gpsimd
        def _(pool):
            def root(w):
                pool.wait_ge(var_ok, w.next(var_ok))
                nc.gpsimd.tensor_scalar(veps[0:S], mv[0:S, 1:2], EPS, None, ALU.add)
                pool.drain()
                nc.gpsimd.tensor_tensor(rstd[0:S], veps[0:S], half[0:S], ALU.pow).then_inc(rstd_ok, 1)

            if first:
                pool.sem_inc(xt_free, 1)
                pool.sem_inc(x_free, 1)
            with pool.Fori(0, B) as b:
                w = Counts(pool)
                if first:
                    pool.wait_ge(xb_used, w.next(xb_used))
                    pool.wait_ge(ld_xt, w.next(ld_xt, 16))
                    nc.gpsimd.tensor_copy(x_hi[:], xt[:])
                    pool.drain()
                    nc.gpsimd.tensor_tensor(x_lo[:], xt[:], x_hi[:].bitcast(F32), ALU.subtract).then_inc(split_x, 1)
                    pool.drain().then_inc(xt_free, 1)
                    pool.wait_ge(ld_x, w.next(ld_x, 16))
                    nc.gpsimd.tensor_tensor(xb[0:S], xb[0:S], bias[0:S], ALU.add).then_inc(xb_ok, 1)
                    root(w)
                root(w)
                if not first:
                    root(w)
                w.take_off()

        def norm(dve, w, src, dst, done):
            for h in range(2):
                nc.vector.bn_stats(st[0:S, 6 * h:6 * h + 6], src[0:S, 512 * h:512 * h + 512])
            dve.drain()
            nc.vector.bn_aggr(mv[0:S, :], st[0:S, :]).then_inc(var_ok, 1)
            dve.wait_ge(rstd_ok, w.next(rstd_ok))
            last = nc.vector.tensor_scalar(dst[0:S, 0:D], src[0:S, 0:D], mv[0:S, 0:1], rstd[0:S, 0:1],
                                           ALU.subtract, ALU.mult)
            last.then_inc(done, 1)

        @block.tensor
        def _(pe):
            def turn_tile(w, src, signal):
                for h in range(2):
                    for j in range(4):
                        k = 4 * h + j
                        mm = pe.transpose(wide[:, h, S * j:S * j + S], src[0:S, P * k:P * k + P], ident[0:S, 0:S])
                    mm.then_inc(signal, 1)

            def linear(out, hi, lo, w_hi, w_lo, cols, kt=KT):
                n = 0
                for k in range(kt):
                    for a, c in split_passes(hi, lo, w_hi, w_lo):
                        mm = pe.matmul(out, a[:, k, :], c[:, k, cols], start=(n == 0), stop=(n == 3 * kt - 1))
                        n += 1
                return mm

            def cross(w):
                pe.wait_ge(ld_q, w.next(ld_q, 16 * 16))
                pe.wait_ge(ld_k, w.next(ld_k, 16 * 4))
                for n in range(NH + 8):
                    if n < NH:
                        u, gi = divmod(n, 4)
                        gq, r = divmod(u, NR)
                        g = 4 * gq + gi
                        pe.matmul(scores[0:S, n % 3, 0:TP], qrep[:, g, r, :], krep[:, g, :],
                                  start=True, stop=True).then_inc(score_ok, 1)
                    m = n - 2
                    if 0 <= m < NH:
                        pe.wait_ge(prob_ok, w.next(prob_ok))
                        if m >= 2:
                            pe.wait_ge(copied_v if m % 2 == 0 else copied_s, w.next(copied_v if m % 2 == 0 else copied_s))
                        for j in range(TJ):
                            mm = pe.transpose(turned[0:TC, m % 2, S * j:S * j + S],
                                              probs[0:S, m % 4, TC * j:TC * j + TC], ident[0:S, 0:S])
                        mm.then_inc(turned_v if m % 2 == 0 else turned_s, 1)
                    if n >= 8 and n % 4 == 0:
                        pv(w, n // 4 - 2)

            def pv(w, u):
                gq, r = divmod(u, NR)
                if u == 0:
                    pe.wait_ge(ld_v, w.next(ld_v, 16))
                if u == NH // 4 - 1:
                    pe.wait_ge(copied_v, w.next(copied_v))
                    pe.wait_ge(copied_s, w.next(copied_s))
                for j in range(TJ):
                    for gi in range(4):
                        g = 4 * gq + gi
                        mm = pe.matmul(wide[HD * gi:HD * gi + HD, gq, S * r:S * r + S],
                                       val[:, j, HD * g:HD * g + HD], probsT[:, (4 * u + gi) % 8, j, :],
                                       start=(j == 0), stop=(j == TJ - 1))
                        if u == NH // 4 - 1 and j == 0 and gi == 0:
                            mm.then_inc(k_free, 1)
                if u == 3:
                    mm.then_inc(pv_s, 1)
                if u == 7:
                    mm.then_inc(pv_v, 1)

            with pe.Fori(0, B) as b:
                w = Counts(pe)
                if first:
                    pe.wait_ge(split_x, w.next(split_x))
                    for h in range(2):
                        linear(wide[0:S, h, :], x_hi, x_lo, w0_hi, w0_lo,
                               slice(512 * h, 512 * h + 512)).then_inc(lin_ok, 1)
                    pe.wait_ge(x_ok, w.next(x_ok))
                else:
                    pe.wait_ge(ld_x, w.next(ld_x, 16))
                    pe.wait_ge(tail_free, w.next(tail_free))
                turn_tile(w, xcur, turn_ok)
                cross(w)
                for h in range(2):
                    pe.wait_ge((oT_s, oT_v)[h], w.next((oT_s, oT_v)[h]))
                    for j in range(4):
                        mm = pe.transpose(wide[0:S, h, P * j:P * j + P], oT[:, 4 * h + j, :], ident[:, :])
                        if h == 0 and j == 0:
                            mm.then_inc(v_free, 1)
                    mm.then_inc(attn_ok, 1)
                pe.wait_ge(x2_ok, w.next(x2_ok))
                turn_tile(w, row, turn_ok)
                pe.wait_ge(lo_ok, w.next(lo_ok, 2))
                if first:
                    linear(wide[0:S, 0, 0:UH], tT_hi, tT_lo, wu_hi, wu_lo, slice(0, UH)).then_inc(gate_h_ok, 1)
                    n = 0
                    for k in range(KT):
                        for a, c in split_passes(wq_hi, wq_lo, tT_hi, tT_lo):
                            mm = pe.matmul(wide[0:BOT, 1, 0:S], a[:, k, :], c[:, k, :],
                                           start=(n == 0), stop=(n == 3 * KT - 1))
                            n += 1
                    mm.then_inc(queryT_ok, 1)
                    pe.wait_ge(qaug_ok, w.next(qaug_ok))
                    pe.matmul(scores[0:S, 0, :], qaug[:, :], route[:, :], start=True, stop=True).then_inc(route_ok, 1)
                    pe.wait_ge(slot_w_ok, w.next(slot_w_ok))
                    for j in range(2):
                        mm = pe.transpose(turned[:, 0, S * j:S * j + S], slot_w[0:S, P * j:P * j + P], ident[0:S, 0:S])
                    mm.then_inc(slotT_ok, 1)
                    pe.wait_ge(wT_ok, w.next(wT_ok))
                    for j in range(2):
                        mm = pe.matmul(scores[0:S, 1, 0:BOT], wT[:, j, :], u_val[:, j, :],
                                       start=(j == 0), stop=(j == 1))
                    mm.then_inc(z_ok, 1)
                else:
                    linear(wide[0:S, 1, 0:NE], tT_hi, tT_lo, r_hi, r_lo, slice(0, NE)).then_inc(rscore_ok, 1)
                    linear(wide[0:S, 0, :], tT_hi, tT_lo, a_hi, a_lo, slice(0, BN)).then_inc(bottleneck_ok, 1)
                    pe.wait_ge(gated_ok, w.next(gated_ok))
                    for j in range(4):
                        mm = pe.transpose(turned[:, 0, S * j:S * j + S], zg[0:S, P * j:P * j + P], ident[0:S, 0:S])
                    mm.then_inc(gatedT_ok, 1)
                    pe.wait_ge(z_lo_ok, w.next(z_lo_ok))
                    for h in range(2):
                        linear(wide[0:S, h, :], z_hi, z_lo, b_hi, b_lo,
                               slice(512 * h, 512 * h + 512), kt=4).then_inc(out_ok, 1)
                w.take_off()

        @block.scalar
        def _(act):
            def high_part(w):
                for h in range(2):
                    act.wait_ge(turn_ok, w.next(turn_ok))
                    nc.scalar.copy(tT_hi[:, 4 * h:4 * h + 4, :],
                                   wide[:, h, 0:4 * S].rearrange("p (k s) -> p k s", s=S)).then_inc(hi_ok, 1)

            def cross(w):
                for n in range(NH + 3):
                    if n < NH:
                        act.wait_ge(least_ok, w.next(least_ok))
                        nc.scalar.activation(probs[0:S, n % 4, :], masked[0:S, n % 3, :], ACT.Exp,
                                             bias=least[0:S, n:n + 1], scale=-1.0,
                                             accum_out=rsum[0:S, n:n + 1]).then_inc(prob_ok, 1)
                    m = n - 3
                    if 0 <= m and m % 2 == 1:
                        act.wait_ge(turned_s, w.next(turned_s))
                        nc.scalar.copy(probsT[:, m % 8, :, :],
                                       turned[0:TC, 1, 0:TJ * S].rearrange("p (j s) -> p j s", s=S)).then_inc(copied_s, 1)
                act.wait_ge(pv_s, w.next(pv_s))
                nc.scalar.copy(oT[:, 0:4, :], wide[:, 0, 0:4 * S].rearrange("p (u s) -> p u s", s=S)).then_inc(oT_s, 1)

            with act.Fori(0, B) as b:
                w = Counts(act)
                high_part(w)
                cross(w)
                high_part(w)
                if first:
                    act.wait_ge(queryT_ok, w.next(queryT_ok))
                    nc.scalar.copy(qaug[0:BOT, :], wide[0:BOT, 1, 0:S]).then_inc(qaug_ok, 1)
                    act.wait_ge(route_ok, w.next(route_ok))
                    nc.scalar.copy(ra[0:S, :], scores[0:S, 0, :]).then_inc(ra_ok, 1)
                    act.wait_ge(gelu_arg_ok, w.next(gelu_arg_ok))
                    nc.scalar.activation(uc[0:S, :], ub[0:S, :], ACT.Tanh, scale=0.7978845608028654).then_inc(tanh_ok, 1)
                    act.wait_ge(least_pen_ok, w.next(least_pen_ok))
                    nc.scalar.activation(slot_w[0:S, :], pen[0:S, :], ACT.Exp, bias=sm[0:S, 1:2], scale=1.0,
                                         accum_out=sm[0:S, 2:3]).then_inc(slot_exp_ok, 1)
                    act.wait_ge(slotT_ok, w.next(slotT_ok))
                    nc.scalar.copy(wT[:, :, :], turned[:, 0, 0:2 * S].rearrange("p (j s) -> p j s", s=S)).then_inc(wT_ok, 1)
                    act.wait_ge(row_ok, w.next(row_ok))
                    act.dma_start(io["rows"][b], row[0:S, :]).then_inc(stored, 16)
                else:
                    act.wait_ge(top_ok, w.next(top_ok))
                    nc.scalar.activation(egate[0:S, :], sc[0:S, :], ACT.Exp, bias=sm[0:S, 1:2], scale=1.0).then_inc(egate_ok, 1)
                    act.wait_ge(gatedT_ok, w.next(gatedT_ok))
                    nc.scalar.copy(z_hi[:, :, :], turned[:, 0, 0:4 * S].rearrange("p (j s) -> p j s", s=S)).then_inc(z_hi_ok, 1)
                    act.wait_ge(res_ok, w.next(res_ok))
                    act.dma_start(io["out"][b], res[0:S, :]).then_inc(stored, 16)
                w.take_off()

        @block.vector
        def _(dve):
            def low_part(w, signal):
                for h in range(2):
                    dve.wait_ge(hi_ok, w.next(hi_ok))
                    nc.vector.tensor_tensor(tT_lo[:, 4 * h:4 * h + 4, :],
                                            wide[:, h, 0:4 * S].rearrange("p (k s) -> p k s", s=S),
                                            tT_hi[:, 4 * h:4 * h + 4, :].bitcast(F32), ALU.subtract).then_inc(signal, 1)

            def cross(w):
                for n in range(NH + 3):
                    m = n - 3
                    if 0 <= m and m % 2 == 0:
                        dve.wait_ge(turned_v, w.next(turned_v))
                        nc.vector.tensor_copy(probsT[:, m % 8, :, :],
                                              turned[0:TC, 0, 0:TJ * S].rearrange("p (j s) -> p j s", s=S)).then_inc(copied_v, 1)
                    if n < NH:
                        dve.wait_ge(score_ok, w.next(score_ok))
                        nc.vector.tensor_tensor_reduce(
                            out=masked[0:S, n % 3, :], in0=scores[0:S, n % 3, 0:T], in1=nmask[0:S, :],
                            scale=1.0, scalar=HUGE, op0=ALU.add, op1=ALU.min,
                            accum_out=least[0:S, n:n + 1]).then_inc(least_ok, 1)
                dve.wait_ge(pv_v, w.next(pv_v))
                nc.vector.tensor_copy(oT[:, 4:8, :], wide[:, 1, 0:4 * S].rearrange("p (u s) -> p u s", s=S)).then_inc(oT_v, 1)
                nc.vector.reciprocal(rinv[0:S, :], rsum[0:S, :])
                dve.drain()
                for gq in range(2):
                    dve.wait_ge(attn_ok, w.next(attn_ok))
                    nc.vector.tensor_tensor(
                        attn[0:S, 512 * gq:512 * gq + 512].rearrange("p (gi r d) -> p r gi d", gi=4, r=NR),
                        wide[0:S, gq, :].rearrange("p (r gi d) -> p r gi d", r=NR, gi=4),
                        rinv[0:S, 16 * gq:16 * gq + 16].rearrange("p (r gi) -> p r gi", r=NR)
                        .unsqueeze(3).broadcast_to([S, NR, 4, HD]), ALU.mult)
                dve.drain()
                nc.vector.tensor_tensor(attn[0:S, :], attn[0:S, :], xcur[0:S, :], ALU.add)
                dve.drain()

            if first:
                dve.sem_inc(xb_used, 1)
            else:
                dve.sem_inc(x_free, 1)
                dve.sem_inc(tail_free, 1)
            dve.sem_inc(k_free, 1)
            dve.sem_inc(v_free, 1)
            dve.sem_inc(stored, 16)
            with dve.Fori(0, B) as b:
                w = Counts(dve)
                if first:
                    dve.wait_ge(xb_ok, w.next(xb_ok))
                    for h in range(2):
                        dve.wait_ge(lin_ok, w.next(lin_ok))
                        nc.vector.tensor_tensor(xcur[0:S, 512 * h:512 * h + 512], wide[0:S, h, :],
                                                xb[0:S, 512 * h:512 * h + 512], ALU.add)
                    dve.drain().then_inc(x_free, 1)
                    dve.drain().then_inc(xb_used, 1)
                    norm(dve, w, xcur, xcur, x_ok)
                low_part(w, q_ok)
                cross(w)
                dve.wait_ge(stored, w.next(stored, 16))
                if not first:
                    dve.drain().then_inc(x_free, 1)
                norm(dve, w, attn, row, x2_ok)
                low_part(w, lo_ok)
                if first:
                    slot_ffn_vector(dve, w)
                else:
                    routed_ffn_vector(dve, w)
                w.take_off()
            dve.wait_ge(stored, 16)
            dve.sem_inc(stored, -16)


def self_attention(nc, io, sem):
    NBLK = S // 8
    NC = NBLK // 2
    TH = NC * P
    NKV, QPG, DH = 8, 4, 128
    UNITS = QPG + 2
    CHUNKS = (slice(0, 512), slice(512, TH))

    with ExitStack() as ctx:
        def sb(name, shape, dt=F32):
            return ctx.enter_context(nc.sbuf_tensor(f"sa_{name}", shape, dt))

        feat = ctx.enter_context(nc.psum_tensor("sa_feat", [P, 2, 2, 512], F32))
        score = ctx.enter_context(nc.psum_tensor("sa_score", [P, 512], F32))
        ring = ctx.enter_context(nc.psum_tensor("sa_ring", [P, 3, 512], F32))

        ident, causal = sb("ident", [P, P]), sb("causal", [P, 32])
        gate = sb("gate", [P, NBLK])
        half_exp = sb("half_exp", [P, 1])
        x_hi, x_lo = sb("x_hi", [P, KT, TH], F32R), sb("x_lo", [P, KT, TH], F32R)
        acc = sb("acc", [P, NC, D])
        st, mv, veps, rstd = sb("st", [P, 12]), sb("mv", [P, 2]), sb("veps", [P, 1]), sb("rstd", [P, 1])

        gate_stage(nc, io, sem, ident, causal, half_exp, gate, ring, NBLK)
        for half in range(2):
            load_half(nc, io, sem, half, NC, ident, half_exp, gate, x_hi, x_lo, acc, st, mv, veps, rstd, feat, ring)
            heads_half(nc, io, sem, half, NC, TH, NKV, QPG, DH, UNITS, CHUNKS,
                       ident, causal, x_hi, x_lo, acc, feat, score, ring)
            store_half(nc, io, sem, half, NC, half_exp, acc, st, mv, veps, rstd)


def gate_stage(nc, io, sem, ident, causal, half_exp, gate, ring, NBLK):
    with ExitStack() as ctx:
        def sb(name, shape):
            return ctx.enter_context(nc.sbuf_tensor(f"gate_{name}", shape, F32))

        pair = sb("pair", [P, NBLK, 2])
        ones, w1, gb = sb("ones", [P, P]), sb("w1", [P, 1]), sb("gb", [P, 1])
        lv, lsum, u, t = sb("lv", [P, NBLK]), sb("lsum", [P, 1]), sb("u", [P, NBLK]), sb("t", [P, NBLK])
        mean = sb("mean", [P, 1])
        loaded, log_ok, sum_ok, tanh_ok, arg_ok, tanh2_ok = (
            sem(f"gate_{n}") for n in ("loaded", "log", "sum", "tanh", "arg", "tanh2"))
        block = ctx.enter_context(nc.Block())
        srcs = 8

        @block.sync
        def _(sp):
            for dst, src in ((ident, "ident"), (causal, "causal"), (ones, "ones"), (w1, "gate_w1"), (gb, "gate_bias")):
                sp.dma_start(dst[:], io[src]).then_inc(loaded, 16)
            rows = io["rows"].rearrange("b (c l) n -> l b c n", l=8)
            for l in range(srcs):
                sp.dma_start(pair[16 * l:16 * l + 16, :, :], rows[l, :, :, COL_LEARNED:COL_VAR + 1]).then_inc(loaded, 16)

        @block.scalar
        def _(act):
            act.wait_ge(loaded, 16 * (5 + srcs))
            nc.scalar.activation(t[:], pair[:, :, 0], ACT.Tanh, scale=0.5).then_inc(tanh_ok, 1)
            nc.scalar.activation(lv[:], pair[:, :, 1], ACT.Ln, bias=1.0, scale=1.0, accum_out=lsum[:]).then_inc(log_ok, 1)
            act.wait_ge(arg_ok, 1)
            nc.scalar.activation(t[:], u[:], ACT.Tanh, scale=0.5).then_inc(tanh2_ok, 1)

        @block.tensor
        def _(pe):
            pe.wait_ge(log_ok, 1)
            pe.matmul(ring[:, 0, 0:1], ones[:], lsum[:], start=True, stop=True).then_inc(sum_ok, 1)

        @block.vector
        def _(dve):
            v = nc.vector
            v.memset(half_exp[:], -0.5)
            dve.wait_ge(tanh_ok, 1)
            v.tensor_scalar(t[:], t[:], 1.0, 1.25, ALU.add, ALU.mult)
            dve.wait_ge(sum_ok, 1)
            v.tensor_scalar(mean[:], ring[:, 0, 0:1], 1.0 / (B * S), 1e-6, ALU.mult, ALU.add)
            dve.drain()
            v.reciprocal(mean[:], mean[:])
            dve.drain()
            v.tensor_scalar(lv[:], lv[:], mean[:, 0:1], 0.5, ALU.mult, ALU.mult)
            dve.drain()
            v.tensor_tensor(u[:], lv[:], t[:], ALU.add)
            dve.drain()
            v.tensor_scalar(u[:], u[:], 0.0, 5.0, ALU.max, ALU.min)
            dve.drain()
            v.tensor_scalar(u[:], u[:], -0.5, 1.0 / 1.5, ALU.add, ALU.mult)
            dve.drain()
            v.tensor_scalar(u[:], u[:], 0.0, 1.0, ALU.max, ALU.min)
            dve.drain()
            v.tensor_scalar(u[:], u[:], w1[:, 0:1], gb[:, 0:1], ALU.mult, ALU.add).then_inc(arg_ok, 1)
            dve.wait_ge(tanh2_ok, 1)
            v.tensor_scalar(t[:], t[:], 1.0, 0.5, ALU.add, ALU.mult)
            dve.drain()
            v.tensor_scalar(u[:], t[:], 0.05, None, ALU.is_ge)
            dve.drain()
            v.tensor_tensor(gate[:], t[:], u[:], ALU.mult)


def load_half(nc, io, sem, half, NC, ident, half_exp, gate, x_hi, x_lo, acc, st, mv, veps, rstd, feat, ring):
    with ExitStack() as ctx:
        def sb(name, shape, dt=F32):
            return ctx.enter_context(nc.sbuf_tensor(f"load{half}_{name}", shape, dt))

        def s(name):
            return sem(f"load{half}_{name}")

        wvu = sb("wvu", [BOT, D])
        x2z = sb("x2z", [P, D + BOT])
        zT = sb("zT", [BOT, P])
        g = sb("g", [P, 1])
        y = sb("y", [P, D])
        ld_w, ld_row, row_free, zt_ok, zT_ok, aux_ok = s("ld_w"), s("ld_row"), s("row_free"), s("zt"), s("zT"), s("aux")
        var_ok, rstd_ok, x3_ok, turn_ok, hi_ok, lo_ok = s("var"), s("rstd"), s("x3"), s("turn"), s("hi"), s("lo")
        block = ctx.enter_context(nc.Block())

        @block.sync
        def _(sp):
            sp.dma_start(wvu[:], io["wvuT"]).then_inc(ld_w, 16)
            rows = io["rows"].rearrange("b (h c l) n -> h c l b n", h=2, l=8)[half]
            with sp.Fori(0, NC) as c:
                w = Counts(sp)
                sp.wait_ge(row_free, w.next(row_free))
                for l in range(8):
                    sp.dma_start(x2z[16 * l:16 * l + 16, :], rows[c, l, :, 0:D + BOT]).then_inc(ld_row, 16)
                w.take_off()

        @block.gpsimd
        def _(pool):
            with pool.Fori(0, NC) as c:
                w = Counts(pool)
                pool.wait_ge(var_ok, w.next(var_ok))
                nc.gpsimd.tensor_scalar(veps[:], mv[:, 1:2], EPS, None, ALU.add)
                pool.drain()
                nc.gpsimd.tensor_tensor(rstd[:], veps[:], half_exp[:], ALU.pow).then_inc(rstd_ok, 1)
                w.take_off()

        @block.tensor
        def _(pe):
            pe.wait_ge(ld_w, 16)
            with pe.Fori(0, NC) as c:
                w = Counts(pe)
                pe.wait_ge(ld_row, w.next(ld_row, 16 * 8))
                pe.transpose(ring[0:BOT, 0, 0:P], x2z[:, D:D + BOT], ident[:]).then_inc(zt_ok, 1)
                pe.wait_ge(zT_ok, w.next(zT_ok))
                for h in range(2):
                    pe.matmul(ring[:, 1 + h, :], zT[:], wvu[:, 512 * h:512 * h + 512],
                              start=True, stop=True).then_inc(aux_ok, 1)
                pe.wait_ge(x3_ok, w.next(x3_ok))
                pe.wait_ge(lo_ok, w.next(lo_ok, 2))
                for h in range(2):
                    for j in range(4):
                        k = 4 * h + j
                        mm = pe.transpose(feat[:, 0, h, P * j:P * j + P], y[:, P * k:P * k + P], ident[:])
                    mm.then_inc(turn_ok, 1)
                w.take_off()

        @block.scalar
        def _(act):
            with act.Fori(0, NC) as c:
                w = Counts(act)
                act.wait_ge(zt_ok, w.next(zt_ok))
                nc.scalar.copy(zT[:], ring[0:BOT, 0, 0:P]).then_inc(zT_ok, 1)
                for h in range(2):
                    act.wait_ge(turn_ok, w.next(turn_ok))
                    nc.scalar.copy(x_hi[:, 4 * h:4 * h + 4, bass.ds(c * P, P)],
                                   feat[:, 0, h, :].rearrange("p (k t) -> p k t", k=4)).then_inc(hi_ok, 1)
                w.take_off()

        @block.vector
        def _(dve):
            v = nc.vector
            dve.sem_inc(row_free, 1)
            dve.sem_inc(lo_ok, 2)
            with dve.Fori(0, NC) as c:
                w = Counts(dve)
                v.tensor_copy(g[:], gate[:, bass.ds(c + half * NC, 1)])
                dve.drain()
                for h in range(2):
                    cols = slice(512 * h, 512 * h + 512)
                    dve.wait_ge(aux_ok, w.next(aux_ok))
                    v.scalar_tensor_tensor(out=y[:, cols], in0=ring[:, 1 + h, :], scalar=g[:, 0:1],
                                           in1=x2z[:, cols], op0=ALU.mult, op1=ALU.add)
                dve.drain()
                v.tensor_tensor(y[:], y[:], x2z[:, 0:D], ALU.add)
                dve.drain().then_inc(row_free, 1)
                for h in range(2):
                    v.bn_stats(st[:, 6 * h:6 * h + 6], y[:, 512 * h:512 * h + 512])
                dve.drain()
                v.bn_aggr(mv[:], st[:]).then_inc(var_ok, 1)
                dve.wait_ge(rstd_ok, w.next(rstd_ok))
                v.tensor_scalar(y[:], y[:], mv[:, 0:1], rstd[:, 0:1], ALU.subtract, ALU.mult).then_inc(x3_ok, 1)
                dve.drain()
                v.tensor_copy(acc[:, bass.ds(c, 1), :], y[:].unsqueeze(1))
                for h in range(2):
                    dve.wait_ge(hi_ok, w.next(hi_ok))
                    v.tensor_tensor(x_lo[:, 4 * h:4 * h + 4, bass.ds(c * P, P)],
                                    feat[:, 0, h, :].rearrange("p (k t) -> p k t", k=4),
                                    x_hi[:, 4 * h:4 * h + 4, bass.ds(c * P, P)].bitcast(F32), ALU.subtract).then_inc(lo_ok, 1)
                w.take_off()


def heads_half(nc, io, sem, half, NC, TH, NKV, QPG, DH, UNITS, CHUNKS,
               ident, causal, x_hi, x_lo, acc, feat, score, ring):
    with ExitStack() as ctx:
        def sb(name, shape, dt=F32):
            return ctx.enter_context(nc.sbuf_tensor(f"heads{half}_{name}", shape, dt))

        def s(name):
            return sem(f"heads{half}_{name}")

        raw = sb("raw", [P, 2, D])
        w_hi, w_lo = sb("w_hi", [P, 2, KT, DH], F32R), sb("w_lo", [P, 2, KT, DH], F32R)
        p_hi, p_lo = sb("p_hi", [P, QPG, D], F32R), sb("p_lo", [P, QPG, D], F32R)
        qT, kT, vT = sb("qT", [P, QPG, TH]), sb("kT", [P, TH]), sb("vT", [P, TH])
        val = sb("val", [P, NC, DH])
        sm, ex = sb("sm", [P, NC, 32]), sb("ex", [P, NC, 32])
        most, total = sb("most", [P, NC]), sb("total", [P, NC])
        probsT = sb("probsT", [P, QPG, NC, P])
        o_hi, o_lo = sb("o_hi", [P, QPG, TH], F32R), sb("o_lo", [P, QPG, TH], F32R)

        ld_raw, raw_free = [s("ld_raw0"), s("ld_raw1")], s("raw_free")
        unit_ok, w_free, p_free = s("unit_ok"), s("w_free"), s("p_free")
        feat_ok, feat_sb = s("feat_ok"), s("feat_sb")
        score_ok, score_free, arg_ok, exp_ok, probs_ok = s("score_ok"), s("score_free"), s("arg_ok"), s("exp_ok"), s("probs_ok")
        vt_ok, val_ok, pv_ok, o_hi_ok, o_lo_ok = s("vt_ok"), s("val_ok"), s("pv_ok"), s("o_hi_ok"), s("o_lo_ok")
        proj_ok, acc_ok = s("proj_ok"), s("acc_ok")
        block = ctx.enter_context(nc.Block())
        ORDER = [QPG] + list(range(QPG)) + [QPG + 1]

        @block.sync
        def _(sp):
            with sp.Fori(0, NKV) as g:
                w = Counts(sp)
                for u in range(UNITS + QPG):
                    sp.wait_ge(raw_free, w.next(raw_free))
                    src = io["wqkvU"][g, ORDER[u]] if u < UNITS else io["wprojU"][g, u - UNITS]
                    sp.dma_start(raw[:, u % 2, :], src).then_inc(ld_raw[u % 2], 16)
                w.take_off()

        @block.gpsimd
        def _(pool):
            with pool.Fori(0, NKV) as g:
                w = Counts(pool)
                for u in range(UNITS + QPG):
                    pool.wait_ge(ld_raw[u % 2], w.next(ld_raw[u % 2], 16))
                    if u < UNITS:
                        pool.wait_ge(w_free, w.next(w_free))
                        hi, lo = w_hi[:, u % 2, :, :], w_lo[:, u % 2, :, :]
                        src = raw[:, u % 2, :].rearrange("p (k n) -> p k n", k=KT)
                    else:
                        if u == UNITS:
                            pool.wait_ge(p_free, w.next(p_free))
                        hi, lo, src = p_hi[:, u - UNITS, :], p_lo[:, u - UNITS, :], raw[:, u % 2, :]
                    nc.gpsimd.tensor_copy(hi, src)
                    pool.drain()
                    nc.gpsimd.tensor_tensor(lo, src, hi.bitcast(F32), ALU.subtract).then_inc(unit_ok, 1)
                    pool.drain().then_inc(raw_free, 1)
                w.take_off()

        @block.tensor
        def _(pe):
            def scores(w, j):
                pe.wait_ge(score_free, w.next(score_free))
                for c in range(NC):
                    for p in range(4):
                        t = slice(P * c + 32 * p, P * c + 32 * p + 32)
                        mm = pe.matmul(score[32 * p:32 * p + 32, 32 * c:32 * c + 32], qT[:, j, t], kT[:, t],
                                       start=True, stop=True)
                mm.then_inc(score_ok, 1)

            with pe.Fori(0, NKV) as g:
                w = Counts(pe)
                for u in range(UNITS):
                    pe.wait_ge(unit_ok, w.next(unit_ok))
                    for i, t in enumerate(CHUNKS):
                        n = 0
                        for k in range(KT):
                            for a, b in split_passes(w_hi, w_lo, x_hi, x_lo):
                                mm = pe.matmul(feat[:, u % 2, i, 0:t.stop - t.start], a[:, u % 2, k, :], b[:, k, t],
                                               start=(n == 0), stop=(n == 3 * KT - 1))
                                n += 1
                        mm.then_inc(feat_ok, 1)
                    if u >= 2:
                        pe.wait_ge(feat_sb, w.next(feat_sb, 2 if u == 2 else 1))
                        scores(w, u - 2)
                pe.wait_ge(feat_sb, w.next(feat_sb))
                for i in range(2):
                    pe.wait_ge(acc_ok, w.next(acc_ok))
                    for c in range(4 * i, min(4 * i + 4, NC)):
                        mm = pe.transpose(ring[:, i, P * (c % 4):P * (c % 4) + P], vT[:, P * c:P * c + P], ident[:])
                    mm.then_inc(vt_ok, 1)
                pe.wait_ge(probs_ok, w.next(probs_ok, QPG))
                pe.wait_ge(val_ok, w.next(val_ok, 2))
                for c in range(NC):
                    if c == 0:
                        pe.wait_ge(acc_ok, w.next(acc_ok))
                    if c >= 3:
                        pe.wait_ge(o_lo_ok, w.next(o_lo_ok))
                    pe.matmul(ring[:, (2 + c) % 3, :], val[:, c, :], probsT[:, :, c, :],
                              start=True, stop=True).then_inc(pv_ok, 1)
                pe.wait_ge(unit_ok, w.next(unit_ok, QPG))
                for c in range(NC):
                    for h in range(2):
                        n = 2 * c + h
                        pe.wait_ge(o_lo_ok if n < 3 else acc_ok, w.next(o_lo_ok if n < 3 else acc_ok))
                        i = 0
                        for j in range(QPG):
                            for a, b in split_passes(o_hi, o_lo, p_hi, p_lo):
                                mm = pe.matmul(ring[:, (2 + NC + n) % 3, :], a[:, j, P * c:P * c + P],
                                               b[:, j, 512 * h:512 * h + 512], start=(i == 0), stop=(i == 3 * QPG - 1))
                                i += 1
                        mm.then_inc(proj_ok, 1)
                w.take_off()

        @block.scalar
        def _(act):
            def take_exp(w):
                act.wait_ge(arg_ok, w.next(arg_ok))
                nc.scalar.activation(ex[:], sm[:], ACT.Exp).then_inc(exp_ok, 1)

            with act.Fori(0, NKV) as g:
                w = Counts(act)
                for u in range(UNITS):
                    dst = kT[:, :] if u == 0 else (vT[:, :] if u == UNITS - 1 else qT[:, u - 1, :])
                    for i, t in enumerate(CHUNKS):
                        act.wait_ge(feat_ok, w.next(feat_ok))
                        last = nc.scalar.copy(dst[:, t], feat[:, u % 2, i, 0:t.stop - t.start])
                    last.then_inc(w_free, 1)
                    act.drain().then_inc(feat_sb, 1)
                    if u >= 3:
                        take_exp(w)
                take_exp(w)
                for i in range(2):
                    act.wait_ge(vt_ok, w.next(vt_ok))
                    n = min(4, NC - 4 * i)
                    nc.scalar.copy(val[:, 4 * i:4 * i + n, :],
                                   ring[:, i, 0:P * n].rearrange("p (c d) -> p c d", c=n)).then_inc(val_ok, 1)
                for c in range(NC):
                    act.wait_ge(pv_ok, w.next(pv_ok))
                    nc.scalar.copy(o_hi[:, :, P * c:P * c + P],
                                   ring[:, (2 + c) % 3, :].rearrange("p (j t) -> p j t", j=QPG)).then_inc(o_hi_ok, 1)
                w.take_off()

        @block.vector
        def _(dve):
            v = nc.vector
            v.memset(probsT[:].bitcast(F32), 0.0)
            dve.drain()
            dve.sem_inc(raw_free, 2)
            dve.sem_inc(w_free, 2)
            dve.sem_inc(p_free, 1)
            dve.sem_inc(score_free, 1)
            dve.sem_inc(acc_ok, 3)
            with dve.Fori(0, NKV) as g:
                w = Counts(dve)
                for j in range(QPG):
                    dve.wait_ge(score_ok, w.next(score_ok))
                    v.scalar_tensor_tensor(out=sm[:], in0=score[:, 0:32 * NC].rearrange("p (c t) -> p c t", c=NC),
                                           scalar=float(DH) ** -0.5, in1=causal[:].unsqueeze(1).broadcast_to([P, NC, 32]),
                                           op0=ALU.mult, op1=ALU.add)
                    dve.drain().then_inc(score_free, 1)
                    v.tensor_reduce(most[:], sm[:], AX.X, ALU.max)
                    dve.drain()
                    v.tensor_tensor(sm[:], sm[:], most[:].unsqueeze(2).broadcast_to([P, NC, 32]),
                                    ALU.subtract).then_inc(arg_ok, 1)
                    dve.wait_ge(exp_ok, w.next(exp_ok))
                    v.tensor_reduce(total[:], ex[:], AX.X, ALU.add)
                    dve.drain()
                    v.reciprocal(total[:], total[:])
                    dve.drain()
                    v.tensor_tensor(ex[:], ex[:], total[:].unsqueeze(2).broadcast_to([P, NC, 32]), ALU.mult)
                    dve.drain()
                    for p in range(4):
                        q = slice(32 * p, 32 * p + 32)
                        v.transpose(probsT[q, j, :, q], ex[q, :, :])
                    dve.drain().then_inc(probs_ok, 1)
                for c in range(NC):
                    dve.wait_ge(o_hi_ok, w.next(o_hi_ok))
                    v.tensor_tensor(o_lo[:, :, P * c:P * c + P],
                                    ring[:, (2 + c) % 3, :].rearrange("p (j t) -> p j t", j=QPG),
                                    o_hi[:, :, P * c:P * c + P].bitcast(F32), ALU.subtract).then_inc(o_lo_ok, 1)
                for c in range(NC):
                    for h in range(2):
                        n = 2 * c + h
                        cols = slice(512 * h, 512 * h + 512)
                        dve.wait_ge(proj_ok, w.next(proj_ok))
                        v.tensor_tensor(acc[:, c, cols], acc[:, c, cols], ring[:, (2 + NC + n) % 3, :],
                                        ALU.add).then_inc(acc_ok, 1)
                dve.drain().then_inc(p_free, 1)
                w.take_off()


def store_half(nc, io, sem, half, NC, half_exp, acc, st, mv, veps, rstd):
    with ExitStack() as ctx:
        y = ctx.enter_context(nc.sbuf_tensor(f"store{half}_y", [P, D], F32))
        var_ok, rstd_ok, y_ok, stored = (sem(f"store{half}_{n}") for n in ("var", "rstd", "y", "stored"))
        block = ctx.enter_context(nc.Block())

        @block.sync
        def _(sp):
            dst = io["x4"].rearrange("b (h c l) n -> h c l b n", h=2, l=8)[half]
            with sp.Fori(0, NC) as c:
                w = Counts(sp)
                sp.wait_ge(y_ok, w.next(y_ok))
                for l in range(8):
                    sp.dma_start(dst[c, l, :, :], y[16 * l:16 * l + 16, :]).then_inc(stored, 16)
                w.take_off()

        @block.gpsimd
        def _(pool):
            with pool.Fori(0, NC) as c:
                w = Counts(pool)
                pool.wait_ge(var_ok, w.next(var_ok))
                nc.gpsimd.tensor_scalar(veps[:], mv[:, 1:2], EPS, None, ALU.add)
                pool.drain()
                nc.gpsimd.tensor_tensor(rstd[:], veps[:], half_exp[:], ALU.pow).then_inc(rstd_ok, 1)
                w.take_off()

        @block.vector
        def _(dve):
            v = nc.vector
            dve.sem_inc(stored, 16 * 8)
            with dve.Fori(0, NC) as c:
                w = Counts(dve)
                for h in range(2):
                    v.bn_stats(st[:, 6 * h:6 * h + 6], acc[:, bass.ds(c, 1), 512 * h:512 * h + 512])
                dve.drain()
                v.bn_aggr(mv[:], st[:]).then_inc(var_ok, 1)
                dve.wait_ge(rstd_ok, w.next(rstd_ok))
                dve.wait_ge(stored, w.next(stored, 16 * 8))
                v.tensor_scalar(y[:].unsqueeze(1), acc[:, bass.ds(c, 1), :], mv[:, 0:1], rstd[:, 0:1],
                                ALU.subtract, ALU.mult).then_inc(y_ok, 1)
                w.take_off()
            dve.wait_ge(stored, 16 * 8)
            dve.sem_inc(stored, -16 * 8)


def build(nc, io, out):
    ks = nc.dram_tensor("ctx_parts", [2, C, B, T], F32).ap()
    rows = nc.dram_tensor("rows", [B, S, ROW], F32).ap()
    x4 = nc.dram_tensor("x4", [B, S, D], F32).ap()
    io = dict(io, ks=ks, rows=rows, x4=x4, out=out)

    def stage(fn, *args):
        with ExitStack() as ctx:
            used = []

            def sem(name):
                used.append(ctx.enter_context(nc.semaphore(name)))
                return used[-1]

            fn(*args, sem)
            with nc.Block() as block:
                @block.gpsimd
                def _(pool):
                    for one in used:
                        pool.sem_clear(one)

    stage(split_context, nc, io["ctxT"], ks)
    stage(token_stage, nc, 0, io)
    stage(self_attention, nc, io)
    stage(token_stage, nc, 1, io)


def layouts(a):
    def rows(v, n=P):
        return np.broadcast_to(np.reshape(v, (1, -1)), (n, np.size(v)))

    lr = np.reshape(a["L0_ffn_log_rel"], (1, -1))
    r = np.arange(P) % 32
    allowed = (r[:, None] // 16 == np.arange(32)[None] // 16) & (np.arange(32)[None] % 16 <= r[:, None] % 16)
    return {
        "x": a["x"], "xT": np.transpose(a["x"], (2, 0, 1)),
        "ctx": a["ctx_1024"], "ctxT": np.transpose(a["ctx_1024"], (2, 0, 1)),
        "mask": a["mask_SxS2_ff0"],
        "bmaskT": np.transpose(a["L0_attn_mask"]), "w0T": np.transpose(a["L0_attn_weight"]),
        "b0": rows(a["L0_attn_bias"]),
        "wu1T": np.transpose(a["L0_ffn_Wu1"]), "bu1": rows(a["L0_ffn_bu1"]),
        "wu2": rows(a["L0_ffn_Wu2"]), "bu2": rows(a["L0_ffn_bu2"]),
        "wqT": np.transpose(a["L0_ffn_Wq"]), "wr": a["L0_ffn_Wr"], "wrT": np.transpose(a["L0_ffn_Wr"]),
        "keysT": np.transpose(a["L0_ffn_aux_keys"]), "valuesT": np.transpose(a["L0_ffn_aux_values"]),
        "log_rel": np.concatenate([lr, lr], axis=1),
        "wvdT": np.transpose(a["L0_ffn_Wvd"]), "wvuT": np.transpose(a["L0_ffn_Wvu"]),
        "gate_w1": rows(a["L0_ffn_gate_w1"]), "gate_bias": rows(a["L0_ffn_gate_bias"]),
        "wqkvU": np.reshape(np.transpose(np.reshape(a["L1_attn_weight_qkv"], (8, 6, P, KT, P)), (0, 1, 4, 3, 2)),
                            (8, 6, P, D)),
        "wprojU": np.reshape(np.transpose(a["L1_attn_weight_proj"]), (8, 4, P, D)),
        "awT": np.transpose(a["L1_ffn_A_w"]), "bwT": np.transpose(a["L1_ffn_B_w"]),
        "rq": a["L1_ffn_Wq_w"], "rkeysT": np.transpose(a["L1_ffn_keys"]),
        "ident": np.eye(P, dtype=np.float32),
        "ones": np.ones((P, P), np.float32),
        "blocks": np.kron(np.eye(4, dtype=np.float32), np.ones((32, 32), np.float32)),
        "causal": np.where(allowed, 0.0, -HUGE).astype(np.float32),
    }


def kernel(**inputs):
    import concourse.bacc as _bacc
    from concourse.bass_utils import run_bass_kernel_spmd as _run

    nc = _bacc.Bacc("TRN2", target_bir_lowering=False, num_devices=1, dynamic_dma_scratch_size=1024)
    arrays, args = {}, {}
    for name, a in layouts({k: np.asarray(v) for k, v in inputs.items()}).items():
        a = np.ascontiguousarray(a)
        arrays[f"in_{name}_dram"] = a
        args[name] = nc.dram_tensor(f"in_{name}_dram", a.shape, mybir.dt.from_np(a.dtype), kind="ExternalInput").ap()
    out = nc.dram_tensor("out_0_dram", (B, S, D), F32, kind="ExternalOutput").ap()
    build(nc, args, out)
    r = _run(nc, [arrays], core_ids=[0])
    return r.results[0]["out_0_dram"]
```

```python
from contextlib import ExitStack

import numpy as np
import concourse.bass as bass
from concourse import mybir

F32 = mybir.dt.float32
F32R = mybir.dt.float32r
I32 = mybir.dt.int32
ALU = mybir.AluOpType
ACT = mybir.ActivationFunctionType
AX = mybir.AxisListType

P = 128
B, S, D = 16, 112, 1024
T, C = 375, 256
KT = D // P
HD = 32
NG, NR = 8, 4
NH = NG * NR
TC, TJ = 125, 3
TP = T + 1
EPS = 1e-5
BOT, SLOTS, UH = 64, 256, 256
ROW = 1096
COL_Z, COL_LEARNED, COL_VAR = D, D + BOT, D + BOT + 1
NE, RANK = 64, 8
BN = NE * RANK
HUGE = 3.0e38


class Counts:

    def __init__(self, eng):
        self.eng, self.counts = eng, {}

    def next(self, sem, n=1):
        total = self.counts.get(sem.name, (sem, 0))[1] + n
        self.counts[sem.name] = (sem, total)
        return total

    def take_off(self):
        for sem, total in self.counts.values():
            self.eng.sem_inc(sem, -total)
        self.counts = {}


def split_passes(hi_a, lo_a, hi_b, lo_b):
    return ((hi_a, hi_b), (hi_a, lo_b), (lo_a, hi_b))


def token_stage(nc, layer, io, sem):
    first = layer == 0
    with ExitStack() as ctx:
        def sb(name, shape, dt=F32):
            return ctx.enter_context(nc.sbuf_tensor(f"L{layer}_{name}", shape, dt))

        def s(name):
            return sem(f"L{layer}_{name}")

        wide = ctx.enter_context(nc.psum_tensor(f"L{layer}_wide", [P, 2, 512], F32))
        scores = ctx.enter_context(nc.psum_tensor(f"L{layer}_scores", [P, 3, 512], F32))
        turned = ctx.enter_context(nc.psum_tensor(f"L{layer}_turned", [P, 2, 512], F32))

        spare = ctx.enter_context(nc.psum_tensor(f"L{layer}_spare", [P, 512], F32))

        ident = sb("ident", [P, P])
        nmask = sb("nmask", [P, T])
        xcur = sb("xcur", [P, D])
        xnew = sb("xnew", [P, D])
        row = sb("row", [P, ROW])
        attn = sb("attn", [P, D])
        tT_hi = sb("tT_hi", [P, KT, S], F32R)
        tT_lo = sb("tT_lo", [P, KT, S], F32R)
        qT_hi = sb("qT_hi", [P, KT, S], F32R)
        qT_lo = sb("qT_lo", [P, KT, S], F32R)
        qrep = sb("qrep", [P, NG, NR, S], F32R)
        krep = sb("krep", [P, NG, TP], F32R)
        val = sb("val", [TC, TJ, C])
        masked = sb("masked", [P, 3, T])
        probs = sb("probs", [P, 4, T])
        probsT = sb("probsT", [TC, 8, TJ, S])
        oT = sb("oT", [P, 8, S])
        least = sb("least", [P, NH])
        rsum = sb("rsum", [P, NH])
        rinv = sb("rinv", [P, NH])
        st = sb("st", [P, 36])
        mv = sb("mv", [P, 6])
        veps = sb("veps", [P, 3])
        rstd = sb("rstd", [P, 3])
        half = sb("half", [P, 1])

        ld_x, ld_xt, ld_c, x_free, xt_free = s("ld_x"), s("ld_xt"), s("ld_c"), s("x_free"), s("xt_free")
        ld_kq, ld_v, k_free, v_free, q_stored = ([s(f"{n}{h}") for h in range(2)]
                                                 for n in ("ld_kq", "ld_v", "k_free", "v_free", "q_stored"))
        x_hi_ok, split_x, xb_ok, lin_ok, lin_read = s("x_hi_ok"), s("split_x"), s("xb_ok"), s("lin_ok"), s("lin_read")
        c_hi_ok, c_lo_ok, c_stored, x_ok, x_moved = s("c_hi_ok"), s("c_lo_ok"), s("c_stored"), s("x_ok"), s("x_moved")
        turn_ok, q_hi_ok, q_lo_ok, q_read = s("turn"), s("q_hi"), s("q_lo"), s("q_read")
        turn2_ok, hi2_ok, lo2_ok = s("turn2"), s("hi2"), s("lo2")
        score_ok, least_ok, prob_ok = s("score"), s("least"), s("prob")
        turned_v, turned_s, copied_v, copied_s = s("turned_v"), s("turned_s"), s("copied_v"), s("copied_s")
        pv_s, pv_v, oT_s, oT_v = s("pv_s"), s("pv_v"), s("oT_s"), s("oT_v")
        attn_ok, attn_read, attn_out, sum_ok, sum_done = s("attn_ok"), s("attn_read"), s("attn_out"), s("sum_ok"), s("sum_done")
        var_ok, rstd_ok = ([s(f"{n}{i}") for i in range(3)] for n in ("var", "rstd"))
        x2_ok, stored = s("x2"), s("stored")

        if first:
            gate_h_ok, gate_h_read, gelu_arg_ok, least_pen_ok = s("gate_h_ok"), s("gate_h_read"), s("gelu_arg_ok"), s("least_pen_ok")
            qaug_ok, z_read = s("qaug_ok"), s("z_read")
            ra_ok, route_ok, row_ok, slotT_ok, slot_exp_ok = (s("ra_ok"), s("route_ok"), s("row_ok"), s("slotT_ok"), s("slot_exp_ok"))
            slot_w_ok, tanh_ok, wT_ok, z_ok = (s("slot_w_ok"), s("tanh_ok"), s("wT_ok"), s("z_ok"))
            craw = sb("craw", [P, 2, T])
            c_hi, c_lo = sb("c_hi", [P, 2, T], F32R), sb("c_lo", [P, 2, T], F32R)
            w0_hi, w0_lo = sb("w0_hi", [P, KT, D], F32R), sb("w0_lo", [P, KT, D], F32R)
            xt = sb("xt", [P, KT, S])
            x_hi, x_lo = sb("x_hi", [P, KT, S], F32R), sb("x_lo", [P, KT, S], F32R)
            xb = sb("xb", [P, D])
            bias = sb("bias", [P, D])
            wu_hi, wu_lo = sb("wu_hi", [P, KT, UH], F32R), sb("wu_lo", [P, KT, UH], F32R)
            wq_hi, wq_lo = sb("wq_hi", [P, KT, BOT], F32R), sb("wq_lo", [P, KT, BOT], F32R)
            route = sb("route", [BOT + 1, 2 * SLOTS])
            u_val = sb("u_val", [P, 2, BOT])
            bu1, wu2, bu2 = sb("bu1", [P, UH]), sb("wu2", [P, UH]), sb("bu2", [P, 1])
            qaug = sb("qaug", [BOT + 1, S])
            ra = sb("ra", [P, 2 * SLOTS])
            top8 = sb("top8", [P, 8])
            left = sb("left", [P, SLOTS])
            pen = sb("pen", [P, SLOTS])
            slot_w = sb("slot_w", [P, SLOTS])
            sm = sb("sm", [P, 4])
            wT = sb("wT", [P, 2, S])
            ua, ub, uc = sb("ua", [P, UH]), sb("ub", [P, UH]), sb("uc", [P, UH])
        else:
            bottleneck_ok, egate_ok, gatedT_ok, gated_ok, out_ok = (s("bottleneck_ok"), s("egate_ok"), s("gatedT_ok"), s("gated_ok"), s("out_ok"))
            out_read, sc_read = s("out_read"), s("sc_read")
            res_ok, rscore_ok, top_ok, z_hi_ok, z_lo_ok = (s("res_ok"), s("rscore_ok"), s("top_ok"), s("z_hi_ok"), s("z_lo_ok"))
            a_hi, a_lo = sb("a_hi", [P, KT, BN], F32R), sb("a_lo", [P, KT, BN], F32R)
            r_hi, r_lo = sb("r_hi", [P, KT, NE], F32R), sb("r_lo", [P, KT, NE], F32R)
            b_hi, b_lo = sb("b_hi", [P, 4, D], F32R), sb("b_lo", [P, 4, D], F32R)
            sc = sb("sc", [P, NE])
            sc1, sc2 = sb("sc1", [P, NE]), sb("sc2", [P, NE])
            top8, top16 = sb("top8", [P, 8]), sb("top16", [P, 8])
            egate = sb("egate", [P, NE])
            sel = sb("sel", [P, NE])
            sm = sb("sm", [P, 4])
            zg = sb("zg", [P, BN])
            z_hi, z_lo = sb("z_hi", [P, 4, S], F32R), sb("z_lo", [P, 4, S], F32R)
            res = sb("res", [P, D])

        once = ExitStack()

        def tmp(name, shape, dt=F32):
            return once.enter_context(nc.sbuf_tensor(f"L{layer}_once_{name}", shape, dt))

        stage = (attn, row, xnew, xcur)
        NST = len(stage)
        part_of = []
        if first:
            bmask = [buf[:].rearrange("p a t -> p (a t)")[:, 0:D].bitcast(I32) for buf in (probs, masked)]
            brow = tmp("brow", [P, KT * 32])
            bm = tmp("bm", [P, KT, 32])
            blocks = tmp("blocks", [P, P])
            wr, wrT, keysT = tmp("wr", [48, BOT]), tmp("wrT", [BOT, 48]), tmp("keysT", [BOT, SLOTS])
            wvdT = tmp("wvdT", [P, KT, BOT])
            xt_cols = xt[:].rearrange("p k s -> p (k s)")
            valT = ([xb[:, SLOTS * k:SLOTS * k + SLOTS] for k in range(4)]
                    + [xt_cols[:, SLOTS * k:SLOTS * k + SLOTS] for k in range(3)] + [ua[:, :]])
            rkT = tmp("rkT", [48, SLOTS])
            for k in range(KT):
                rows_k = slice(P * k, P * k + P)
                part_of.append((io["w0T"][rows_k], D, k, w0_hi[:, k, :], w0_lo[:, k, :]))
                part_of.append((io["wu1T"][rows_k], UH, None, wu_hi[:, k, :], wu_lo[:, k, :]))
                part_of.append((io["wqT"][rows_k], BOT, None, wq_hi[:, k, :], wq_lo[:, k, :]))
            small = [(blocks[:], io["blocks"]),
                     (wr[:], io["wr"]), (wrT[:], io["wrT"]), (keysT[:], io["keysT"]),
                     (wvdT[:], io["wvdT"].rearrange("(k p) n -> p k n", p=P)),
                     (route[BOT:BOT + 1, :], io["log_rel"]), (bias[:], io["b0"]), (bu1[:], io["bu1"]),
                     (wu2[:], io["wu2"]), (bu2[:], io["bu2"])]
            small += [(valT[k], io["valuesT"][P * k:P * k + P]) for k in range(KT)]
        else:
            rq, rkeysT = tmp("rq", [16, D]), tmp("rkeysT", [16, NE])
            for k in range(KT):
                part_of.append((io["awT"][P * k:P * k + P], BN, None, a_hi[:, k, :], a_lo[:, k, :]))
            for k in range(4):
                part_of.append((io["bwT"][P * k:P * k + P], D, None, b_hi[:, k, :], b_lo[:, k, :]))
            small = [(rq[:], io["rq"]), (rkeysT[:], io["rkeysT"])]
        small += [(ident[:], io["ident"]), (nmask[0:S, :], io["mask"])]
        small_in, chunk_done, prep_pe, prep_dve = s("small_in"), s("chunk_done"), s("prep_pe"), s("prep_dve")
        chunk_in = [s(f"chunk_in{i}") for i in range(NST)]
        bmask_in, brow_ok = [s("bmask_in0"), s("bmask_in1")], s("brow_ok")
        prep = once.enter_context(nc.Block())

        @prep.sync
        def _(sp):
            for dst, src in small:
                sp.dma_start(dst, src).then_inc(small_in, 16)
            if first:
                for k in range(KT):
                    if k >= 2:
                        sp.wait_ge(brow_ok, k - 1)
                    sp.dma_start(bmask[k % 2], io["bmaskT"][P * k:P * k + P]).then_inc(bmask_in[k % 2], 16)
            for i, (src, cols, _, _, _) in enumerate(part_of):
                if i >= NST:
                    sp.wait_ge(chunk_done, i - NST + 1)
                sp.dma_start(stage[i % NST][:, 0:cols], src).then_inc(chunk_in[i % NST], 16)

        @prep.tensor
        def _(pe):
            pe.wait_ge(small_in, 16 * len(small))
            if first:
                pe.wait_ge(brow_ok, KT)
                pe.matmul(wide[:, 0, 0:KT * 32], blocks[:], brow[:], start=True, stop=True)
                pe.matmul(wide[0:48, 1, 0:SLOTS], wrT[:], keysT[:], start=True, stop=True)
                for j in range(2):
                    for k in range(KT):
                        mm = pe.matmul(scores[:, j, 0:BOT], valT[k][:, P * j:P * j + P], wvdT[:, k, :],
                                       start=(k == 0), stop=(k == KT - 1))
                mm.then_inc(prep_pe, 1)
                pe.wait_ge(prep_dve, 1)
                pe.matmul(scores[0:BOT, 2, 0:SLOTS], wr[:], rkT[:], start=True, stop=True).then_inc(prep_pe, 1)
            else:
                for k in range(KT):
                    mm = pe.matmul(wide[:, 0, NE * k:NE * k + NE], rq[:, P * k:P * k + P], rkeysT[:],
                                   start=True, stop=True)
                mm.then_inc(prep_pe, 1)

        @prep.vector
        def _(dve):
            v = nc.vector
            v.memset(half[:], -0.5)
            v.memset(row[:, COL_VAR + 1:ROW], 0.0)
            v.memset(krep[:, :, T:TP].bitcast(F32), 0.0)
            dve.wait_ge(small_in, 16 * len(small))
            v.tensor_scalar(nmask[0:S, :], nmask[0:S, :], -1.0, None, ALU.mult)
            if first:
                v.memset(qaug[BOT:BOT + 1, :], 1.0)
                for k in range(KT):
                    dve.wait_ge(bmask_in[k % 2], 16 * (k // 2 + 1))
                    v.tensor_reduce(brow[:, 32 * k:32 * k + 32],
                                    bmask[k % 2].rearrange("p (n j) -> p n j", j=32), AX.X, ALU.add).then_inc(brow_ok, 1)
                v.tensor_scalar(route[0:BOT, SLOTS:2 * SLOTS], keysT[:], BOT ** -0.5, None, ALU.mult)
                dve.wait_ge(prep_pe, 1)
                v.tensor_copy(rkT[:], wide[0:48, 1, 0:SLOTS]).then_inc(prep_dve, 1)
                v.tensor_scalar(bm[:], wide[:, 0, 0:KT * 32].rearrange("p (k n) -> p k n", k=KT), 0.0, None, ALU.is_gt)
                for j in range(2):
                    v.tensor_copy(u_val[:, j, :], scores[:, j, 0:BOT])
                dve.wait_ge(prep_pe, 2)
                v.tensor_scalar(route[0:BOT, 0:SLOTS], scores[0:BOT, 2, 0:SLOTS], 48 ** -0.5, None, ALU.mult)
            else:
                dve.wait_ge(prep_pe, 1)
                psum = wide[:, 0, :].rearrange("p (k e) -> p k e", k=KT)
                v.tensor_copy(r_hi[:], psum)
                dve.drain()
                v.tensor_tensor(r_lo[:], psum, r_hi[:].bitcast(F32), ALU.subtract)
            dve.drain()
            for i, (_, cols, k, hi, lo) in enumerate(part_of):
                raw = stage[i % NST][:, 0:cols]
                dve.wait_ge(chunk_in[i % NST], 16 * (i // NST + 1))
                if k is not None:
                    v.tensor_tensor(raw.rearrange("p (n j) -> p n j", j=32), raw.rearrange("p (n j) -> p n j", j=32),
                                    bm[:, k, :].unsqueeze(2).broadcast_to([P, 32, 32]), ALU.mult)
                    dve.drain()
                v.tensor_copy(hi, raw)
                dve.drain()
                v.tensor_tensor(lo, raw, hi.bitcast(F32), ALU.subtract).then_inc(chunk_done, 1)

        once.close()

        STEPS = 40

        def turns(eng, body):
            for b, before, cross, after in ((-1, True, False, False), (0, True, True, False)):
                w = Counts(eng)
                body(b, w, before, cross, after)
                w.take_off()
            with eng.Fori(1, B - 1) as b:
                w = Counts(eng)
                body(b, w, True, True, True)
                w.take_off()
            for b, before, cross, after in ((B - 1, False, True, True), (B, False, False, True)):
                w = Counts(eng)
                body(b, w, before, cross, after)
                w.take_off()

        def copied(m):
            return copied_v if m % 3 == 0 else copied_s

        block = ctx.enter_context(nc.Block())

        @block.sync
        def _(sp):
            ks, qs = io["ks"], io["qs"]

            def load_keys(w, nb, h):
                sp.wait_ge(k_free[h], w.next(k_free[h]))
                for c in range(4):
                    src = ks[c % 2, nb].rearrange("(g d) t -> d g t", d=HD)
                    sp.dma_start(krep[HD * c:HD * c + HD, 4 * h:4 * h + 4, 0:T].bitcast(F32),
                                 src[:, 4 * h:4 * h + 4, :]).then_inc(ld_kq[h], 16)

            def load_values(w, vb, h):
                sp.wait_ge(v_free[h], w.next(v_free[h]))
                sp.dma_start(val[:, :, P * h:P * h + P],
                             io["ctx"][vb].rearrange("(j t) c -> t j c", t=TC)[:, :, P * h:P * h + P]).then_inc(ld_v[h], 16)

            def store_queries(w, nb, h):
                sp.wait_ge(q_lo_ok, w.next(q_lo_ok))
                for part, src in ((0, qT_hi), (1, qT_lo)):
                    sp.dma_start(qs[part, nb][4 * h:4 * h + 4].rearrange("k p s -> p k s"),
                                 src[:, 4 * h:4 * h + 4, :].bitcast(F32)).then_inc(q_stored[h], 16)

            def load_queries(w, nb, h):
                sp.wait_ge(q_stored[h], w.next(q_stored[h], 32))
                for c in range(4):
                    src = qs[c // 2, nb][4 * h:4 * h + 4].rearrange("g (r d) s -> d g r s", d=HD)
                    sp.dma_start(qrep[HD * c:HD * c + HD, 4 * h:4 * h + 4, :, :].bitcast(F32), src).then_inc(ld_kq[h], 16)

            def body(b, w, before, cross, after):
                nb = b + 1
                if before and first:
                    sp.wait_ge(xt_free, w.next(xt_free))
                    sp.dma_start(xt[:], io["xT"][nb]).then_inc(ld_xt, 16)
                    sp.dma_start(craw[:], io["ctxT"][nb]).then_inc(ld_c, 16)
                    sp.wait_ge(x_free, w.next(x_free))
                    sp.dma_start(xb[0:S, :], io["x"][nb]).then_inc(ld_x, 16)
                if cross:
                    load_values(w, b, 1)
                if before and first:
                    sp.wait_ge(c_lo_ok, w.next(c_lo_ok))
                    for part, src in ((0, c_hi), (1, c_lo)):
                        sp.dma_start(ks[part, nb].rearrange("(h p) t -> p h t", p=P), src[:, :, 0:T].bitcast(F32)).then_inc(c_stored, 16)
                    sp.wait_ge(c_stored, w.next(c_stored, 32))
                if before:
                    if not first:
                        sp.wait_ge(x_free, w.next(x_free))
                        sp.dma_start(xnew[0:S, :], io["x4"][nb]).then_inc(ld_x, 16)
                    load_keys(w, nb, 0)
                    load_values(w, nb, 0)
                    store_queries(w, nb, 0)
                    load_queries(w, nb, 0)
                    store_queries(w, nb, 1)
                    load_keys(w, nb, 1)
                    load_queries(w, nb, 1)

            turns(sp, body)

        @block.gpsimd
        def _(pool):
            def root(w, i):
                pool.wait_ge(var_ok[i], w.next(var_ok[i]))
                nc.gpsimd.tensor_scalar(veps[0:S, i:i + 1], mv[0:S, 2 * i + 1:2 * i + 2], EPS, None, ALU.add)
                pool.drain()
                nc.gpsimd.tensor_tensor(rstd[0:S, i:i + 1], veps[0:S, i:i + 1], half[0:S], ALU.pow).then_inc(rstd_ok[i], 1)

            def body(b, w, before, cross, after):
                if after:
                    pool.wait_ge(attn_out, w.next(attn_out))
                    nc.gpsimd.tensor_tensor(attn[0:S, :], attn[0:S, :], xcur[0:S, :], ALU.add).then_inc(sum_ok, 1)
                    pool.drain().then_inc(sum_done, 1)
                    root(w, 1)
                if before and first:
                    pool.wait_ge(x_hi_ok, w.next(x_hi_ok))
                    nc.gpsimd.tensor_tensor(x_lo[:], xt[:], x_hi[:].bitcast(F32), ALU.subtract).then_inc(split_x, 1)
                    pool.drain().then_inc(xt_free, 1)
                    pool.wait_ge(ld_x, w.next(ld_x, 16))
                    nc.gpsimd.tensor_tensor(xb[0:S], xb[0:S], bias[0:S], ALU.add).then_inc(xb_ok, 1)
                    root(w, 0)
                if after and not first:
                    root(w, 2)

            if first:
                pool.sem_inc(xt_free, 1)
            turns(pool, body)

        def stats(src, i, signal):
            for h in range(2):
                nc.vector.bn_stats(st[0:S, 12 * i + 6 * h:12 * i + 6 * h + 6], src[0:S, 512 * h:512 * h + 512])
            nc.vector.drain()
            nc.vector.bn_aggr(mv[0:S, 2 * i:2 * i + 2], st[0:S, 12 * i:12 * i + 12]).then_inc(signal, 1)

        def normed(dst, src, i, signal):
            nc.vector.tensor_scalar(dst[0:S, 0:D], src[0:S, 0:D], mv[0:S, 2 * i:2 * i + 1], rstd[0:S, i:i + 1],
                                    ALU.subtract, ALU.mult).then_inc(signal, 1)

        @block.tensor
        def _(pe):
            def turn_half(bank, src, h):
                for j in range(4):
                    k = 4 * h + j
                    mm = pe.transpose(bank[:, S * j:S * j + S], src[0:S, P * k:P * k + P], ident[0:S, 0:S])
                return mm

            def products(out, left, right, cols, kt, start, stop):
                n = 0
                for k in range(kt):
                    for a, c in split_passes(left[0], left[1], right[0], right[1]):
                        if start <= n < stop:
                            mm = pe.matmul(out, a[:, k, :], c[:, k, cols], start=(n == 0), stop=(n == 3 * kt - 1))
                        n += 1
                return mm

            def cross_step(w, n):
                if n < NH:
                    u, gi = divmod(n, 4)
                    gq, r = divmod(u, NR)
                    g = 4 * gq + gi
                    if n % 16 == 0:
                        pe.wait_ge(ld_kq[gq], w.next(ld_kq[gq], 16 * 8))
                    pe.matmul(scores[0:S, n % 3, 0:TP], qrep[:, g, r, :], krep[:, g, :],
                              start=True, stop=True).then_inc(score_ok, 1)
                m = n - 2
                if 0 <= m < NH:
                    pe.wait_ge(prob_ok, w.next(prob_ok))
                    if m >= 2:
                        pe.wait_ge(copied(m - 2), w.next(copied(m - 2)))
                    for j in range(TJ):
                        mm = pe.transpose(turned[0:TC, m % 2, S * j:S * j + S],
                                          probs[0:S, m % 4, TC * j:TC * j + TC], ident[0:S, 0:S])
                        if j == 0 and m in (14, 30):
                            mm.then_inc(k_free[m // 16], 1)
                    mm.then_inc(turned_v if m % 3 == 0 else turned_s, 1)
                if n >= 8 and n % 4 == 0:
                    pv(w, n // 4 - 2)

            def pv(w, u):
                gq, r = divmod(u, NR)
                if r == 0:
                    pe.wait_ge(ld_v[gq], w.next(ld_v[gq], 16))
                if u == NH // 4 - 1:
                    pe.wait_ge(copied(NH - 2), w.next(copied(NH - 2)))
                    pe.wait_ge(copied(NH - 1), w.next(copied(NH - 1)))
                for j in range(TJ):
                    for gi in range(4):
                        g = 4 * gq + gi
                        mm = pe.matmul(wide[HD * gi:HD * gi + HD, gq, S * r:S * r + S],
                                       val[:, j, HD * g:HD * g + HD], probsT[:, (4 * u + gi) % 8, j, :],
                                       start=(j == 0), stop=(j == TJ - 1))
                        if u == 4 and j == 0 and gi == 0:
                            mm.then_inc(v_free[0], 1)
                if r == NR - 1:
                    mm.then_inc((pv_s, pv_v)[gq], 1)

            def after_step(w, n):
                if n == 1:
                    pe.wait_ge(oT_v, w.next(oT_v))
                    for h in range(2):
                        for j in range(4):
                            mm = pe.transpose(wide[0:S, h, P * j:P * j + P], oT[:, 4 * h + j, :], ident[:, :])
                            if h == 0 and j == 0:
                                mm.then_inc(v_free[1], 1)
                        mm.then_inc(attn_ok, 1)
                if n == 5:
                    pe.wait_ge(attn_read, w.next(attn_read, 2))
                if n == 9:
                    pe.wait_ge(x2_ok, w.next(x2_ok))
                    turn_half(spare, row, 0).then_inc(turn2_ok, 1)
                if n == 12:
                    pe.wait_ge(lo2_ok, w.next(lo2_ok))
                    turn_half(spare, row, 1).then_inc(turn2_ok, 1)
                if n == 15:
                    pe.wait_ge(lo2_ok, w.next(lo2_ok))
                if first:
                    if n in (15, 16):
                        mm = products(spare[0:S, 0:UH], (tT_hi, tT_lo), (wu_hi, wu_lo), slice(0, UH), KT,
                                      12 * (n - 15), 12 * (n - 14))
                    if n in (17, 18):
                        mm = products(spare[0:BOT, UH:UH + S], (wq_hi, wq_lo), (tT_hi, tT_lo), slice(0, S), KT,
                                      12 * (n - 17), 12 * (n - 16))
                    if n == 18:
                        mm.then_inc(gate_h_ok, 1)
                    if n == 21:
                        pe.wait_ge(qaug_ok, w.next(qaug_ok))
                        pe.matmul(spare[0:S, :], qaug[:, :], route[:, :], start=True, stop=True).then_inc(route_ok, 1)
                    if n == 31:
                        pe.wait_ge(slot_w_ok, w.next(slot_w_ok))
                        for j in range(2):
                            mm = pe.transpose(spare[:, S * j:S * j + S], slot_w[0:S, P * j:P * j + P], ident[0:S, 0:S])
                        mm.then_inc(slotT_ok, 1)
                    if n == 33:
                        pe.wait_ge(wT_ok, w.next(wT_ok))
                        for j in range(2):
                            mm = pe.matmul(spare[0:S, UH:UH + BOT], wT[:, j, :], u_val[:, j, :], start=(j == 0), stop=(j == 1))
                        mm.then_inc(z_ok, 1)
                    if n == 39:
                        pe.wait_ge(z_read, w.next(z_read))
                else:
                    if n == 15:
                        products(wide[0:S, 1, 0:NE], (tT_hi, tT_lo), (r_hi, r_lo), slice(0, NE), KT, 0, 24).then_inc(rscore_ok, 1)
                    if 16 <= n < 22:
                        mm = products(spare[0:S, :], (tT_hi, tT_lo), (a_hi, a_lo), slice(0, BN), KT,
                                      4 * (n - 16), 4 * (n - 15))
                    if n == 21:
                        mm.then_inc(bottleneck_ok, 1)
                    if n == 23:
                        pe.wait_ge(sc_read, w.next(sc_read))
                    if n == 25:
                        pe.wait_ge(gated_ok, w.next(gated_ok))
                        for j in range(4):
                            mm = pe.transpose(spare[:, S * j:S * j + S], zg[0:S, P * j:P * j + P], ident[0:S, 0:S])
                        mm.then_inc(gatedT_ok, 1)
                    if n == 28:
                        pe.wait_ge(z_lo_ok, w.next(z_lo_ok))
                    if n == 34:
                        pe.wait_ge(out_read, w.next(out_read))
                    for h, n0 in ((0, 28), (1, 34)):
                        if n0 <= n < n0 + 3:
                            mm = products(spare[0:S, :], (z_hi, z_lo), (b_hi, b_lo), slice(512 * h, 512 * h + 512), 4,
                                          4 * (n - n0), 4 * (n - n0 + 1))
                            if n == n0 + 2:
                                mm.then_inc(out_ok, 1)
                    if n == 39:
                        pe.wait_ge(out_read, w.next(out_read))

            def before_step(w, n, cross):
                if first:
                    if n == 9:
                        pe.wait_ge(split_x, w.next(split_x))
                    if n in (16, 23):
                        pe.wait_ge(lin_read, w.next(lin_read))
                    for h, n0 in ((0, 9), (1, 16)):
                        if n0 <= n < n0 + 6:
                            mm = products(wide[0:S, 1, :], (x_hi, x_lo), (w0_hi, w0_lo), slice(512 * h, 512 * h + 512),
                                          KT, 4 * (n - n0), 4 * (n - n0 + 1))
                            if n == n0 + 5:
                                mm.then_inc(lin_ok, 1)
                if n == 26:
                    if first:
                        pe.wait_ge(x_ok, w.next(x_ok))
                    else:
                        pe.wait_ge(ld_x, w.next(ld_x, 16))
                    turn_half(wide[:, 0, :], xnew, 0).then_inc(turn_ok, 1)
                if n in (29, 32):
                    pe.wait_ge(q_read, w.next(q_read))
                if n == 29:
                    turn_half(wide[:, 0, :], xnew, 1).then_inc(turn_ok, 1)

            def body(b, w, before, cross, after):
                for n in range(STEPS):
                    if cross:
                        cross_step(w, n)
                    if cross and n == 25:
                        pe.wait_ge(oT_s, w.next(oT_s))
                    if after:
                        after_step(w, n)
                    if before:
                        before_step(w, n, cross)

            turns(pe, body)

        @block.scalar
        def _(act):
            def after_step(w, n):
                if n in (10, 13):
                    h = n // 13
                    act.wait_ge(turn2_ok, w.next(turn2_ok))
                    nc.scalar.copy(tT_hi[:, 4 * h:4 * h + 4, :],
                                   spare[:, 0:4 * S].rearrange("p (k s) -> p k s", s=S)).then_inc(hi2_ok, 1)
                if first:
                    if n == 20:
                        act.wait_ge(gate_h_read, w.next(gate_h_read))
                        nc.scalar.copy(qaug[0:BOT, :], spare[0:BOT, UH:UH + S]).then_inc(qaug_ok, 1)
                    if n == 22:
                        act.wait_ge(route_ok, w.next(route_ok))
                        nc.scalar.copy(ra[0:S, :], spare[0:S, :]).then_inc(ra_ok, 1)
                    if n == 22:
                        act.wait_ge(gelu_arg_ok, w.next(gelu_arg_ok))
                        nc.scalar.activation(uc[0:S, :], ub[0:S, :], ACT.Tanh, scale=0.7978845608028654).then_inc(tanh_ok, 1)
                    if n == 27:
                        act.wait_ge(least_pen_ok, w.next(least_pen_ok))
                        nc.scalar.activation(slot_w[0:S, :], pen[0:S, :], ACT.Exp, bias=sm[0:S, 1:2], scale=1.0,
                                             accum_out=sm[0:S, 2:3]).then_inc(slot_exp_ok, 1)
                    if n == 32:
                        act.wait_ge(slotT_ok, w.next(slotT_ok))
                        nc.scalar.copy(wT[:, :, :], spare[:, 0:2 * S].rearrange("p (j s) -> p j s", s=S)).then_inc(wT_ok, 1)
                else:
                    if n == 18:
                        act.wait_ge(top_ok, w.next(top_ok))
                        nc.scalar.activation(egate[0:S, :], sc[0:S, :], ACT.Exp, bias=sm[0:S, 1:2], scale=1.0).then_inc(egate_ok, 1)
                    if n == 26:
                        act.wait_ge(gatedT_ok, w.next(gatedT_ok))
                        nc.scalar.copy(z_hi[:, :, :], spare[:, 0:4 * S].rearrange("p (j s) -> p j s", s=S)).then_inc(z_hi_ok, 1)

            def before_step(w, n):
                if first and n == 4:
                    act.wait_ge(ld_xt, w.next(ld_xt, 16))
                    nc.scalar.copy(x_hi[:], xt[:]).then_inc(x_hi_ok, 1)
                if first and n == 6:
                    act.wait_ge(ld_c, w.next(ld_c, 16))
                    nc.scalar.mul(c_hi[:, :, 0:T], craw[:], -float(HD) ** -0.5).then_inc(c_hi_ok, 1)
                if n in (27, 30):
                    h = n // 30
                    act.wait_ge(turn_ok, w.next(turn_ok))
                    nc.scalar.copy(qT_hi[:, 4 * h:4 * h + 4, :],
                                   wide[:, 0, 0:4 * S].rearrange("p (k s) -> p k s", s=S)).then_inc(q_hi_ok, 1)

            def cross_step(w, n):
                m = n - 3
                if 0 <= m < NH and m % 3:
                    act.wait_ge(turned_s, w.next(turned_s))
                    nc.scalar.copy(probsT[:, m % 8, :, :],
                                   turned[0:TC, m % 2, 0:TJ * S].rearrange("p (j s) -> p j s", s=S)).then_inc(copied_s, 1)
                if n < NH:
                    act.wait_ge(least_ok, w.next(least_ok))
                    nc.scalar.activation(probs[0:S, n % 4, :], masked[0:S, n % 3, :], ACT.Exp,
                                         bias=least[0:S, n:n + 1], scale=-1.0,
                                         accum_out=rsum[0:S, n:n + 1]).then_inc(prob_ok, 1)
                if n == 22:
                    act.wait_ge(pv_s, w.next(pv_s))
                    nc.scalar.copy(oT[:, 0:4, :], wide[:, 0, 0:4 * S].rearrange("p (u s) -> p u s", s=S)).then_inc(oT_s, 1)

            def body(b, w, before, cross, after):
                for n in range(STEPS):
                    if cross:
                        cross_step(w, n)
                    if after:
                        if n == 5:
                            act.wait_ge(sum_done, w.next(sum_done))
                        after_step(w, n)
                    if cross and n == 5:
                        nc.scalar.copy(xcur[0:S, :], xnew[0:S, :]).then_inc(x_moved, 1)
                    if before:
                        before_step(w, n)
                if after and first:
                    act.wait_ge(row_ok, w.next(row_ok))
                    act.dma_start(io["rows"][b - 1], row[0:S, :]).then_inc(stored, 16)
                if after and not first:
                    act.wait_ge(res_ok, w.next(res_ok))
                    act.dma_start(io["out"][b - 1], res[0:S, :]).then_inc(stored, 16)

            turns(act, body)

        @block.vector
        def _(dve):
            v = nc.vector

            def cross_step(w, n):
                m = n - 3
                if 0 <= m < NH and m % 3 == 0:
                    dve.wait_ge(turned_v, w.next(turned_v))
                    v.tensor_copy(probsT[:, m % 8, :, :],
                                  turned[0:TC, m % 2, 0:TJ * S].rearrange("p (j s) -> p j s", s=S)).then_inc(copied_v, 1)
                if n < NH:
                    dve.wait_ge(score_ok, w.next(score_ok))
                    v.tensor_tensor_reduce(
                        out=masked[0:S, n % 3, :], in0=scores[0:S, n % 3, 0:T], in1=nmask[0:S, :],
                        scale=1.0, scalar=HUGE, op0=ALU.add, op1=ALU.min,
                        accum_out=least[0:S, n:n + 1]).then_inc(least_ok, 1)
                if n == 14:
                    dve.wait_ge(x_moved, w.next(x_moved))
                    if not first:
                        dve.sem_inc(x_free, 1)
                if n == 37:
                    dve.wait_ge(pv_v, w.next(pv_v))
                    v.reciprocal(rinv[0:S, :], rsum[0:S, :])
                    v.tensor_copy(oT[:, 4:8, :], wide[:, 1, 0:4 * S].rearrange("p (u s) -> p u s", s=S)).then_inc(oT_v, 1)

            def after_step(w, n):
                if n == 2:
                    for gq in range(2):
                        dve.wait_ge(attn_ok, w.next(attn_ok))
                        v.tensor_tensor(
                            attn[0:S, 512 * gq:512 * gq + 512].rearrange("p (gi r d) -> p r gi d", gi=4, r=NR),
                            wide[0:S, gq, :].rearrange("p (r gi d) -> p r gi d", r=NR, gi=4),
                            rinv[0:S, 16 * gq:16 * gq + 16].rearrange("p (r gi) -> p r gi", r=NR)
                            .unsqueeze(3).broadcast_to([S, NR, 4, HD]), ALU.mult).then_inc(attn_read, 1)
                    dve.drain().then_inc(attn_out, 1)
                if n == 4:
                    dve.wait_ge(sum_ok, w.next(sum_ok))
                    stats(attn, 1, var_ok[1])
                if n == 6:
                    dve.wait_ge(rstd_ok[1], w.next(rstd_ok[1]))
                    if first:
                        dve.wait_ge(stored, w.next(stored, 16))
                    normed(row, attn, 1, x2_ok)
                if n in (11, 14):
                    h = n // 14
                    dve.wait_ge(hi2_ok, w.next(hi2_ok))
                    v.tensor_tensor(tT_lo[:, 4 * h:4 * h + 4, :], spare[:, 0:4 * S].rearrange("p (k s) -> p k s", s=S),
                                    tT_hi[:, 4 * h:4 * h + 4, :].bitcast(F32), ALU.subtract).then_inc(lo2_ok, 1)
                if first:
                    slot_ffn_step(w, n)
                else:
                    routed_ffn_step(w, n)

            def slot_ffn_step(w, n):
                if n == 9:
                    dve.drain()
                    for h in range(2):
                        v.bn_stats(st[0:S, 24 + 6 * h:30 + 6 * h], row[0:S, 512 * h:512 * h + 512])
                if n == 10:
                    dve.drain()
                    v.bn_aggr(mv[0:S, 4:6], st[0:S, 24:36])
                if n == 13:
                    dve.drain()
                    v.tensor_copy(row[0:S, COL_VAR:COL_VAR + 1], mv[0:S, 5:6])
                if n == 19:
                    dve.wait_ge(gate_h_ok, w.next(gate_h_ok))
                    v.tensor_tensor(ua[0:S, :], spare[0:S, 0:UH], bu1[0:S, :], ALU.add).then_inc(gate_h_read, 1)
                    dve.drain()
                    v.tensor_tensor(ub[0:S, :], ua[0:S, :], ua[0:S, :], ALU.mult)
                if n == 20:
                    dve.drain()
                    v.tensor_scalar(ub[0:S, :], ub[0:S, :], 0.044715, 1.0, ALU.mult, ALU.add)
                    dve.drain()
                    v.tensor_tensor(ub[0:S, :], ub[0:S, :], ua[0:S, :], ALU.mult).then_inc(gelu_arg_ok, 1)
                if n == 23:
                    dve.wait_ge(ra_ok, w.next(ra_ok))
                    v.max(top8[0:S, :], ra[0:S, 0:SLOTS])
                    dve.drain()
                    v.match_replace(out=left[0:S, :], in_to_replace=top8[0:S, :], in_values=ra[0:S, 0:SLOTS], imm_value=-HUGE)
                if n == 25:
                    dve.drain()
                    v.tensor_tensor(left[0:S, :], left[0:S, :], ra[0:S, 0:SLOTS], ALU.not_equal)
                    dve.drain()
                    v.tensor_scalar(left[0:S, :], left[0:S, :], HUGE, -HUGE, ALU.mult, ALU.add)
                if n == 26:
                    dve.drain()
                    v.tensor_tensor_reduce(out=pen[0:S, :], in0=ra[0:S, SLOTS:2 * SLOTS], in1=left[0:S, :], scale=1.0,
                                           scalar=-HUGE, op0=ALU.add, op1=ALU.max, accum_out=sm[0:S, 0:1])
                    dve.drain()
                    v.tensor_scalar(sm[0:S, 1:2], sm[0:S, 0:1], -1.0, None, ALU.mult).then_inc(least_pen_ok, 1)
                if n == 27:
                    dve.wait_ge(tanh_ok, w.next(tanh_ok))
                    v.tensor_scalar(uc[0:S, :], uc[0:S, :], 1.0, 0.5, ALU.add, ALU.mult)
                if n == 29:
                    dve.wait_ge(slot_exp_ok, w.next(slot_exp_ok))
                    v.reciprocal(sm[0:S, 2:3], sm[0:S, 2:3])
                    dve.drain()
                    v.tensor_tensor(uc[0:S, :], uc[0:S, :], ua[0:S, :], ALU.mult)
                    v.tensor_scalar(slot_w[0:S, :], slot_w[0:S, :], sm[0:S, 2:3], None, ALU.mult).then_inc(slot_w_ok, 1)
                if n == 32:
                    dve.drain()
                    v.tensor_tensor(uc[0:S, :], uc[0:S, :], wu2[0:S, :], ALU.mult)
                    dve.drain()
                    v.tensor_reduce(sm[0:S, 3:4], uc[0:S, :], AX.X, ALU.add)
                if n == 34:
                    dve.wait_ge(z_ok, w.next(z_ok))
                    v.tensor_copy(row[0:S, COL_Z:COL_Z + BOT], spare[0:S, UH:UH + BOT]).then_inc(z_read, 1)
                    dve.drain()
                    v.tensor_tensor(row[0:S, COL_LEARNED:COL_LEARNED + 1], sm[0:S, 3:4], bu2[0:S, :], ALU.add)
                    dve.drain().then_inc(row_ok, 1)

            def routed_ffn_step(w, n):
                if n == 16:
                    dve.wait_ge(rscore_ok, w.next(rscore_ok))
                    v.tensor_copy(sc[0:S, :], wide[0:S, 1, 0:NE]).then_inc(sc_read, 1)
                    dve.drain()
                    v.max(top8[0:S, :], sc[0:S, :])
                    dve.drain()
                    v.tensor_scalar(sm[0:S, 1:2], top8[0:S, 0:1], -1.0, None, ALU.mult).then_inc(top_ok, 1)
                if n == 18:
                    v.match_replace(out=sc1[0:S, :], in_to_replace=top8[0:S, :], in_values=sc[0:S, :], imm_value=-HUGE)
                    dve.drain()
                    v.max(top16[0:S, :], sc1[0:S, :])
                if n == 19:
                    dve.drain()
                    v.match_replace(out=sc2[0:S, :], in_to_replace=top16[0:S, :], in_values=sc1[0:S, :], imm_value=-HUGE)
                if n == 20:
                    dve.drain()
                    v.tensor_tensor(sel[0:S, :], sc2[0:S, :], sc[0:S, :], ALU.not_equal)
                    dve.drain()
                    dve.wait_ge(egate_ok, w.next(egate_ok))
                    v.tensor_tensor(sel[0:S, :], sel[0:S, :], egate[0:S, :], ALU.mult)
                if n == 21:
                    dve.drain()
                    v.tensor_reduce(sm[0:S, 2:3], sel[0:S, :], AX.X, ALU.add)
                    dve.drain()
                    v.reciprocal(sm[0:S, 2:3], sm[0:S, 2:3])
                if n == 22:
                    dve.drain()
                    v.tensor_scalar(sel[0:S, :], sel[0:S, :], sm[0:S, 2:3], None, ALU.mult)
                    dve.drain()
                if n == 23:
                    dve.wait_ge(bottleneck_ok, w.next(bottleneck_ok))
                    v.tensor_tensor(zg[0:S, :].rearrange("p (e k) -> p e k", k=RANK),
                                    spare[0:S, :].rearrange("p (e k) -> p e k", k=RANK),
                                    sel[0:S, :].unsqueeze(2).broadcast_to([S, NE, RANK]), ALU.mult).then_inc(gated_ok, 1)
                if n == 27:
                    dve.wait_ge(z_hi_ok, w.next(z_hi_ok))
                    v.tensor_tensor(z_lo[:, :, :], spare[:, 0:4 * S].rearrange("p (j s) -> p j s", s=S),
                                    z_hi[:, :, :].bitcast(F32), ALU.subtract).then_inc(z_lo_ok, 1)
                if n in (32, 38):
                    h = n // 38
                    if h == 0:
                        dve.wait_ge(stored, w.next(stored, 16))
                    cols = slice(512 * h, 512 * h + 512)
                    dve.wait_ge(out_ok, w.next(out_ok))
                    v.scalar_tensor_tensor(out=res[0:S, cols], in0=spare[0:S, :], scalar=2.0,
                                           in1=row[0:S, cols], op0=ALU.mult, op1=ALU.add).then_inc(out_read, 1)
                if n == 38:
                    dve.drain()
                    stats(res, 2, var_ok[2])
                if n == 39:
                    dve.wait_ge(rstd_ok[2], w.next(rstd_ok[2]))
                    normed(res, res, 2, res_ok)

            def before_step(w, n):
                if first:
                    if n == 8:
                        dve.wait_ge(c_hi_ok, w.next(c_hi_ok))
                        v.scalar_tensor_tensor(out=c_lo[:, :, 0:T], in0=craw[:], scalar=-float(HD) ** -0.5,
                                               in1=c_hi[:, :, 0:T].bitcast(F32), op0=ALU.mult, op1=ALU.subtract).then_inc(c_lo_ok, 1)
                    if n == 15:
                        dve.wait_ge(xb_ok, w.next(xb_ok))
                    if n in (15, 22):
                        cols = slice(0, 512) if n == 15 else slice(512, 1024)
                        dve.wait_ge(lin_ok, w.next(lin_ok))
                        v.tensor_tensor(xb[0:S, cols], wide[0:S, 1, :], xb[0:S, cols], ALU.add).then_inc(lin_read, 1)
                    if n == 22:
                        dve.drain()
                        stats(xb, 0, var_ok[0])
                    if n == 24:
                        dve.wait_ge(rstd_ok[0], w.next(rstd_ok[0]))
                        normed(xnew, xb, 0, x_ok)
                        dve.drain().then_inc(x_free, 1)
                if n in (28, 31):
                    h = n // 31
                    dve.wait_ge(q_hi_ok, w.next(q_hi_ok))
                    v.tensor_tensor(qT_lo[:, 4 * h:4 * h + 4, :], wide[:, 0, 0:4 * S].rearrange("p (k s) -> p k s", s=S),
                                    qT_hi[:, 4 * h:4 * h + 4, :].bitcast(F32), ALU.subtract).then_inc(q_read, 1)
                    dve.drain().then_inc(q_lo_ok, 1)

            def body(b, w, before, cross, after):
                for n in range(STEPS):
                    if cross:
                        cross_step(w, n)
                    if after:
                        after_step(w, n)
                    if before:
                        before_step(w, n)

            for h in range(2):
                dve.sem_inc(k_free[h], 1)
                dve.sem_inc(v_free[h], 1)
            dve.sem_inc(x_free, 1)
            dve.sem_inc(stored, 16)
            turns(dve, body)
            dve.wait_ge(stored, 16)
            dve.sem_inc(stored, -16)


def self_attention(nc, io, sem):
    NBLK = S // 8
    NC = NBLK // 2
    TH = NC * P
    NKV, QPG, DH = 8, 4, 128
    UNITS = QPG + 2
    CHUNKS = (slice(0, 512), slice(512, TH))

    with ExitStack() as ctx:
        def sb(name, shape, dt=F32):
            return ctx.enter_context(nc.sbuf_tensor(f"sa_{name}", shape, dt))

        feat = ctx.enter_context(nc.psum_tensor("sa_feat", [P, 2, 2, 512], F32))
        score = ctx.enter_context(nc.psum_tensor("sa_score", [P, 512], F32))
        ring = ctx.enter_context(nc.psum_tensor("sa_ring", [P, 3, 512], F32))

        ident, causal = sb("ident", [P, P]), sb("causal", [P, 32])
        gate = sb("gate", [P, NBLK])
        half_exp = sb("half_exp", [P, 1])
        x_hi, x_lo = sb("x_hi", [P, KT, TH], F32R), sb("x_lo", [P, KT, TH], F32R)
        acc = sb("acc", [P, NC, D])
        st, mv, veps, rstd = sb("st", [P, 12]), sb("mv", [P, 2]), sb("veps", [P, 1]), sb("rstd", [P, 1])

        gate_stage(nc, io, sem, ident, causal, half_exp, gate, ring, NBLK)
        for half in range(2):
            load_half(nc, io, sem, half, NC, ident, half_exp, gate, x_hi, x_lo, acc, st, mv, veps, rstd, feat, ring)
            heads_half(nc, io, sem, half, NC, TH, NKV, QPG, DH, UNITS, CHUNKS,
                       ident, causal, x_hi, x_lo, acc, feat, score, ring)
            store_half(nc, io, sem, half, NC, half_exp, acc, st, mv, veps, rstd)


def gate_stage(nc, io, sem, ident, causal, half_exp, gate, ring, NBLK):
    with ExitStack() as ctx:
        def sb(name, shape):
            return ctx.enter_context(nc.sbuf_tensor(f"gate_{name}", shape, F32))

        pair = sb("pair", [P, NBLK, 2])
        ones, w1, gb = sb("ones", [P, P]), sb("w1", [P, 1]), sb("gb", [P, 1])
        lv, lsum, u, t = sb("lv", [P, NBLK]), sb("lsum", [P, 1]), sb("u", [P, NBLK]), sb("t", [P, NBLK])
        mean = sb("mean", [P, 1])
        loaded, log_ok, sum_ok, tanh_ok, arg_ok, tanh2_ok = (
            sem(f"gate_{n}") for n in ("loaded", "log", "sum", "tanh", "arg", "tanh2"))
        block = ctx.enter_context(nc.Block())
        srcs = 8

        @block.sync
        def _(sp):
            for dst, src in ((ident, "ident"), (causal, "causal"), (ones, "ones"), (w1, "gate_w1"), (gb, "gate_bias")):
                sp.dma_start(dst[:], io[src]).then_inc(loaded, 16)
            rows = io["rows"].rearrange("b (c l) n -> l b c n", l=8)
            for l in range(srcs):
                sp.dma_start(pair[16 * l:16 * l + 16, :, :], rows[l, :, :, COL_LEARNED:COL_VAR + 1]).then_inc(loaded, 16)

        @block.scalar
        def _(act):
            act.wait_ge(loaded, 16 * (5 + srcs))
            nc.scalar.activation(t[:], pair[:, :, 0], ACT.Tanh, scale=0.5).then_inc(tanh_ok, 1)
            nc.scalar.activation(lv[:], pair[:, :, 1], ACT.Ln, bias=1.0, scale=1.0, accum_out=lsum[:]).then_inc(log_ok, 1)
            act.wait_ge(arg_ok, 1)
            nc.scalar.activation(t[:], u[:], ACT.Tanh, scale=0.5).then_inc(tanh2_ok, 1)

        @block.tensor
        def _(pe):
            pe.wait_ge(log_ok, 1)
            pe.matmul(ring[:, 0, 0:1], ones[:], lsum[:], start=True, stop=True).then_inc(sum_ok, 1)

        @block.vector
        def _(dve):
            v = nc.vector
            v.memset(half_exp[:], -0.5)
            dve.wait_ge(tanh_ok, 1)
            v.tensor_scalar(t[:], t[:], 1.0, 1.25, ALU.add, ALU.mult)
            dve.wait_ge(sum_ok, 1)
            v.tensor_scalar(mean[:], ring[:, 0, 0:1], 1.0 / (B * S), 1e-6, ALU.mult, ALU.add)
            dve.drain()
            v.reciprocal(mean[:], mean[:])
            dve.drain()
            v.tensor_scalar(lv[:], lv[:], mean[:, 0:1], 0.5, ALU.mult, ALU.mult)
            dve.drain()
            v.tensor_tensor(u[:], lv[:], t[:], ALU.add)
            dve.drain()
            v.tensor_scalar(u[:], u[:], 0.0, 5.0, ALU.max, ALU.min)
            dve.drain()
            v.tensor_scalar(u[:], u[:], -0.5, 1.0 / 1.5, ALU.add, ALU.mult)
            dve.drain()
            v.tensor_scalar(u[:], u[:], 0.0, 1.0, ALU.max, ALU.min)
            dve.drain()
            v.tensor_scalar(u[:], u[:], w1[:, 0:1], gb[:, 0:1], ALU.mult, ALU.add).then_inc(arg_ok, 1)
            dve.wait_ge(tanh2_ok, 1)
            v.tensor_scalar(t[:], t[:], 1.0, 0.5, ALU.add, ALU.mult)
            dve.drain()
            v.tensor_scalar(u[:], t[:], 0.05, None, ALU.is_ge)
            dve.drain()
            v.tensor_tensor(gate[:], t[:], u[:], ALU.mult)


def load_half(nc, io, sem, half, NC, ident, half_exp, gate, x_hi, x_lo, acc, st, mv, veps, rstd, feat, ring):
    with ExitStack() as ctx:
        def sb(name, shape, dt=F32):
            return ctx.enter_context(nc.sbuf_tensor(f"load{half}_{name}", shape, dt))

        def s(name):
            return sem(f"load{half}_{name}")

        wvu = sb("wvu", [BOT, D])
        x2z = sb("x2z", [P, D + BOT])
        zT = sb("zT", [BOT, P])
        g = sb("g", [P, 1])
        y = sb("y", [P, D])
        ld_w, ld_row, row_free, zt_ok, zT_ok, aux_ok = s("ld_w"), s("ld_row"), s("row_free"), s("zt"), s("zT"), s("aux")
        var_ok, rstd_ok, x3_ok, turn_ok, hi_ok, lo_ok = s("var"), s("rstd"), s("x3"), s("turn"), s("hi"), s("lo")
        block = ctx.enter_context(nc.Block())

        @block.sync
        def _(sp):
            sp.dma_start(wvu[:], io["wvuT"]).then_inc(ld_w, 16)
            rows = io["rows"].rearrange("b (h c l) n -> h c l b n", h=2, l=8)[half]
            with sp.Fori(0, NC) as c:
                w = Counts(sp)
                sp.wait_ge(row_free, w.next(row_free))
                for l in range(8):
                    sp.dma_start(x2z[16 * l:16 * l + 16, :], rows[c, l, :, 0:D + BOT]).then_inc(ld_row, 16)
                w.take_off()

        @block.gpsimd
        def _(pool):
            with pool.Fori(0, NC) as c:
                w = Counts(pool)
                pool.wait_ge(var_ok, w.next(var_ok))
                nc.gpsimd.tensor_scalar(veps[:], mv[:, 1:2], EPS, None, ALU.add)
                pool.drain()
                nc.gpsimd.tensor_tensor(rstd[:], veps[:], half_exp[:], ALU.pow).then_inc(rstd_ok, 1)
                w.take_off()

        @block.tensor
        def _(pe):
            pe.wait_ge(ld_w, 16)
            with pe.Fori(0, NC) as c:
                w = Counts(pe)
                pe.wait_ge(ld_row, w.next(ld_row, 16 * 8))
                pe.transpose(ring[0:BOT, 0, 0:P], x2z[:, D:D + BOT], ident[:]).then_inc(zt_ok, 1)
                pe.wait_ge(zT_ok, w.next(zT_ok))
                for h in range(2):
                    pe.matmul(ring[:, 1 + h, :], zT[:], wvu[:, 512 * h:512 * h + 512],
                              start=True, stop=True).then_inc(aux_ok, 1)
                pe.wait_ge(x3_ok, w.next(x3_ok))
                pe.wait_ge(lo_ok, w.next(lo_ok, 2))
                for h in range(2):
                    for j in range(4):
                        k = 4 * h + j
                        mm = pe.transpose(feat[:, 0, h, P * j:P * j + P], y[:, P * k:P * k + P], ident[:])
                    mm.then_inc(turn_ok, 1)
                w.take_off()

        @block.scalar
        def _(act):
            with act.Fori(0, NC) as c:
                w = Counts(act)
                act.wait_ge(zt_ok, w.next(zt_ok))
                nc.scalar.copy(zT[:], ring[0:BOT, 0, 0:P]).then_inc(zT_ok, 1)
                for h in range(2):
                    act.wait_ge(turn_ok, w.next(turn_ok))
                    nc.scalar.copy(x_hi[:, 4 * h:4 * h + 4, bass.ds(c * P, P)],
                                   feat[:, 0, h, :].rearrange("p (k t) -> p k t", k=4)).then_inc(hi_ok, 1)
                w.take_off()

        @block.vector
        def _(dve):
            v = nc.vector
            dve.sem_inc(row_free, 1)
            dve.sem_inc(lo_ok, 2)
            with dve.Fori(0, NC) as c:
                w = Counts(dve)
                v.tensor_copy(g[:], gate[:, bass.ds(c + half * NC, 1)])
                dve.drain()
                for h in range(2):
                    cols = slice(512 * h, 512 * h + 512)
                    dve.wait_ge(aux_ok, w.next(aux_ok))
                    v.scalar_tensor_tensor(out=y[:, cols], in0=ring[:, 1 + h, :], scalar=g[:, 0:1],
                                           in1=x2z[:, cols], op0=ALU.mult, op1=ALU.add)
                dve.drain()
                v.tensor_tensor(y[:], y[:], x2z[:, 0:D], ALU.add)
                dve.drain().then_inc(row_free, 1)
                for h in range(2):
                    v.bn_stats(st[:, 6 * h:6 * h + 6], y[:, 512 * h:512 * h + 512])
                dve.drain()
                v.bn_aggr(mv[:], st[:]).then_inc(var_ok, 1)
                dve.wait_ge(rstd_ok, w.next(rstd_ok))
                v.tensor_scalar(y[:], y[:], mv[:, 0:1], rstd[:, 0:1], ALU.subtract, ALU.mult).then_inc(x3_ok, 1)
                dve.drain()
                v.tensor_copy(acc[:, bass.ds(c, 1), :], y[:].unsqueeze(1))
                for h in range(2):
                    dve.wait_ge(hi_ok, w.next(hi_ok))
                    v.tensor_tensor(x_lo[:, 4 * h:4 * h + 4, bass.ds(c * P, P)],
                                    feat[:, 0, h, :].rearrange("p (k t) -> p k t", k=4),
                                    x_hi[:, 4 * h:4 * h + 4, bass.ds(c * P, P)].bitcast(F32), ALU.subtract).then_inc(lo_ok, 1)
                w.take_off()


def heads_half(nc, io, sem, half, NC, TH, NKV, QPG, DH, UNITS, CHUNKS,
               ident, causal, x_hi, x_lo, acc, feat, score, ring):
    with ExitStack() as ctx:
        def sb(name, shape, dt=F32):
            return ctx.enter_context(nc.sbuf_tensor(f"heads{half}_{name}", shape, dt))

        def s(name):
            return sem(f"heads{half}_{name}")

        raw = sb("raw", [P, 2, D])
        w_hi, w_lo = sb("w_hi", [P, 2, KT, DH], F32R), sb("w_lo", [P, 2, KT, DH], F32R)
        p_hi, p_lo = sb("p_hi", [P, QPG, D], F32R), sb("p_lo", [P, QPG, D], F32R)
        qT, kT, vT = sb("qT", [P, QPG, TH]), sb("kT", [P, TH]), sb("vT", [P, TH])
        val = sb("val", [P, NC, DH])
        sm, ex = sb("sm", [P, NC, 32]), sb("ex", [P, NC, 32])
        most, total = sb("most", [P, NC]), sb("total", [P, NC])
        probsT = sb("probsT", [P, QPG, NC, P])
        o_hi, o_lo = sb("o_hi", [P, QPG, TH], F32R), sb("o_lo", [P, QPG, TH], F32R)

        ld_raw, raw_free = [s("ld_raw0"), s("ld_raw1")], s("raw_free")
        unit_ok, w_free, p_free = s("unit_ok"), s("w_free"), s("p_free")
        feat_ok, feat_sb = s("feat_ok"), s("feat_sb")
        score_ok, score_free, arg_ok, exp_ok, probs_ok = s("score_ok"), s("score_free"), s("arg_ok"), s("exp_ok"), s("probs_ok")
        vt_ok, val_ok, pv_ok, o_hi_ok, o_lo_ok = s("vt_ok"), s("val_ok"), s("pv_ok"), s("o_hi_ok"), s("o_lo_ok")
        proj_ok, acc_ok = s("proj_ok"), s("acc_ok")
        block = ctx.enter_context(nc.Block())
        ORDER = [QPG] + list(range(QPG)) + [QPG + 1]

        @block.sync
        def _(sp):
            with sp.Fori(0, NKV) as g:
                w = Counts(sp)
                for u in range(UNITS + QPG):
                    sp.wait_ge(raw_free, w.next(raw_free))
                    src = io["wqkvU"][g, ORDER[u]] if u < UNITS else io["wprojU"][g, u - UNITS]
                    sp.dma_start(raw[:, u % 2, :], src).then_inc(ld_raw[u % 2], 16)
                w.take_off()

        @block.gpsimd
        def _(pool):
            with pool.Fori(0, NKV) as g:
                w = Counts(pool)
                for u in range(UNITS + QPG):
                    pool.wait_ge(ld_raw[u % 2], w.next(ld_raw[u % 2], 16))
                    if u < UNITS:
                        pool.wait_ge(w_free, w.next(w_free))
                        hi, lo = w_hi[:, u % 2, :, :], w_lo[:, u % 2, :, :]
                        src = raw[:, u % 2, :].rearrange("p (k n) -> p k n", k=KT)
                    else:
                        if u == UNITS:
                            pool.wait_ge(p_free, w.next(p_free))
                        hi, lo, src = p_hi[:, u - UNITS, :], p_lo[:, u - UNITS, :], raw[:, u % 2, :]
                    nc.gpsimd.tensor_copy(hi, src)
                    pool.drain()
                    nc.gpsimd.tensor_tensor(lo, src, hi.bitcast(F32), ALU.subtract).then_inc(unit_ok, 1)
                    pool.drain().then_inc(raw_free, 1)
                w.take_off()

        @block.tensor
        def _(pe):
            def scores(w, j):
                pe.wait_ge(score_free, w.next(score_free))
                for c in range(NC):
                    for p in range(4):
                        t = slice(P * c + 32 * p, P * c + 32 * p + 32)
                        mm = pe.matmul(score[32 * p:32 * p + 32, 32 * c:32 * c + 32], qT[:, j, t], kT[:, t],
                                       start=True, stop=True)
                mm.then_inc(score_ok, 1)

            with pe.Fori(0, NKV) as g:
                w = Counts(pe)
                for u in range(UNITS):
                    pe.wait_ge(unit_ok, w.next(unit_ok))
                    for i, t in enumerate(CHUNKS):
                        n = 0
                        for k in range(KT):
                            for a, b in split_passes(w_hi, w_lo, x_hi, x_lo):
                                mm = pe.matmul(feat[:, u % 2, i, 0:t.stop - t.start], a[:, u % 2, k, :], b[:, k, t],
                                               start=(n == 0), stop=(n == 3 * KT - 1))
                                n += 1
                        mm.then_inc(feat_ok, 1)
                    if u >= 2:
                        pe.wait_ge(feat_sb, w.next(feat_sb, 2 if u == 2 else 1))
                        scores(w, u - 2)
                pe.wait_ge(feat_sb, w.next(feat_sb))
                for i in range(2):
                    pe.wait_ge(acc_ok, w.next(acc_ok))
                    for c in range(4 * i, min(4 * i + 4, NC)):
                        mm = pe.transpose(ring[:, i, P * (c % 4):P * (c % 4) + P], vT[:, P * c:P * c + P], ident[:])
                    mm.then_inc(vt_ok, 1)
                pe.wait_ge(probs_ok, w.next(probs_ok, QPG))
                pe.wait_ge(val_ok, w.next(val_ok, 2))
                for c in range(NC):
                    if c == 0:
                        pe.wait_ge(acc_ok, w.next(acc_ok))
                    if c >= 3:
                        pe.wait_ge(o_lo_ok, w.next(o_lo_ok))
                    pe.matmul(ring[:, (2 + c) % 3, :], val[:, c, :], probsT[:, :, c, :],
                              start=True, stop=True).then_inc(pv_ok, 1)
                pe.wait_ge(unit_ok, w.next(unit_ok, QPG))
                for c in range(NC):
                    for h in range(2):
                        n = 2 * c + h
                        pe.wait_ge(o_lo_ok if n < 3 else acc_ok, w.next(o_lo_ok if n < 3 else acc_ok))
                        i = 0
                        for j in range(QPG):
                            for a, b in split_passes(o_hi, o_lo, p_hi, p_lo):
                                mm = pe.matmul(ring[:, (2 + NC + n) % 3, :], a[:, j, P * c:P * c + P],
                                               b[:, j, 512 * h:512 * h + 512], start=(i == 0), stop=(i == 3 * QPG - 1))
                                i += 1
                        mm.then_inc(proj_ok, 1)
                w.take_off()

        @block.scalar
        def _(act):
            def take_exp(w):
                act.wait_ge(arg_ok, w.next(arg_ok))
                nc.scalar.activation(ex[:], sm[:], ACT.Exp).then_inc(exp_ok, 1)

            with act.Fori(0, NKV) as g:
                w = Counts(act)
                for u in range(UNITS):
                    dst = kT[:, :] if u == 0 else (vT[:, :] if u == UNITS - 1 else qT[:, u - 1, :])
                    for i, t in enumerate(CHUNKS):
                        act.wait_ge(feat_ok, w.next(feat_ok))
                        last = nc.scalar.copy(dst[:, t], feat[:, u % 2, i, 0:t.stop - t.start])
                    last.then_inc(w_free, 1)
                    act.drain().then_inc(feat_sb, 1)
                    if u >= 3:
                        take_exp(w)
                take_exp(w)
                for i in range(2):
                    act.wait_ge(vt_ok, w.next(vt_ok))
                    n = min(4, NC - 4 * i)
                    nc.scalar.copy(val[:, 4 * i:4 * i + n, :],
                                   ring[:, i, 0:P * n].rearrange("p (c d) -> p c d", c=n)).then_inc(val_ok, 1)
                for c in range(NC):
                    act.wait_ge(pv_ok, w.next(pv_ok))
                    nc.scalar.copy(o_hi[:, :, P * c:P * c + P],
                                   ring[:, (2 + c) % 3, :].rearrange("p (j t) -> p j t", j=QPG)).then_inc(o_hi_ok, 1)
                w.take_off()

        @block.vector
        def _(dve):
            v = nc.vector
            v.memset(probsT[:].bitcast(F32), 0.0)
            dve.drain()
            dve.sem_inc(raw_free, 2)
            dve.sem_inc(w_free, 2)
            dve.sem_inc(p_free, 1)
            dve.sem_inc(score_free, 1)
            dve.sem_inc(acc_ok, 3)
            with dve.Fori(0, NKV) as g:
                w = Counts(dve)
                for j in range(QPG):
                    dve.wait_ge(score_ok, w.next(score_ok))
                    v.scalar_tensor_tensor(out=sm[:], in0=score[:, 0:32 * NC].rearrange("p (c t) -> p c t", c=NC),
                                           scalar=float(DH) ** -0.5, in1=causal[:].unsqueeze(1).broadcast_to([P, NC, 32]),
                                           op0=ALU.mult, op1=ALU.add)
                    dve.drain().then_inc(score_free, 1)
                    v.tensor_reduce(most[:], sm[:], AX.X, ALU.max)
                    dve.drain()
                    v.tensor_tensor(sm[:], sm[:], most[:].unsqueeze(2).broadcast_to([P, NC, 32]),
                                    ALU.subtract).then_inc(arg_ok, 1)
                    dve.wait_ge(exp_ok, w.next(exp_ok))
                    v.tensor_reduce(total[:], ex[:], AX.X, ALU.add)
                    dve.drain()
                    v.reciprocal(total[:], total[:])
                    dve.drain()
                    v.tensor_tensor(ex[:], ex[:], total[:].unsqueeze(2).broadcast_to([P, NC, 32]), ALU.mult)
                    dve.drain()
                    for p in range(4):
                        q = slice(32 * p, 32 * p + 32)
                        v.transpose(probsT[q, j, :, q], ex[q, :, :])
                    dve.drain().then_inc(probs_ok, 1)
                for c in range(NC):
                    dve.wait_ge(o_hi_ok, w.next(o_hi_ok))
                    v.tensor_tensor(o_lo[:, :, P * c:P * c + P],
                                    ring[:, (2 + c) % 3, :].rearrange("p (j t) -> p j t", j=QPG),
                                    o_hi[:, :, P * c:P * c + P].bitcast(F32), ALU.subtract).then_inc(o_lo_ok, 1)
                for c in range(NC):
                    for h in range(2):
                        n = 2 * c + h
                        cols = slice(512 * h, 512 * h + 512)
                        dve.wait_ge(proj_ok, w.next(proj_ok))
                        v.tensor_tensor(acc[:, c, cols], acc[:, c, cols], ring[:, (2 + NC + n) % 3, :],
                                        ALU.add).then_inc(acc_ok, 1)
                dve.drain().then_inc(p_free, 1)
                w.take_off()


def store_half(nc, io, sem, half, NC, half_exp, acc, st, mv, veps, rstd):
    with ExitStack() as ctx:
        y = ctx.enter_context(nc.sbuf_tensor(f"store{half}_y", [P, D], F32))
        var_ok, rstd_ok, y_ok, stored = (sem(f"store{half}_{n}") for n in ("var", "rstd", "y", "stored"))
        block = ctx.enter_context(nc.Block())

        @block.sync
        def _(sp):
            dst = io["x4"].rearrange("b (h c l) n -> h c l b n", h=2, l=8)[half]
            with sp.Fori(0, NC) as c:
                w = Counts(sp)
                sp.wait_ge(y_ok, w.next(y_ok))
                for l in range(8):
                    sp.dma_start(dst[c, l, :, :], y[16 * l:16 * l + 16, :]).then_inc(stored, 16)
                w.take_off()

        @block.gpsimd
        def _(pool):
            with pool.Fori(0, NC) as c:
                w = Counts(pool)
                pool.wait_ge(var_ok, w.next(var_ok))
                nc.gpsimd.tensor_scalar(veps[:], mv[:, 1:2], EPS, None, ALU.add)
                pool.drain()
                nc.gpsimd.tensor_tensor(rstd[:], veps[:], half_exp[:], ALU.pow).then_inc(rstd_ok, 1)
                w.take_off()

        @block.vector
        def _(dve):
            v = nc.vector
            dve.sem_inc(stored, 16 * 8)
            with dve.Fori(0, NC) as c:
                w = Counts(dve)
                for h in range(2):
                    v.bn_stats(st[:, 6 * h:6 * h + 6], acc[:, bass.ds(c, 1), 512 * h:512 * h + 512])
                dve.drain()
                v.bn_aggr(mv[:], st[:]).then_inc(var_ok, 1)
                dve.wait_ge(rstd_ok, w.next(rstd_ok))
                dve.wait_ge(stored, w.next(stored, 16 * 8))
                v.tensor_scalar(y[:].unsqueeze(1), acc[:, bass.ds(c, 1), :], mv[:, 0:1], rstd[:, 0:1],
                                ALU.subtract, ALU.mult).then_inc(y_ok, 1)
                w.take_off()
            dve.wait_ge(stored, 16 * 8)
            dve.sem_inc(stored, -16 * 8)


def build(nc, io, out):
    ks = nc.dram_tensor("ctx_parts", [2, B, C, T], F32).ap()
    qs = nc.dram_tensor("query_parts", [2, B, KT, P, S], F32).ap()
    rows = nc.dram_tensor("rows", [B, S, ROW], F32).ap()
    x4 = nc.dram_tensor("x4", [B, S, D], F32).ap()
    io = dict(io, ks=ks, qs=qs, rows=rows, x4=x4, out=out)

    def stage(fn, *args):
        with ExitStack() as ctx:
            used = []

            def sem(name):
                used.append(ctx.enter_context(nc.semaphore(name)))
                return used[-1]

            fn(*args, sem)
            with nc.Block() as block:
                @block.gpsimd
                def _(pool):
                    for one in used:
                        pool.sem_clear(one)

    stage(token_stage, nc, 0, io)
    stage(self_attention, nc, io)
    stage(token_stage, nc, 1, io)


def layouts(a):
    def rows(v, n=P):
        return np.broadcast_to(np.reshape(v, (1, -1)), (n, np.size(v)))

    lr = np.reshape(a["L0_ffn_log_rel"], (1, -1))
    r = np.arange(P) % 32
    allowed = (r[:, None] // 16 == np.arange(32)[None] // 16) & (np.arange(32)[None] % 16 <= r[:, None] % 16)
    return {
        "x": a["x"], "xT": np.transpose(np.reshape(a["x"], (B, S, KT, P)), (0, 3, 2, 1)),
        "ctx": a["ctx_1024"], "ctxT": np.transpose(np.reshape(a["ctx_1024"], (B, T, 2, P)), (0, 3, 2, 1)),
        "mask": a["mask_SxS2_ff0"],
        "bmaskT": np.transpose(a["L0_attn_mask"]), "w0T": np.transpose(a["L0_attn_weight"]),
        "b0": rows(a["L0_attn_bias"]),
        "wu1T": np.transpose(a["L0_ffn_Wu1"]), "bu1": rows(a["L0_ffn_bu1"]),
        "wu2": rows(a["L0_ffn_Wu2"]), "bu2": rows(a["L0_ffn_bu2"]),
        "wqT": np.transpose(a["L0_ffn_Wq"]), "wr": a["L0_ffn_Wr"], "wrT": np.transpose(a["L0_ffn_Wr"]),
        "keysT": np.transpose(a["L0_ffn_aux_keys"]), "valuesT": np.transpose(a["L0_ffn_aux_values"]),
        "log_rel": np.concatenate([lr, lr], axis=1),
        "wvdT": np.transpose(a["L0_ffn_Wvd"]), "wvuT": np.transpose(a["L0_ffn_Wvu"]),
        "gate_w1": rows(a["L0_ffn_gate_w1"]), "gate_bias": rows(a["L0_ffn_gate_bias"]),
        "wqkvU": np.reshape(np.transpose(np.reshape(a["L1_attn_weight_qkv"], (8, 6, P, KT, P)), (0, 1, 4, 3, 2)),
                            (8, 6, P, D)),
        "wprojU": np.reshape(np.transpose(a["L1_attn_weight_proj"]), (8, 4, P, D)),
        "awT": np.transpose(a["L1_ffn_A_w"]), "bwT": np.transpose(a["L1_ffn_B_w"]),
        "rq": a["L1_ffn_Wq_w"], "rkeysT": np.transpose(a["L1_ffn_keys"]),
        "ident": np.eye(P, dtype=np.float32),
        "ones": np.ones((P, P), np.float32),
        "blocks": np.kron(np.eye(4, dtype=np.float32), np.ones((32, 32), np.float32)),
        "causal": np.where(allowed, 0.0, -HUGE).astype(np.float32),
    }


def kernel(**inputs):
    import concourse.bacc as _bacc
    from concourse.bass_utils import run_bass_kernel_spmd as _run

    nc = _bacc.Bacc("TRN2", target_bir_lowering=False, num_devices=1, dynamic_dma_scratch_size=1024)
    arrays, args = {}, {}
    for name, a in layouts({k: np.asarray(v) for k, v in inputs.items()}).items():
        a = np.ascontiguousarray(a)
        arrays[f"in_{name}_dram"] = a
        args[name] = nc.dram_tensor(f"in_{name}_dram", a.shape, mybir.dt.from_np(a.dtype), kind="ExternalInput").ap()
    out = nc.dram_tensor("out_0_dram", (B, S, D), F32, kind="ExternalOutput").ap()
    build(nc, args, out)
    r = _run(nc, [arrays], core_ids=[0])
    return r.results[0]["out_0_dram"]
```

```python
from contextlib import ExitStack

import numpy as np
import concourse.bass as bass
from concourse import mybir

F32 = mybir.dt.float32
F32R = mybir.dt.float32r
I32 = mybir.dt.int32
ALU = mybir.AluOpType
ACT = mybir.ActivationFunctionType
AX = mybir.AxisListType

P = 128
B, S, D = 16, 112, 1024
T, C = 375, 256
KT = D // P
HD = 32
NG, NR = 8, 4
NH = NG * NR
TC, TJ = 125, 3
TP = T + 1
EPS = 1e-5
BOT, SLOTS, UH = 64, 256, 256
ROW = 1096
COL_Z, COL_LEARNED, COL_VAR = D, D + BOT, D + BOT + 1
NE, RANK = 64, 8
BN = NE * RANK
HUGE = 3.0e38


class Counts:

    def __init__(self, eng):
        self.eng, self.counts = eng, {}

    def next(self, sem, n=1):
        total = self.counts.get(sem.name, (sem, 0))[1] + n
        self.counts[sem.name] = (sem, total)
        return total

    def take_off(self):
        for sem, total in self.counts.values():
            self.eng.sem_inc(sem, -total)
        self.counts = {}


def split_passes(hi_a, lo_a, hi_b, lo_b):
    return ((hi_a, hi_b), (hi_a, lo_b), (lo_a, hi_b))


def token_stage(nc, layer, io, sem):
    first = layer == 0
    with ExitStack() as ctx:
        def sb(name, shape, dt=F32):
            return ctx.enter_context(nc.sbuf_tensor(f"L{layer}_{name}", shape, dt))

        def s(name):
            return sem(f"L{layer}_{name}")

        wide = ctx.enter_context(nc.psum_tensor(f"L{layer}_wide", [P, 2, 512], F32))
        scores = ctx.enter_context(nc.psum_tensor(f"L{layer}_scores", [P, 3, 512], F32))
        turned = ctx.enter_context(nc.psum_tensor(f"L{layer}_turned", [P, 2, 512], F32))

        spare = ctx.enter_context(nc.psum_tensor(f"L{layer}_spare", [P, 512], F32))

        ident = sb("ident", [P, P])
        nmask = sb("nmask", [P, T])
        xcur = sb("xcur", [P, D])
        xnew = sb("xnew", [P, D])
        row = sb("row", [P, ROW])
        attn = sb("attn", [P, D])
        tT_hi = sb("tT_hi", [P, KT, S], F32R)
        tT_lo = sb("tT_lo", [P, KT, S], F32R)
        qT_hi = sb("qT_hi", [P, KT, S], F32R)
        qT_lo = sb("qT_lo", [P, KT, S], F32R)
        qrep = sb("qrep", [P, 2, NR, 4, S], F32R)
        krep = sb("krep", [P, NG, TP], F32R)
        val = sb("val", [TC, TJ, C])
        masked = sb("masked", [P, 3, T])
        probs = sb("probs", [P, 4, T])
        probsT = sb("probsT", [TC, 8, TJ, S])
        oT = sb("oT", [P, 8, S])
        least = sb("least", [P, NH])
        rsum = sb("rsum", [P, NH])
        rinv = sb("rinv", [P, NH])
        st = sb("st", [P, 36])
        mv = sb("mv", [P, 6])
        veps = sb("veps", [P, 3])
        rstd = sb("rstd", [P, 3])
        half = sb("half", [P, 1])

        ld_x, ld_xt, ld_c, x_free, xt_free = s("ld_x"), s("ld_xt"), s("ld_c"), s("x_free"), s("xt_free")
        ld_kq, ld_v, k_free, v_free, q_stored = ([s(f"{n}{h}") for h in range(2)]
                                                 for n in ("ld_kq", "ld_v", "k_free", "v_free", "q_stored"))
        x_hi_ok, split_x, xb_ok, lin_ok, lin_read = s("x_hi_ok"), s("split_x"), s("xb_ok"), s("lin_ok"), s("lin_read")
        c_hi_ok, c_lo_ok, c_stored, x_ok, x_moved = s("c_hi_ok"), s("c_lo_ok"), s("c_stored"), s("x_ok"), s("x_moved")
        turn_ok, q_hi_ok, q_lo_ok, q_read = s("turn"), s("q_hi"), s("q_lo"), s("q_read")
        turn2_ok, hi2_ok, lo2_ok = s("turn2"), s("hi2"), s("lo2")
        score_ok, least_ok, prob_ok = s("score"), s("least"), s("prob")
        turned_v, turned_s, copied_v, copied_s = s("turned_v"), s("turned_s"), s("copied_v"), s("copied_s")
        pv_s, pv_v, oT_s, oT_v = s("pv_s"), s("pv_v"), s("oT_s"), s("oT_v")
        attn_ok, attn_read, attn_out, sum_ok, sum_done = s("attn_ok"), s("attn_read"), s("attn_out"), s("sum_ok"), s("sum_done")
        var_ok, rstd_ok = ([s(f"{n}{i}") for i in range(3)] for n in ("var", "rstd"))
        x2_ok, stored = s("x2"), s("stored")

        if first:
            gate_h_ok, gate_h_read, gelu_arg_ok, least_pen_ok = s("gate_h_ok"), s("gate_h_read"), s("gelu_arg_ok"), s("least_pen_ok")
            qaug_ok, z_read = s("qaug_ok"), s("z_read")
            ra_ok, route_ok, row_ok, slotT_ok, slot_exp_ok = (s("ra_ok"), s("route_ok"), s("row_ok"), s("slotT_ok"), s("slot_exp_ok"))
            slot_w_ok, tanh_ok, wT_ok, z_ok = (s("slot_w_ok"), s("tanh_ok"), s("wT_ok"), s("z_ok"))
            craw = sb("craw", [P, 2, T])
            c_hi, c_lo = sb("c_hi", [P, 2, TP], F32R), sb("c_lo", [P, 2, TP], F32R)
            w0_hi, w0_lo = sb("w0_hi", [P, KT, D], F32R), sb("w0_lo", [P, KT, D], F32R)
            xt = sb("xt", [P, KT, S])
            x_hi, x_lo = sb("x_hi", [P, KT, S], F32R), sb("x_lo", [P, KT, S], F32R)
            xb = sb("xb", [P, D])
            bias = sb("bias", [P, D])
            wu_hi, wu_lo = sb("wu_hi", [P, KT, UH], F32R), sb("wu_lo", [P, KT, UH], F32R)
            wq_hi, wq_lo = sb("wq_hi", [P, KT, BOT], F32R), sb("wq_lo", [P, KT, BOT], F32R)
            route = sb("route", [BOT + 1, 2 * SLOTS])
            u_val = sb("u_val", [P, 2, BOT])
            bu1, wu2, bu2 = sb("bu1", [P, UH]), sb("wu2", [P, UH]), sb("bu2", [P, 1])
            qaug = sb("qaug", [BOT + 1, S])
            ra = sb("ra", [P, 2 * SLOTS])
            top8 = sb("top8", [P, 8])
            left = sb("left", [P, SLOTS])
            pen = sb("pen", [P, SLOTS])
            slot_w = sb("slot_w", [P, SLOTS])
            sm = sb("sm", [P, 4])
            wT = sb("wT", [P, 2, S])
            ua, ub, uc = sb("ua", [P, UH]), sb("ub", [P, UH]), sb("uc", [P, UH])
        else:
            bottleneck_ok, egate_ok, gatedT_ok, gated_ok, out_ok = (s("bottleneck_ok"), s("egate_ok"), s("gatedT_ok"), s("gated_ok"), s("out_ok"))
            out_read, sc_read = s("out_read"), s("sc_read")
            res_ok, rscore_ok, top_ok, z_hi_ok, z_lo_ok = (s("res_ok"), s("rscore_ok"), s("top_ok"), s("z_hi_ok"), s("z_lo_ok"))
            a_hi, a_lo = sb("a_hi", [P, KT, BN], F32R), sb("a_lo", [P, KT, BN], F32R)
            r_hi, r_lo = sb("r_hi", [P, KT, NE], F32R), sb("r_lo", [P, KT, NE], F32R)
            b_hi, b_lo = sb("b_hi", [P, 4, D], F32R), sb("b_lo", [P, 4, D], F32R)
            sc = sb("sc", [P, NE])
            sc1, sc2 = sb("sc1", [P, NE]), sb("sc2", [P, NE])
            top8, top16 = sb("top8", [P, 8]), sb("top16", [P, 8])
            egate = sb("egate", [P, NE])
            sel = sb("sel", [P, NE])
            sm = sb("sm", [P, 4])
            zg = sb("zg", [P, BN])
            z_hi, z_lo = sb("z_hi", [P, 4, S], F32R), sb("z_lo", [P, 4, S], F32R)
            res = sb("res", [P, D])

        once = ExitStack()

        def tmp(name, shape, dt=F32):
            return once.enter_context(nc.sbuf_tensor(f"L{layer}_once_{name}", shape, dt))

        stage = [attn[:], row[:], xnew[:], xcur[:]] + [buf[:].rearrange("p a t -> p (a t)") for buf in (probs, masked)]
        NST = len(stage)
        part_of = []
        if first:
            brow = tmp("brow", [P, KT * 32])
            bm = tmp("bm", [P, KT, 32])
            blocks = tmp("blocks", [P, P])
            wr, wrT, keysT = tmp("wr", [48, BOT]), tmp("wrT", [BOT, 48]), tmp("keysT", [BOT, SLOTS])
            wvdT = tmp("wvdT", [P, KT, BOT])
            xt_cols = xt[:].rearrange("p k s -> p (k s)")
            valT = ([xb[:, SLOTS * k:SLOTS * k + SLOTS] for k in range(4)]
                    + [xt_cols[:, SLOTS * k:SLOTS * k + SLOTS] for k in range(3)] + [ua[:, :]])
            rkT = tmp("rkT", [48, SLOTS])
            for k in range(KT):
                part_of.append((io["bmaskT"][P * k:P * k + P], D, "sum", brow[:, 32 * k:32 * k + 32], None))
            for k in range(KT):
                rows_k = slice(P * k, P * k + P)
                part_of.append((io["wu1T"][rows_k], UH, None, wu_hi[:, k, :], wu_lo[:, k, :]))
                part_of.append((io["wqT"][rows_k], BOT, None, wq_hi[:, k, :], wq_lo[:, k, :]))
            for k in range(KT):
                part_of.append((io["w0T"][P * k:P * k + P], D, k, w0_hi[:, k, :], w0_lo[:, k, :]))
            small = [(blocks[:], io["blocks"]),
                     (wr[:], io["wr"]), (wrT[:], io["wrT"]), (keysT[:], io["keysT"]),
                     (wvdT[:], io["wvdT"].rearrange("(k p) n -> p k n", p=P)),
                     (route[BOT:BOT + 1, :], io["log_rel"]), (bias[:], io["b0"]), (bu1[:], io["bu1"]),
                     (wu2[:], io["wu2"]), (bu2[:], io["bu2"])]
            small += [(valT[k], io["valuesT"][P * k:P * k + P]) for k in range(KT)]
        else:
            rq, rkeysT = tmp("rq", [16, D]), tmp("rkeysT", [16, NE])
            for k in range(KT):
                part_of.append((io["awT"][P * k:P * k + P], BN, None, a_hi[:, k, :], a_lo[:, k, :]))
            for k in range(4):
                part_of.append((io["bwT"][P * k:P * k + P], D, None, b_hi[:, k, :], b_lo[:, k, :]))
            small = [(rq[:], io["rq"]), (rkeysT[:], io["rkeysT"])]
        small += [(ident[:], io["ident"]), (nmask[0:S, :], io["mask"])]
        small_in, chunk_done, prep_pe, prep_dve = s("small_in"), s("chunk_done"), s("prep_pe"), s("prep_dve")
        chunk_in = [s(f"chunk_in{i}") for i in range(NST)]
        chunk_masked, chunk_hi = s("chunk_masked"), s("chunk_hi")
        prep = once.enter_context(nc.Block())

        def chunk(i):
            what = part_of[i][2]
            raw = stage[i % NST][:, 0:part_of[i][1]]
            return raw.bitcast(I32) if what == "sum" else raw

        @prep.sync
        def _(sp):
            for i, (src, cols, _, _, _) in enumerate(part_of):
                if i >= NST:
                    sp.wait_ge(chunk_done, i - NST + 1)
                sp.dma_start(chunk(i), src).then_inc(chunk_in[i % NST], 16)

        @prep.scalar
        def _(act):
            for dst, src in small:
                act.dma_start(dst, src).then_inc(small_in, 16)
            for i, (_, _, what, hi, _) in enumerate(part_of):
                if what is None:
                    act.wait_ge(chunk_in[i % NST], 16 * (i // NST + 1))
                elif what != "sum":
                    act.wait_ge(chunk_masked, what + 1)
                if what != "sum":
                    nc.scalar.copy(hi, chunk(i)).then_inc(chunk_hi, 1)

        @prep.tensor
        def _(pe):
            pe.wait_ge(small_in, 16 * len(small))
            if first:
                pe.wait_ge(chunk_done, KT)
                pe.matmul(wide[:, 0, 0:KT * 32], blocks[:], brow[:], start=True, stop=True)
                pe.matmul(wide[0:48, 1, 0:SLOTS], wrT[:], keysT[:], start=True, stop=True)
                for j in range(2):
                    for k in range(KT):
                        mm = pe.matmul(scores[:, j, 0:BOT], valT[k][:, P * j:P * j + P], wvdT[:, k, :],
                                       start=(k == 0), stop=(k == KT - 1))
                mm.then_inc(prep_pe, 1)
                pe.wait_ge(prep_dve, 1)
                pe.matmul(scores[0:BOT, 2, 0:SLOTS], wr[:], rkT[:], start=True, stop=True).then_inc(prep_pe, 1)
            else:
                for k in range(KT):
                    mm = pe.matmul(wide[:, 0, NE * k:NE * k + NE], rq[:, P * k:P * k + P], rkeysT[:],
                                   start=True, stop=True)
                mm.then_inc(prep_pe, 1)

        @prep.vector
        def _(dve):
            v = nc.vector
            v.memset(half[:], -0.5)
            v.memset(row[:, COL_VAR + 1:ROW], 0.0)
            if first:
                for part in (c_hi, c_lo):
                    v.memset(part[:, :, T:TP].bitcast(F32), 0.0)

            def constants():
                dve.wait_ge(small_in, 16 * len(small))
                v.tensor_scalar(nmask[0:S, :], nmask[0:S, :], -1.0, None, ALU.mult)
                if first:
                    v.memset(qaug[BOT:BOT + 1, :], 1.0)
                    v.tensor_scalar(route[0:BOT, SLOTS:2 * SLOTS], keysT[:], BOT ** -0.5, None, ALU.mult)
                    dve.wait_ge(prep_pe, 1)
                    v.tensor_copy(rkT[:], wide[0:48, 1, 0:SLOTS]).then_inc(prep_dve, 1)
                    v.tensor_scalar(bm[:], wide[:, 0, 0:KT * 32].rearrange("p (k n) -> p k n", k=KT), 0.0, None, ALU.is_gt)
                    for j in range(2):
                        v.tensor_copy(u_val[:, j, :], scores[:, j, 0:BOT])
                    dve.wait_ge(prep_pe, 2)
                    v.tensor_scalar(route[0:BOT, 0:SLOTS], scores[0:BOT, 2, 0:SLOTS], 48 ** -0.5, None, ALU.mult)
                else:
                    dve.wait_ge(prep_pe, 1)
                    psum = wide[:, 0, :].rearrange("p (k e) -> p k e", k=KT)
                    v.tensor_copy(r_hi[:], psum)
                    dve.drain()
                    v.tensor_tensor(r_lo[:], psum, r_hi[:].bitcast(F32), ALU.subtract)
                dve.drain()

            split = 0
            for i in range(len(part_of) + 1):
                what = part_of[i][2] if i < len(part_of) else None
                if i == (3 * KT if first else len(part_of)):
                    constants()
                if what is not None:
                    dve.wait_ge(chunk_in[i % NST], 16 * (i // NST + 1))
                if what == "sum":
                    v.tensor_reduce(part_of[i][3], chunk(i).rearrange("p (n j) -> p n j", j=32), AX.X, ALU.add).then_inc(chunk_done, 1)
                elif what is not None:
                    raw = chunk(i).rearrange("p (n j) -> p n j", j=32)
                    v.tensor_tensor(raw, raw, bm[:, what, :].unsqueeze(2).broadcast_to([P, 32, 32]), ALU.mult).then_inc(chunk_masked, 1)
                if i >= 1 and part_of[i - 1][2] != "sum":
                    split += 1
                    dve.wait_ge(chunk_hi, split)
                    v.tensor_tensor(part_of[i - 1][4], chunk(i - 1), part_of[i - 1][3].bitcast(F32), ALU.subtract).then_inc(chunk_done, 1)

        once.close()

        STEPS = 40

        def turns(eng, body):
            for b, before, cross, after in ((-1, True, False, False), (0, True, True, False)):
                w = Counts(eng)
                body(b, w, before, cross, after)
                w.take_off()
            with eng.Fori(1, B - 1) as b:
                w = Counts(eng)
                body(b, w, True, True, True)
                w.take_off()
            for b, before, cross, after in ((B - 1, False, True, True), (B, False, False, True)):
                w = Counts(eng)
                body(b, w, before, cross, after)
                w.take_off()

        AHEAD = 3

        def copied(m):
            return copied_v if m % 3 == 0 else copied_s

        block = ctx.enter_context(nc.Block())

        @block.sync
        def _(sp):
            ks, qs = io["ks"], io["qs"]

            def load_keys(w, nb, h):
                sp.wait_ge(k_free[h], w.next(k_free[h]))
                src = ks[nb][:, 4 * h:4 * h + 4, :].rearrange("d g t -> d (g t)").unsqueeze(0).broadcast_to([2, 2 * HD, 4 * TP])
                sp.dma_start(krep[:, 4 * h:4 * h + 4, :].rearrange("p g t -> p (g t)").bitcast(F32), src).then_inc(ld_kq[h], 16)

            def load_values(w, vb, h):
                sp.wait_ge(v_free[h], w.next(v_free[h]))
                sp.dma_start(val[:, :, P * h:P * h + P],
                             io["ctx"][vb].rearrange("(j t) c -> t j c", t=TC)[:, :, P * h:P * h + P]).then_inc(ld_v[h], 16)

            def store_queries(w, nb, h):
                sp.wait_ge(q_lo_ok, w.next(q_lo_ok))
                for part, src in ((0, qT_hi), (1, qT_lo)):
                    sp.dma_start(qs[nb, part, h].rearrange("d r g s -> r d (g s)"),
                                 src[:, 4 * h:4 * h + 4, :].rearrange("p g s -> p (g s)").bitcast(F32)).then_inc(q_stored[h], 16)

            def load_queries(w, nb, h):
                sp.wait_ge(q_stored[h], w.next(q_stored[h], 32))
                for part in range(2):
                    src = qs[nb, part, h].rearrange("d r g s -> d (r g s)").unsqueeze(0).broadcast_to([2, HD, 4 * NR * S])
                    sp.dma_start(qrep[2 * HD * part:2 * HD * part + 2 * HD, h].rearrange("p r g s -> p (r g s)").bitcast(F32),
                                 src).then_inc(ld_kq[h], 16)

            def body(b, w, before, cross, after):
                nb = b + 1
                if before and first:
                    sp.wait_ge(xt_free, w.next(xt_free))
                    sp.dma_start(xt[:], io["xT"][nb]).then_inc(ld_xt, 16)
                    sp.dma_start(craw[:], io["ctxT"][nb]).then_inc(ld_c, 16)
                    sp.wait_ge(x_free, w.next(x_free))
                    sp.dma_start(xb[0:S, :], io["x"][nb]).then_inc(ld_x, 16)
                if cross:
                    load_keys(w, b, 1)
                    load_queries(w, b, 1)
                    load_values(w, b, 1)
                if before and first:
                    sp.wait_ge(c_lo_ok, w.next(c_lo_ok))
                    for part, src in ((0, c_hi), (1, c_lo)):
                        for h in range(2):
                            sp.dma_start(ks[nb, HD * part:HD * part + HD, 4 * h:4 * h + 4].rearrange("d g t -> g d t"),
                                         src[:, h, :].bitcast(F32)).then_inc(c_stored, 16)
                    sp.wait_ge(c_stored, w.next(c_stored, 64))
                if before:
                    if not first:
                        sp.wait_ge(x_free, w.next(x_free))
                        sp.dma_start(xnew[0:S, :], io["x4"][nb]).then_inc(ld_x, 16)
                    load_keys(w, nb, 0)
                    store_queries(w, nb, 0)
                    load_queries(w, nb, 0)
                    store_queries(w, nb, 1)
                    load_values(w, nb, 0)

            turns(sp, body)

        @block.gpsimd
        def _(pool):
            def root(w, i):
                pool.wait_ge(var_ok[i], w.next(var_ok[i]))
                nc.gpsimd.tensor_scalar(veps[0:S, i:i + 1], mv[0:S, 2 * i + 1:2 * i + 2], EPS, None, ALU.add)
                pool.drain()
                nc.gpsimd.tensor_tensor(rstd[0:S, i:i + 1], veps[0:S, i:i + 1], half[0:S], ALU.pow).then_inc(rstd_ok[i], 1)

            def body(b, w, before, cross, after):
                if before and first:
                    pool.wait_ge(x_hi_ok, w.next(x_hi_ok))
                    nc.gpsimd.tensor_tensor(x_lo[:], xt[:], x_hi[:].bitcast(F32), ALU.subtract).then_inc(split_x, 1)
                    pool.drain().then_inc(xt_free, 1)
                if after:
                    pool.wait_ge(attn_out, w.next(attn_out))
                    nc.gpsimd.tensor_tensor(attn[0:S, :], attn[0:S, :], xcur[0:S, :], ALU.add).then_inc(sum_ok, 1)
                    pool.drain().then_inc(sum_done, 1)
                    root(w, 1)
                if before and first:
                    pool.wait_ge(ld_x, w.next(ld_x, 16))
                    nc.gpsimd.tensor_tensor(xb[0:S], xb[0:S], bias[0:S], ALU.add).then_inc(xb_ok, 1)
                    root(w, 0)
                if after and not first:
                    root(w, 2)

            if first:
                pool.sem_inc(xt_free, 1)
            turns(pool, body)

        def stats(src, i, signal):
            for h in range(2):
                nc.vector.bn_stats(st[0:S, 12 * i + 6 * h:12 * i + 6 * h + 6], src[0:S, 512 * h:512 * h + 512])
            nc.vector.drain()
            nc.vector.bn_aggr(mv[0:S, 2 * i:2 * i + 2], st[0:S, 12 * i:12 * i + 12]).then_inc(signal, 1)

        def normed(dst, src, i, signal):
            nc.vector.tensor_scalar(dst[0:S, 0:D], src[0:S, 0:D], mv[0:S, 2 * i:2 * i + 1], rstd[0:S, i:i + 1],
                                    ALU.subtract, ALU.mult).then_inc(signal, 1)

        @block.tensor
        def _(pe):
            def turn_half(bank, src, h):
                for j in range(4):
                    k = 4 * h + j
                    mm = pe.transpose(bank[:, S * j:S * j + S], src[0:S, P * k:P * k + P], ident[0:S, 0:S])
                return mm

            def products(out, left, right, cols, kt, start, stop):
                n = 0
                for k in range(kt):
                    for a, c in split_passes(left[0], left[1], right[0], right[1]):
                        if start <= n < stop:
                            mm = pe.matmul(out, a[:, k, :], c[:, k, cols], start=(n == 0), stop=(n == 3 * kt - 1))
                        n += 1
                return mm

            def score_step(w, n):
                if n < NH:
                    u, gi = divmod(n, 4)
                    gq, r = divmod(u, NR)
                    g = 4 * gq + gi
                    if n % 16 == 0:
                        pe.wait_ge(ld_kq[gq], w.next(ld_kq[gq], 16 * 3))
                    pe.matmul(scores[0:S, n % 3, 0:TP], qrep[:, gq, r, gi, :], krep[:, g, :],
                              start=True, stop=True).then_inc(score_ok, 1)

            def turn_step(w, m):
                if m < NH:
                    if m >= 2:
                        pe.wait_ge(copied(m - 2), w.next(copied(m - 2)))
                    for j in range(TJ):
                        mm = pe.transpose(turned[0:TC, m % 2, S * j:S * j + S],
                                          probs[0:S, m % 4, TC * j:TC * j + TC], ident[0:S, 0:S])
                        if j == 0 and m in (14, 30):
                            mm.then_inc(k_free[m // 16], 1)
                    mm.then_inc(turned_v if m % 3 == 0 else turned_s, 1)

            def cross_step(w, n, before):
                m = n - 3
                if m < NH:
                    pe.wait_ge(prob_ok, w.next(prob_ok))
                score_step(w, n)
                turn_step(w, m)
                if n == 24 and before:
                    pe.wait_ge(q_read, w.next(q_read))
                if n >= 8 and n % 4 == 0:
                    pv(w, n // 4 - 2)

            def pv(w, u):
                gq, r = divmod(u, NR)
                if r == 0:
                    pe.wait_ge(ld_v[gq], w.next(ld_v[gq], 16))
                if u == NH // 4 - 1:
                    pe.wait_ge(copied(NH - 2), w.next(copied(NH - 2)))
                    pe.wait_ge(copied(NH - 1), w.next(copied(NH - 1)))
                for j in range(TJ):
                    for gi in range(4):
                        g = 4 * gq + gi
                        mm = pe.matmul(wide[HD * gi:HD * gi + HD, gq, S * r:S * r + S],
                                       val[:, j, HD * g:HD * g + HD], probsT[:, (4 * u + gi) % 8, j, :],
                                       start=(j == 0), stop=(j == TJ - 1))
                        if u == 4 and j == 0 and gi == 0:
                            mm.then_inc(v_free[0], 1)
                if r == NR - 1:
                    mm.then_inc((pv_s, pv_v)[gq], 1)

            def after_step(w, n):
                if n == 1:
                    pe.wait_ge(oT_v, w.next(oT_v))
                    for h in range(2):
                        for j in range(4):
                            mm = pe.transpose(wide[0:S, h, P * j:P * j + P], oT[:, 4 * h + j, :], ident[:, :])
                            if h == 0 and j == 0:
                                mm.then_inc(v_free[1], 1)
                        mm.then_inc(attn_ok, 1)
                if n == 5:
                    pe.wait_ge(attn_read, w.next(attn_read, 2))
                if n == 9:
                    bank_read = z_read if first else out_read
                    pe.wait_ge(bank_read, w.next(bank_read))
                    pe.wait_ge(x2_ok, w.next(x2_ok))
                    turn_half(spare, row, 0).then_inc(turn2_ok, 1)
                if n == 12:
                    pe.wait_ge(lo2_ok, w.next(lo2_ok))
                    turn_half(spare, row, 1).then_inc(turn2_ok, 1)
                if n == 15:
                    pe.wait_ge(lo2_ok, w.next(lo2_ok))
                if first:
                    if n in (15, 16):
                        mm = products(spare[0:S, 0:UH], (tT_hi, tT_lo), (wu_hi, wu_lo), slice(0, UH), KT,
                                      12 * (n - 15), 12 * (n - 14))
                    if n in (17, 18):
                        mm = products(spare[0:BOT, UH:UH + S], (wq_hi, wq_lo), (tT_hi, tT_lo), slice(0, S), KT,
                                      12 * (n - 17), 12 * (n - 16))
                    if n == 18:
                        mm.then_inc(gate_h_ok, 1)
                    if n == 21:
                        pe.wait_ge(qaug_ok, w.next(qaug_ok))
                        pe.matmul(spare[0:S, :], qaug[:, :], route[:, :], start=True, stop=True).then_inc(route_ok, 1)
                    if n == 31:
                        pe.wait_ge(slot_w_ok, w.next(slot_w_ok))
                        for j in range(2):
                            mm = pe.transpose(spare[:, S * j:S * j + S], slot_w[0:S, P * j:P * j + P], ident[0:S, 0:S])
                        mm.then_inc(slotT_ok, 1)
                    if n == 33:
                        pe.wait_ge(wT_ok, w.next(wT_ok))
                        for j in range(2):
                            mm = pe.matmul(spare[0:S, UH:UH + BOT], wT[:, j, :], u_val[:, j, :], start=(j == 0), stop=(j == 1))
                        mm.then_inc(z_ok, 1)
                else:
                    if n == 15:
                        products(wide[0:S, 1, 0:NE], (tT_hi, tT_lo), (r_hi, r_lo), slice(0, NE), KT, 0, 24).then_inc(rscore_ok, 1)
                    if 16 <= n < 20:
                        mm = products(spare[0:S, :], (tT_hi, tT_lo), (a_hi, a_lo), slice(0, BN), KT,
                                      6 * (n - 16), 6 * (n - 15))
                    if n == 19:
                        mm.then_inc(bottleneck_ok, 1)
                    if n == 17:
                        pe.wait_ge(sc_read, w.next(sc_read))
                    if n == 23:
                        pe.wait_ge(gated_ok, w.next(gated_ok))
                        for j in range(4):
                            mm = pe.transpose(spare[:, S * j:S * j + S], zg[0:S, P * j:P * j + P], ident[0:S, 0:S])
                        mm.then_inc(gatedT_ok, 1)
                    if n == 26:
                        pe.wait_ge(z_lo_ok, w.next(z_lo_ok))
                    if n == 29:
                        pe.wait_ge(out_read, w.next(out_read))
                    for h, n0 in ((0, 26), (1, 29)):
                        if n0 <= n < n0 + 2:
                            mm = products(spare[0:S, :], (z_hi, z_lo), (b_hi, b_lo), slice(512 * h, 512 * h + 512), 4,
                                          6 * (n - n0), 6 * (n - n0 + 1))
                            if n == n0 + 1:
                                mm.then_inc(out_ok, 1)

            def before_step(w, n, cross):
                if first:
                    if n == 7:
                        pe.wait_ge(split_x, w.next(split_x))
                    if n in (12, 17):
                        pe.wait_ge(lin_read, w.next(lin_read))
                    for h, n0 in ((0, 7), (1, 12)):
                        if n0 <= n < n0 + 4:
                            mm = products(wide[0:S, 1, :], (x_hi, x_lo), (w0_hi, w0_lo), slice(512 * h, 512 * h + 512),
                                          KT, 6 * (n - n0), 6 * (n - n0 + 1))
                            if n == n0 + 3:
                                mm.then_inc(lin_ok, 1)
                if n == 18:
                    if first:
                        pe.wait_ge(x_ok, w.next(x_ok))
                    else:
                        pe.wait_ge(ld_x, w.next(ld_x, 16))
                    turn_half(wide[:, 1, :], xnew, 0).then_inc(turn_ok, 1)
                if n == 21 or n == 24 and not cross:
                    pe.wait_ge(q_read, w.next(q_read))
                if n == 21:
                    turn_half(wide[:, 1, :], xnew, 1).then_inc(turn_ok, 1)

            def body(b, w, before, cross, after):
                for n in range(STEPS):
                    if cross and n >= AHEAD:
                        cross_step(w, n, before)
                    if before and n >= STEPS - AHEAD:
                        score_step(w, n - (STEPS - AHEAD))
                    if cross and n == 25:
                        pe.wait_ge(oT_s, w.next(oT_s))
                    if after:
                        after_step(w, n)
                    if before:
                        before_step(w, n, cross)

            turns(pe, body)

        @block.scalar
        def _(act):
            def after_step(w, n):
                if n in (10, 13):
                    h = n // 13
                    act.wait_ge(turn2_ok, w.next(turn2_ok))
                    nc.scalar.copy(tT_hi[:, 4 * h:4 * h + 4, :],
                                   spare[:, 0:4 * S].rearrange("p (k s) -> p k s", s=S)).then_inc(hi2_ok, 1)
                if first:
                    if n == 20:
                        act.wait_ge(gate_h_read, w.next(gate_h_read))
                        nc.scalar.copy(qaug[0:BOT, :], spare[0:BOT, UH:UH + S]).then_inc(qaug_ok, 1)
                    if n == 23:
                        act.wait_ge(route_ok, w.next(route_ok))
                        nc.scalar.copy(ra[0:S, :], spare[0:S, :]).then_inc(ra_ok, 1)
                    if n == 24:
                        act.wait_ge(gelu_arg_ok, w.next(gelu_arg_ok))
                        nc.scalar.activation(uc[0:S, :], ub[0:S, :], ACT.Tanh, scale=0.7978845608028654).then_inc(tanh_ok, 1)
                    if n == 27:
                        act.wait_ge(least_pen_ok, w.next(least_pen_ok))
                        nc.scalar.activation(slot_w[0:S, :], pen[0:S, :], ACT.Exp, bias=sm[0:S, 1:2], scale=1.0,
                                             accum_out=sm[0:S, 2:3]).then_inc(slot_exp_ok, 1)
                    if n == 32:
                        act.wait_ge(slotT_ok, w.next(slotT_ok))
                        nc.scalar.copy(wT[:, :, :], spare[:, 0:2 * S].rearrange("p (j s) -> p j s", s=S)).then_inc(wT_ok, 1)
                else:
                    if n == 18:
                        act.wait_ge(top_ok, w.next(top_ok))
                        nc.scalar.activation(egate[0:S, :], sc[0:S, :], ACT.Exp, bias=sm[0:S, 1:2], scale=1.0).then_inc(egate_ok, 1)
                    if n == 24:
                        act.wait_ge(gatedT_ok, w.next(gatedT_ok))
                        nc.scalar.copy(z_hi[:, :, :], spare[:, 0:4 * S].rearrange("p (j s) -> p j s", s=S)).then_inc(z_hi_ok, 1)

            def before_step(w, n):
                if first and n == 1:
                    act.wait_ge(ld_xt, w.next(ld_xt, 16))
                    nc.scalar.copy(x_hi[:], xt[:]).then_inc(x_hi_ok, 1)
                if first and n == 6:
                    act.wait_ge(ld_c, w.next(ld_c, 16))
                    nc.scalar.mul(c_hi[:, :, 0:T], craw[:], -float(HD) ** -0.5).then_inc(c_hi_ok, 1)
                if n in (19, 22):
                    h = n // 22
                    act.wait_ge(turn_ok, w.next(turn_ok))
                    nc.scalar.copy(qT_hi[:, 4 * h:4 * h + 4, :],
                                   wide[:, 1, 0:4 * S].rearrange("p (k s) -> p k s", s=S)).then_inc(q_hi_ok, 1)

            def cross_step(w, n):
                m = n - 4
                if 0 <= m < NH and m % 3:
                    act.wait_ge(turned_s, w.next(turned_s))
                    nc.scalar.copy(probsT[:, m % 8, :, :],
                                   turned[0:TC, m % 2, 0:TJ * S].rearrange("p (j s) -> p j s", s=S)).then_inc(copied_s, 1)
                if n < NH:
                    act.wait_ge(least_ok, w.next(least_ok))
                    nc.scalar.activation(probs[0:S, n % 4, :], masked[0:S, n % 3, :], ACT.Exp,
                                         bias=least[0:S, n:n + 1], scale=-1.0,
                                         accum_out=rsum[0:S, n:n + 1]).then_inc(prob_ok, 1)
                if n == 21:
                    act.wait_ge(pv_s, w.next(pv_s))
                    nc.scalar.copy(oT[:, 0:4, :], wide[:, 0, 0:4 * S].rearrange("p (u s) -> p u s", s=S)).then_inc(oT_s, 1)

            def body(b, w, before, cross, after):
                for n in range(STEPS):
                    if cross and n >= AHEAD:
                        cross_step(w, n)
                    if before and n >= STEPS - AHEAD:
                        cross_step(w, n - (STEPS - AHEAD))
                    if after:
                        if n == 8:
                            act.wait_ge(sum_done, w.next(sum_done))
                        after_step(w, n)
                    if cross and n == 8:
                        nc.scalar.copy(xcur[0:S, :], xnew[0:S, :]).then_inc(x_moved, 1)
                    if before:
                        before_step(w, n)
                if after and first:
                    act.wait_ge(row_ok, w.next(row_ok))
                    act.dma_start(io["rows"][b - 1], row[0:S, :]).then_inc(stored, 16)
                if after and not first:
                    act.wait_ge(res_ok, w.next(res_ok))
                    act.dma_start(io["out"][b - 1], res[0:S, :]).then_inc(stored, 16)

            turns(act, body)

        @block.vector
        def _(dve):
            v = nc.vector

            def cross_step(w, n):
                m = n - 4
                if 0 <= m < NH and m % 3 == 0:
                    dve.wait_ge(turned_v, w.next(turned_v))
                    v.tensor_copy(probsT[:, m % 8, :, :],
                                  turned[0:TC, m % 2, 0:TJ * S].rearrange("p (j s) -> p j s", s=S)).then_inc(copied_v, 1)
                if n < NH:
                    dve.wait_ge(score_ok, w.next(score_ok))
                    v.tensor_tensor_reduce(
                        out=masked[0:S, n % 3, :], in0=scores[0:S, n % 3, 0:T], in1=nmask[0:S, :],
                        scale=1.0, scalar=HUGE, op0=ALU.add, op1=ALU.min,
                        accum_out=least[0:S, n:n + 1]).then_inc(least_ok, 1)
                if n == 10:
                    dve.wait_ge(x_moved, w.next(x_moved))
                    if not first:
                        dve.sem_inc(x_free, 1)
                if n == 37:
                    dve.wait_ge(pv_v, w.next(pv_v))
                    v.reciprocal(rinv[0:S, :], rsum[0:S, :])
                    v.tensor_copy(oT[:, 4:8, :], wide[:, 1, 0:4 * S].rearrange("p (u s) -> p u s", s=S)).then_inc(oT_v, 1)

            def after_step(w, n):
                if n == 2:
                    for gq in range(2):
                        dve.wait_ge(attn_ok, w.next(attn_ok))
                        v.tensor_tensor(
                            attn[0:S, 512 * gq:512 * gq + 512].rearrange("p (gi r d) -> p r gi d", gi=4, r=NR),
                            wide[0:S, gq, :].rearrange("p (r gi d) -> p r gi d", r=NR, gi=4),
                            rinv[0:S, 16 * gq:16 * gq + 16].rearrange("p (r gi) -> p r gi", r=NR)
                            .unsqueeze(3).broadcast_to([S, NR, 4, HD]), ALU.mult).then_inc(attn_read, 1)
                    dve.drain().then_inc(attn_out, 1)
                if n == (6 if first else 5):
                    dve.wait_ge(sum_ok, w.next(sum_ok))
                    stats(attn, 1, var_ok[1])
                if n == (8 if first else 7):
                    dve.wait_ge(rstd_ok[1], w.next(rstd_ok[1]))
                    if first:
                        dve.wait_ge(stored, w.next(stored, 16))
                    normed(row, attn, 1, x2_ok)
                if n in (11, 14):
                    h = n // 14
                    dve.wait_ge(hi2_ok, w.next(hi2_ok))
                    v.tensor_tensor(tT_lo[:, 4 * h:4 * h + 4, :], spare[:, 0:4 * S].rearrange("p (k s) -> p k s", s=S),
                                    tT_hi[:, 4 * h:4 * h + 4, :].bitcast(F32), ALU.subtract).then_inc(lo2_ok, 1)
                if first:
                    slot_ffn_step(w, n)
                else:
                    routed_ffn_step(w, n)

            def slot_ffn_step(w, n):
                if n == 9:
                    dve.drain()
                    for h in range(2):
                        v.bn_stats(st[0:S, 24 + 6 * h:30 + 6 * h], row[0:S, 512 * h:512 * h + 512])
                if n == 10:
                    dve.drain()
                    v.bn_aggr(mv[0:S, 4:6], st[0:S, 24:36])
                if n == 13:
                    dve.drain()
                    v.tensor_copy(row[0:S, COL_VAR:COL_VAR + 1], mv[0:S, 5:6])
                if n == 19:
                    dve.wait_ge(gate_h_ok, w.next(gate_h_ok))
                    v.tensor_tensor(ua[0:S, :], spare[0:S, 0:UH], bu1[0:S, :], ALU.add).then_inc(gate_h_read, 1)
                    dve.drain()
                    v.tensor_tensor(ub[0:S, :], ua[0:S, :], ua[0:S, :], ALU.mult)
                if n == 20:
                    dve.drain()
                    v.tensor_scalar(ub[0:S, :], ub[0:S, :], 0.044715, 1.0, ALU.mult, ALU.add)
                    dve.drain()
                    v.tensor_tensor(ub[0:S, :], ub[0:S, :], ua[0:S, :], ALU.mult).then_inc(gelu_arg_ok, 1)
                if n == 24:
                    dve.wait_ge(ra_ok, w.next(ra_ok))
                    v.max(top8[0:S, :], ra[0:S, 0:SLOTS])
                    dve.drain()
                    v.match_replace(out=left[0:S, :], in_to_replace=top8[0:S, :], in_values=ra[0:S, 0:SLOTS], imm_value=-HUGE)
                if n == 25:
                    dve.drain()
                    v.tensor_tensor(left[0:S, :], left[0:S, :], ra[0:S, 0:SLOTS], ALU.not_equal)
                    dve.drain()
                    v.tensor_scalar(left[0:S, :], left[0:S, :], HUGE, -HUGE, ALU.mult, ALU.add)
                if n == 26:
                    dve.drain()
                    v.tensor_tensor_reduce(out=pen[0:S, :], in0=ra[0:S, SLOTS:2 * SLOTS], in1=left[0:S, :], scale=1.0,
                                           scalar=-HUGE, op0=ALU.add, op1=ALU.max, accum_out=sm[0:S, 0:1])
                    dve.drain()
                    v.tensor_scalar(sm[0:S, 1:2], sm[0:S, 0:1], -1.0, None, ALU.mult).then_inc(least_pen_ok, 1)
                if n == 27:
                    dve.wait_ge(tanh_ok, w.next(tanh_ok))
                    v.tensor_scalar(uc[0:S, :], uc[0:S, :], 1.0, 0.5, ALU.add, ALU.mult)
                if n == 29:
                    dve.wait_ge(slot_exp_ok, w.next(slot_exp_ok))
                    v.reciprocal(sm[0:S, 2:3], sm[0:S, 2:3])
                    dve.drain()
                    v.tensor_tensor(uc[0:S, :], uc[0:S, :], ua[0:S, :], ALU.mult)
                    v.tensor_scalar(slot_w[0:S, :], slot_w[0:S, :], sm[0:S, 2:3], None, ALU.mult).then_inc(slot_w_ok, 1)
                if n == 32:
                    dve.drain()
                    v.tensor_tensor(uc[0:S, :], uc[0:S, :], wu2[0:S, :], ALU.mult)
                    dve.drain()
                    v.tensor_reduce(sm[0:S, 3:4], uc[0:S, :], AX.X, ALU.add)
                if n == 34:
                    dve.wait_ge(z_ok, w.next(z_ok))
                    v.tensor_copy(row[0:S, COL_Z:COL_Z + BOT], spare[0:S, UH:UH + BOT]).then_inc(z_read, 1)
                    dve.drain()
                    v.tensor_tensor(row[0:S, COL_LEARNED:COL_LEARNED + 1], sm[0:S, 3:4], bu2[0:S, :], ALU.add)
                    dve.drain().then_inc(row_ok, 1)

            def routed_ffn_step(w, n):
                if n == 16:
                    dve.wait_ge(rscore_ok, w.next(rscore_ok))
                    v.tensor_copy(sc[0:S, :], wide[0:S, 1, 0:NE]).then_inc(sc_read, 1)
                    dve.drain()
                    v.max(top8[0:S, :], sc[0:S, :])
                    dve.drain()
                    v.tensor_scalar(sm[0:S, 1:2], top8[0:S, 0:1], -1.0, None, ALU.mult).then_inc(top_ok, 1)
                if n == 18:
                    v.match_replace(out=sc1[0:S, :], in_to_replace=top8[0:S, :], in_values=sc[0:S, :], imm_value=-HUGE)
                    dve.drain()
                    v.max(top16[0:S, :], sc1[0:S, :])
                if n == 19:
                    dve.drain()
                    v.match_replace(out=sc2[0:S, :], in_to_replace=top16[0:S, :], in_values=sc1[0:S, :], imm_value=-HUGE)
                if n == 19:
                    dve.drain()
                    v.tensor_tensor(sel[0:S, :], sc2[0:S, :], sc[0:S, :], ALU.not_equal)
                    dve.drain()
                    dve.wait_ge(egate_ok, w.next(egate_ok))
                    v.tensor_tensor(sel[0:S, :], sel[0:S, :], egate[0:S, :], ALU.mult)
                if n == 20:
                    dve.drain()
                    v.tensor_reduce(sm[0:S, 2:3], sel[0:S, :], AX.X, ALU.add)
                    dve.drain()
                    v.reciprocal(sm[0:S, 2:3], sm[0:S, 2:3])
                if n == 21:
                    dve.drain()
                    v.tensor_scalar(sel[0:S, :], sel[0:S, :], sm[0:S, 2:3], None, ALU.mult)
                    dve.drain()
                    dve.wait_ge(bottleneck_ok, w.next(bottleneck_ok))
                    v.tensor_tensor(zg[0:S, :].rearrange("p (e k) -> p e k", k=RANK),
                                    spare[0:S, :].rearrange("p (e k) -> p e k", k=RANK),
                                    sel[0:S, :].unsqueeze(2).broadcast_to([S, NE, RANK]), ALU.mult).then_inc(gated_ok, 1)
                if n == 25:
                    dve.wait_ge(z_hi_ok, w.next(z_hi_ok))
                    v.tensor_tensor(z_lo[:, :, :], spare[:, 0:4 * S].rearrange("p (j s) -> p j s", s=S),
                                    z_hi[:, :, :].bitcast(F32), ALU.subtract).then_inc(z_lo_ok, 1)
                if n in (28, 31):
                    h = n // 31
                    if h == 0:
                        dve.wait_ge(stored, w.next(stored, 16))
                    cols = slice(512 * h, 512 * h + 512)
                    dve.wait_ge(out_ok, w.next(out_ok))
                    v.scalar_tensor_tensor(out=res[0:S, cols], in0=spare[0:S, :], scalar=2.0,
                                           in1=row[0:S, cols], op0=ALU.mult, op1=ALU.add).then_inc(out_read, 1)
                if n == 32:
                    dve.drain()
                    stats(res, 2, var_ok[2])
                if n == 34:
                    dve.wait_ge(rstd_ok[2], w.next(rstd_ok[2]))
                    normed(res, res, 2, res_ok)

            def before_step(w, n):
                if first:
                    if n == 8:
                        dve.wait_ge(c_hi_ok, w.next(c_hi_ok))
                        v.scalar_tensor_tensor(out=c_lo[:, :, 0:T], in0=craw[:], scalar=-float(HD) ** -0.5,
                                               in1=c_hi[:, :, 0:T].bitcast(F32), op0=ALU.mult, op1=ALU.subtract).then_inc(c_lo_ok, 1)
                    if n == 11:
                        dve.wait_ge(xb_ok, w.next(xb_ok))
                    if n in (11, 16):
                        cols = slice(0, 512) if n == 11 else slice(512, 1024)
                        dve.wait_ge(lin_ok, w.next(lin_ok))
                        v.tensor_tensor(xb[0:S, cols], wide[0:S, 1, :], xb[0:S, cols], ALU.add).then_inc(lin_read, 1)
                        dve.drain()
                        h = n // 16
                        v.bn_stats(st[0:S, 6 * h:6 * h + 6], xb[0:S, cols])
                    if n == 16:
                        dve.drain()
                        v.bn_aggr(mv[0:S, 0:2], st[0:S, 0:12]).then_inc(var_ok[0], 1)
                    if n == 17:
                        dve.wait_ge(rstd_ok[0], w.next(rstd_ok[0]))
                        normed(xnew, xb, 0, x_ok)
                        dve.drain().then_inc(x_free, 1)
                if n in (20, 22 if first else 23):
                    h = n // 22
                    dve.wait_ge(q_hi_ok, w.next(q_hi_ok))
                    v.tensor_tensor(qT_lo[:, 4 * h:4 * h + 4, :], wide[:, 1, 0:4 * S].rearrange("p (k s) -> p k s", s=S),
                                    qT_hi[:, 4 * h:4 * h + 4, :].bitcast(F32), ALU.subtract).then_inc(q_read, 1)
                    dve.drain().then_inc(q_lo_ok, 1)

            def body(b, w, before, cross, after):
                for n in range(STEPS):
                    if cross and n >= AHEAD:
                        cross_step(w, n)
                    if before and n >= STEPS - AHEAD:
                        cross_step(w, n - (STEPS - AHEAD))
                    if after:
                        after_step(w, n)
                    if before:
                        before_step(w, n)

            for h in range(2):
                dve.sem_inc(k_free[h], 1)
                dve.sem_inc(v_free[h], 1)
            dve.sem_inc(x_free, 1)
            dve.sem_inc(stored, 16)
            dve.sem_inc(z_read if first else out_read, 1)
            turns(dve, body)
            dve.wait_ge(stored, 16)
            dve.sem_inc(stored, -16)


def self_attention(nc, io, sem):
    NBLK = S // 8
    NC = NBLK // 2
    TH = NC * P
    NKV, QPG, DH = 8, 4, 128
    UNITS = QPG + 2
    CHUNKS = (slice(0, 512), slice(512, TH))

    with ExitStack() as ctx:
        def sb(name, shape, dt=F32):
            return ctx.enter_context(nc.sbuf_tensor(f"sa_{name}", shape, dt))

        feat = ctx.enter_context(nc.psum_tensor("sa_feat", [P, 2, 2, 512], F32))
        score = ctx.enter_context(nc.psum_tensor("sa_score", [P, 512], F32))
        ring = ctx.enter_context(nc.psum_tensor("sa_ring", [P, 3, 512], F32))

        ident, causal = sb("ident", [P, P]), sb("causal", [P, 32])
        gate = sb("gate", [P, NBLK])
        half_exp = sb("half_exp", [P, 1])
        x_hi, x_lo = sb("x_hi", [P, KT, TH], F32R), sb("x_lo", [P, KT, TH], F32R)
        acc = sb("acc", [P, NC, D])
        st, mv, veps, rstd = sb("st", [P, 12]), sb("mv", [P, 2]), sb("veps", [P, 1]), sb("rstd", [P, 1])

        gate_stage(nc, io, sem, ident, causal, half_exp, gate, ring, NBLK)
        for half in range(2):
            load_half(nc, io, sem, half, NC, ident, half_exp, gate, x_hi, x_lo, acc, st, mv, veps, rstd, feat, ring, score)
            heads_half(nc, io, sem, half, NC, TH, NKV, QPG, DH, UNITS, CHUNKS,
                       ident, causal, x_hi, x_lo, acc, feat, score, ring)
            store_half(nc, io, sem, half, NC, half_exp, acc, st, mv, veps, rstd)


def gate_stage(nc, io, sem, ident, causal, half_exp, gate, ring, NBLK):
    with ExitStack() as ctx:
        def sb(name, shape):
            return ctx.enter_context(nc.sbuf_tensor(f"gate_{name}", shape, F32))

        pair = sb("pair", [P, NBLK, 2])
        ones, w1, gb = sb("ones", [P, P]), sb("w1", [P, 1]), sb("gb", [P, 1])
        lv, lsum, u, t = sb("lv", [P, NBLK]), sb("lsum", [P, 1]), sb("u", [P, NBLK]), sb("t", [P, NBLK])
        mean = sb("mean", [P, 1])
        loaded, log_ok, sum_ok, tanh_ok, arg_ok, tanh2_ok = (
            sem(f"gate_{n}") for n in ("loaded", "log", "sum", "tanh", "arg", "tanh2"))
        block = ctx.enter_context(nc.Block())
        srcs = 8

        @block.sync
        def _(sp):
            for dst, src in ((ident, "ident"), (causal, "causal"), (ones, "ones"), (w1, "gate_w1"), (gb, "gate_bias")):
                sp.dma_start(dst[:], io[src]).then_inc(loaded, 16)
            rows = io["rows"].rearrange("b (c l) n -> l b c n", l=8)
            for l in range(srcs):
                sp.dma_start(pair[16 * l:16 * l + 16, :, :], rows[l, :, :, COL_LEARNED:COL_VAR + 1]).then_inc(loaded, 16)

        @block.scalar
        def _(act):
            act.wait_ge(loaded, 16 * (5 + srcs))
            nc.scalar.activation(t[:], pair[:, :, 0], ACT.Tanh, scale=0.5).then_inc(tanh_ok, 1)
            nc.scalar.activation(lv[:], pair[:, :, 1], ACT.Ln, bias=1.0, scale=1.0, accum_out=lsum[:]).then_inc(log_ok, 1)
            act.wait_ge(arg_ok, 1)
            nc.scalar.activation(t[:], u[:], ACT.Tanh, scale=0.5).then_inc(tanh2_ok, 1)

        @block.tensor
        def _(pe):
            pe.wait_ge(log_ok, 1)
            pe.matmul(ring[:, 0, 0:1], ones[:], lsum[:], start=True, stop=True).then_inc(sum_ok, 1)

        @block.vector
        def _(dve):
            v = nc.vector
            v.memset(half_exp[:], -0.5)
            dve.wait_ge(tanh_ok, 1)
            v.tensor_scalar(t[:], t[:], 1.0, 1.25, ALU.add, ALU.mult)
            dve.wait_ge(sum_ok, 1)
            v.tensor_scalar(mean[:], ring[:, 0, 0:1], 1.0 / (B * S), 1e-6, ALU.mult, ALU.add)
            dve.drain()
            v.reciprocal(mean[:], mean[:])
            dve.drain()
            v.tensor_scalar(lv[:], lv[:], mean[:, 0:1], 0.5, ALU.mult, ALU.mult)
            dve.drain()
            v.tensor_tensor(u[:], lv[:], t[:], ALU.add)
            dve.drain()
            v.tensor_scalar(u[:], u[:], 0.0, 5.0, ALU.max, ALU.min)
            dve.drain()
            v.tensor_scalar(u[:], u[:], -0.5, 1.0 / 1.5, ALU.add, ALU.mult)
            dve.drain()
            v.tensor_scalar(u[:], u[:], 0.0, 1.0, ALU.max, ALU.min)
            dve.drain()
            v.tensor_scalar(u[:], u[:], w1[:, 0:1], gb[:, 0:1], ALU.mult, ALU.add).then_inc(arg_ok, 1)
            dve.wait_ge(tanh2_ok, 1)
            v.tensor_scalar(t[:], t[:], 1.0, 0.5, ALU.add, ALU.mult)
            dve.drain()
            v.tensor_scalar(u[:], t[:], 0.05, None, ALU.is_ge)
            dve.drain()
            v.tensor_tensor(gate[:], t[:], u[:], ALU.mult)


def load_half(nc, io, sem, half, NC, ident, half_exp, gate, x_hi, x_lo, acc, st, mv, veps, rstd, feat, ring, score):
    with ExitStack() as ctx:
        def sb(name, shape):
            return ctx.enter_context(nc.sbuf_tensor(f"load{half}_{name}", shape, F32))

        def s(name):
            return sem(f"load{half}_{name}")

        wvu = sb("wvu", [BOT, D])
        x2z = sb("x2z", [P, 2, D + BOT])
        zT = sb("zT", [BOT, P])
        g = sb("g", [P, 1])
        y = sb("y", [P, 2, D])
        ld_w, row_free, zt_ok, zT_ok, aux_ok = s("ld_w"), s("row_free"), s("zt"), s("zT"), s("aux")
        ld_row = [s("ld_row0"), s("ld_row1")]
        var_ok, rstd_ok, x3_ok, turn_ok, hi_ok, lo_ok = s("var"), s("rstd"), s("x3"), s("turn"), s("hi"), s("lo")

        def aux(i):
            return ring[:, 0:2, :] if i == 0 else feat[:, 1, :, :]

        def turns(eng, body):
            with eng.Fori(0, NC // 2) as n:
                w = Counts(eng)
                for i in range(2):
                    body(2 * n + i, i, w, False)
                w.take_off()
            w = Counts(eng)
            body(NC - 1, 0, w, True)
            w.take_off()

        block = ctx.enter_context(nc.Block())

        @block.sync
        def _(sp):
            sp.dma_start(wvu[:], io["wvuT"]).then_inc(ld_w, 16)
            rows = io["rows"].rearrange("b (h c l) n -> h c l b n", h=2, l=8)[half]

            def body(c, i, w, last):
                sp.wait_ge(row_free, w.next(row_free))
                for l in range(8):
                    sp.dma_start(x2z[16 * l:16 * l + 16, i, :], rows[c, l, :, 0:D + BOT]).then_inc(ld_row[i], 16)

            turns(sp, body)

        @block.gpsimd
        def _(pool):
            def body(c, i, w, last):
                pool.wait_ge(var_ok, w.next(var_ok))
                nc.gpsimd.tensor_scalar(veps[:], mv[:, 1:2], EPS, None, ALU.add)
                pool.drain()
                nc.gpsimd.tensor_tensor(rstd[:], veps[:], half_exp[:], ALU.pow).then_inc(rstd_ok, 1)

            turns(pool, body)

        @block.tensor
        def _(pe):
            def take_aux(w, i):
                pe.wait_ge(ld_row[i], w.next(ld_row[i], 16 * 8))
                pe.transpose(score[0:BOT, 0:P], x2z[:, i, D:D + BOT], ident[:]).then_inc(zt_ok, 1)
                pe.wait_ge(zT_ok, w.next(zT_ok))
                for h in range(2):
                    pe.matmul(aux(i)[:, h, :], zT[:], wvu[:, 512 * h:512 * h + 512],
                              start=True, stop=True).then_inc(aux_ok, 1)

            def body(c, i, w, last):
                if not last:
                    take_aux(w, 1 - i)
                pe.wait_ge(x3_ok, w.next(x3_ok))
                pe.wait_ge(lo_ok, w.next(lo_ok, 2))
                for h in range(2):
                    for j in range(4):
                        k = 4 * h + j
                        mm = pe.transpose(feat[:, 0, h, P * j:P * j + P], y[:, i, P * k:P * k + P], ident[:])
                    mm.then_inc(turn_ok, 1)

            pe.wait_ge(ld_w, 16)
            w = Counts(pe)
            take_aux(w, 0)
            w.take_off()
            turns(pe, body)

        @block.scalar
        def _(act):
            def turn_z(w):
                act.wait_ge(zt_ok, w.next(zt_ok))
                nc.scalar.copy(zT[:], score[0:BOT, 0:P]).then_inc(zT_ok, 1)

            def body(c, i, w, last):
                if not last:
                    turn_z(w)
                for h in range(2):
                    act.wait_ge(turn_ok, w.next(turn_ok))
                    if h == 1:
                        nc.scalar.copy(acc[:, bass.ds(c, 1), :], y[:, i:i + 1, :])
                    nc.scalar.copy(x_hi[:, 4 * h:4 * h + 4, bass.ds(c * P, P)],
                                   feat[:, 0, h, :].rearrange("p (k t) -> p k t", k=4)).then_inc(hi_ok, 1)

            w = Counts(act)
            turn_z(w)
            w.take_off()
            turns(act, body)

        @block.vector
        def _(dve):
            v = nc.vector

            def low_part(w, c):
                for h in range(2):
                    dve.wait_ge(hi_ok, w.next(hi_ok))
                    v.tensor_tensor(x_lo[:, 4 * h:4 * h + 4, bass.ds(c * P, P)],
                                    feat[:, 0, h, :].rearrange("p (k t) -> p k t", k=4),
                                    x_hi[:, 4 * h:4 * h + 4, bass.ds(c * P, P)].bitcast(F32), ALU.subtract).then_inc(lo_ok, 1)

            def sum_up(w, c, i):
                v.tensor_copy(g[:], gate[:, bass.ds(c + half * NC, 1)])
                dve.drain()
                for h in range(2):
                    cols = slice(512 * h, 512 * h + 512)
                    dve.wait_ge(aux_ok, w.next(aux_ok))
                    v.scalar_tensor_tensor(out=y[:, i, cols], in0=aux(i)[:, h, :], scalar=g[:, 0:1],
                                           in1=x2z[:, i, cols], op0=ALU.mult, op1=ALU.add)
                dve.drain()
                v.tensor_tensor(y[:, i, :], y[:, i, :], x2z[:, i, 0:D], ALU.add)
                dve.drain().then_inc(row_free, 1)
                for h in range(2):
                    v.bn_stats(st[:, 6 * h:6 * h + 6], y[:, i, 512 * h:512 * h + 512])
                dve.drain()
                v.bn_aggr(mv[:], st[:]).then_inc(var_ok, 1)

            def finish(w, i):
                dve.wait_ge(rstd_ok, w.next(rstd_ok))
                v.tensor_scalar(y[:, i, :], y[:, i, :], mv[:, 0:1], rstd[:, 0:1], ALU.subtract, ALU.mult).then_inc(x3_ok, 1)

            def body(c, i, w, last):
                if not last:
                    sum_up(w, c + 1, 1 - i)
                low_part(w, c)
                if not last:
                    finish(w, 1 - i)

            dve.sem_inc(row_free, 2)
            dve.sem_inc(lo_ok, 2)
            w = Counts(dve)
            sum_up(w, 0, 0)
            finish(w, 0)
            w.take_off()
            turns(dve, body)


def heads_half(nc, io, sem, half, NC, TH, NKV, QPG, DH, UNITS, CHUNKS,
               ident, causal, x_hi, x_lo, acc, feat, score, ring):
    with ExitStack() as ctx:
        def sb(name, shape, dt=F32):
            return ctx.enter_context(nc.sbuf_tensor(f"heads{half}_{name}", shape, dt))

        def s(name):
            return sem(f"heads{half}_{name}")

        raw = sb("raw", [P, 2, D])
        w_hi, w_lo = sb("w_hi", [P, 2, KT, DH], F32R), sb("w_lo", [P, 2, KT, DH], F32R)
        p_hi, p_lo = sb("p_hi", [P, QPG, D], F32R), sb("p_lo", [P, QPG, D], F32R)
        qT, kT, vT = sb("qT", [P, QPG, TH]), sb("kT", [P, TH]), sb("vT", [P, TH])
        val = sb("val", [P, NC, DH])
        sm, ex = sb("sm", [P, NC, 32]), sb("ex", [P, NC, 32])
        most, total = sb("most", [P, NC]), sb("total", [P, NC])
        probsT = sb("probsT", [P, QPG, NC, P])
        o_hi, o_lo = sb("o_hi", [P, QPG, TH], F32R), sb("o_lo", [P, QPG, TH], F32R)

        ld_raw, raw_free = [s("ld_raw0"), s("ld_raw1")], s("raw_free")
        unit_ok, w_free, p_free = s("unit_ok"), s("w_free"), s("p_free")
        feat_ok, feat_sb = s("feat_ok"), s("feat_sb")
        score_ok, score_free, arg_ok, exp_ok, probs_ok = s("score_ok"), s("score_free"), s("arg_ok"), s("exp_ok"), s("probs_ok")
        vt_ok, val_ok, pv_ok, o_hi_ok, o_lo_ok = s("vt_ok"), s("val_ok"), s("pv_ok"), s("o_hi_ok"), s("o_lo_ok")
        proj_ok, acc_ok = s("proj_ok"), s("acc_ok")
        block = ctx.enter_context(nc.Block())
        ORDER = [QPG] + list(range(QPG)) + [QPG + 1]
        SPLITS = [(0, None), (1, None), (2, None), (None, 0), (3, None), (4, None), (None, 1), (5, None), (None, 2), (None, 3)]
        p_ok = s("p_ok")

        @block.sync
        def _(sp):
            with sp.Fori(0, NKV) as g:
                w = Counts(sp)
                for i, (u, p) in enumerate(SPLITS):
                    sp.wait_ge(raw_free, w.next(raw_free))
                    src = io["wqkvU"][g, ORDER[u]] if p is None else io["wprojU"][g, p]
                    sp.dma_start(raw[:, i % 2, :], src).then_inc(ld_raw[i % 2], 16)
                w.take_off()

        @block.gpsimd
        def _(pool):
            with pool.Fori(0, NKV) as g:
                w = Counts(pool)
                for i, (u, p) in enumerate(SPLITS):
                    pool.wait_ge(ld_raw[i % 2], w.next(ld_raw[i % 2], 16))
                    if p is None:
                        pool.wait_ge(w_free, w.next(w_free))
                        hi, lo = w_hi[:, u % 2, :, :], w_lo[:, u % 2, :, :]
                        src = raw[:, i % 2, :].rearrange("p (k n) -> p k n", k=KT)
                    else:
                        if p == 0:
                            pool.wait_ge(p_free, w.next(p_free))
                        hi, lo, src = p_hi[:, p, :], p_lo[:, p, :], raw[:, i % 2, :]
                    nc.gpsimd.tensor_copy(hi, src)
                    pool.drain()
                    nc.gpsimd.tensor_tensor(lo, src, hi.bitcast(F32), ALU.subtract).then_inc(unit_ok if p is None else p_ok, 1)
                    pool.drain().then_inc(raw_free, 1)
                w.take_off()

        @block.tensor
        def _(pe):
            def scores(w, j):
                pe.wait_ge(score_free, w.next(score_free))
                for c in range(NC):
                    for p in range(4):
                        t = slice(P * c + 32 * p, P * c + 32 * p + 32)
                        mm = pe.matmul(score[32 * p:32 * p + 32, 32 * c:32 * c + 32], qT[:, j, t], kT[:, t],
                                       start=True, stop=True)
                mm.then_inc(score_ok, 1)

            with pe.Fori(0, NKV) as g:
                w = Counts(pe)
                for u in range(UNITS):
                    pe.wait_ge(unit_ok, w.next(unit_ok))
                    for i, t in enumerate(CHUNKS):
                        n = 0
                        for k in range(KT):
                            if u >= 2 and (i, k) == (0, 3):
                                pe.wait_ge(feat_sb, w.next(feat_sb, 2 if u == 2 else 1))
                                scores(w, u - 2)
                            for a, b in split_passes(w_hi, w_lo, x_hi, x_lo):
                                mm = pe.matmul(feat[:, u % 2, i, 0:t.stop - t.start], a[:, u % 2, k, :], b[:, k, t],
                                               start=(n == 0), stop=(n == 3 * KT - 1))
                                n += 1
                        mm.then_inc(feat_ok, 1)
                pe.wait_ge(feat_sb, w.next(feat_sb))
                for i in range(2):
                    pe.wait_ge(acc_ok, w.next(acc_ok))
                    for c in range(4 * i, min(4 * i + 4, NC)):
                        mm = pe.transpose(ring[:, i, P * (c % 4):P * (c % 4) + P], vT[:, P * c:P * c + P], ident[:])
                    mm.then_inc(vt_ok, 1)
                pe.wait_ge(probs_ok, w.next(probs_ok, QPG))
                pe.wait_ge(val_ok, w.next(val_ok, 2))
                for c in range(NC):
                    if c == 0:
                        pe.wait_ge(acc_ok, w.next(acc_ok))
                    if c >= 3:
                        pe.wait_ge(o_lo_ok, w.next(o_lo_ok))
                    pe.matmul(ring[:, (2 + c) % 3, :], val[:, c, :], probsT[:, :, c, :],
                              start=True, stop=True).then_inc(pv_ok, 1)
                pe.wait_ge(p_ok, w.next(p_ok, QPG))
                for c in range(NC):
                    for h in range(2):
                        n = 2 * c + h
                        pe.wait_ge(o_lo_ok if n < 3 else acc_ok, w.next(o_lo_ok if n < 3 else acc_ok))
                        i = 0
                        for j in range(QPG):
                            for a, b in split_passes(o_hi, o_lo, p_hi, p_lo):
                                mm = pe.matmul(ring[:, (2 + NC + n) % 3, :], a[:, j, P * c:P * c + P],
                                               b[:, j, 512 * h:512 * h + 512], start=(i == 0), stop=(i == 3 * QPG - 1))
                                i += 1
                        mm.then_inc(proj_ok, 1)
                w.take_off()

        @block.scalar
        def _(act):
            def take_exp(w):
                act.wait_ge(arg_ok, w.next(arg_ok))
                nc.scalar.activation(ex[:], sm[:], ACT.Exp).then_inc(exp_ok, 1)

            with act.Fori(0, NKV) as g:
                w = Counts(act)
                for u in range(UNITS):
                    dst = kT[:, :] if u == 0 else (vT[:, :] if u == UNITS - 1 else qT[:, u - 1, :])
                    for i, t in enumerate(CHUNKS):
                        act.wait_ge(feat_ok, w.next(feat_ok))
                        last = nc.scalar.copy(dst[:, t], feat[:, u % 2, i, 0:t.stop - t.start])
                        if u >= 2 and i == 0:
                            take_exp(w)
                    last.then_inc(w_free, 1)
                    act.drain().then_inc(feat_sb, 1)
                for i in range(2):
                    act.wait_ge(vt_ok, w.next(vt_ok))
                    n = min(4, NC - 4 * i)
                    nc.scalar.copy(val[:, 4 * i:4 * i + n, :],
                                   ring[:, i, 0:P * n].rearrange("p (c d) -> p c d", c=n)).then_inc(val_ok, 1)
                for c in range(NC):
                    act.wait_ge(pv_ok, w.next(pv_ok))
                    nc.scalar.copy(o_hi[:, :, P * c:P * c + P],
                                   ring[:, (2 + c) % 3, :].rearrange("p (j t) -> p j t", j=QPG)).then_inc(o_hi_ok, 1)
                w.take_off()

        @block.vector
        def _(dve):
            v = nc.vector
            v.memset(probsT[:].bitcast(F32), 0.0)
            dve.drain()
            dve.sem_inc(raw_free, 2)
            dve.sem_inc(w_free, 2)
            dve.sem_inc(p_free, 1)
            dve.sem_inc(score_free, 1)
            dve.sem_inc(acc_ok, 3)
            with dve.Fori(0, NKV) as g:
                w = Counts(dve)
                for j in range(QPG):
                    dve.wait_ge(score_ok, w.next(score_ok))
                    v.scalar_tensor_tensor(out=sm[:], in0=score[:, 0:32 * NC].rearrange("p (c t) -> p c t", c=NC),
                                           scalar=float(DH) ** -0.5, in1=causal[:].unsqueeze(1).broadcast_to([P, NC, 32]),
                                           op0=ALU.mult, op1=ALU.add)
                    dve.drain().then_inc(score_free, 1)
                    v.tensor_reduce(most[:], sm[:], AX.X, ALU.max)
                    dve.drain()
                    v.tensor_tensor(sm[:], sm[:], most[:].unsqueeze(2).broadcast_to([P, NC, 32]),
                                    ALU.subtract).then_inc(arg_ok, 1)
                    dve.wait_ge(exp_ok, w.next(exp_ok))
                    v.tensor_reduce(total[:], ex[:], AX.X, ALU.add)
                    dve.drain()
                    v.reciprocal(total[:], total[:])
                    dve.drain()
                    v.tensor_tensor(ex[:], ex[:], total[:].unsqueeze(2).broadcast_to([P, NC, 32]), ALU.mult)
                    dve.drain()
                    for p in range(4):
                        q = slice(32 * p, 32 * p + 32)
                        v.transpose(probsT[q, j, :, q], ex[q, :, :])
                    dve.drain().then_inc(probs_ok, 1)
                for c in range(NC):
                    dve.wait_ge(o_hi_ok, w.next(o_hi_ok))
                    v.tensor_tensor(o_lo[:, :, P * c:P * c + P],
                                    ring[:, (2 + c) % 3, :].rearrange("p (j t) -> p j t", j=QPG),
                                    o_hi[:, :, P * c:P * c + P].bitcast(F32), ALU.subtract).then_inc(o_lo_ok, 1)
                for c in range(NC):
                    for h in range(2):
                        n = 2 * c + h
                        cols = slice(512 * h, 512 * h + 512)
                        dve.wait_ge(proj_ok, w.next(proj_ok))
                        v.tensor_tensor(acc[:, c, cols], acc[:, c, cols], ring[:, (2 + NC + n) % 3, :],
                                        ALU.add).then_inc(acc_ok, 1)
                dve.drain().then_inc(p_free, 1)
                w.take_off()


def store_half(nc, io, sem, half, NC, half_exp, acc, st, mv, veps, rstd):
    with ExitStack() as ctx:
        y = ctx.enter_context(nc.sbuf_tensor(f"store{half}_y", [P, D], F32))
        var_ok, rstd_ok, y_ok, stored = (sem(f"store{half}_{n}") for n in ("var", "rstd", "y", "stored"))
        block = ctx.enter_context(nc.Block())

        @block.sync
        def _(sp):
            dst = io["x4"].rearrange("b (h c l) n -> h c l b n", h=2, l=8)[half]
            with sp.Fori(0, NC) as c:
                w = Counts(sp)
                sp.wait_ge(y_ok, w.next(y_ok))
                for l in range(8):
                    sp.dma_start(dst[c, l, :, :], y[16 * l:16 * l + 16, :]).then_inc(stored, 16)
                w.take_off()

        @block.gpsimd
        def _(pool):
            with pool.Fori(0, NC) as c:
                w = Counts(pool)
                pool.wait_ge(var_ok, w.next(var_ok))
                nc.gpsimd.tensor_scalar(veps[:], mv[:, 1:2], EPS, None, ALU.add)
                pool.drain()
                nc.gpsimd.tensor_tensor(rstd[:], veps[:], half_exp[:], ALU.pow).then_inc(rstd_ok, 1)
                w.take_off()

        @block.vector
        def _(dve):
            v = nc.vector
            dve.sem_inc(stored, 16 * 8)
            with dve.Fori(0, NC) as c:
                w = Counts(dve)
                for h in range(2):
                    v.bn_stats(st[:, 6 * h:6 * h + 6], acc[:, bass.ds(c, 1), 512 * h:512 * h + 512])
                dve.drain()
                v.bn_aggr(mv[:], st[:]).then_inc(var_ok, 1)
                dve.wait_ge(rstd_ok, w.next(rstd_ok))
                dve.wait_ge(stored, w.next(stored, 16 * 8))
                v.tensor_scalar(y[:].unsqueeze(1), acc[:, bass.ds(c, 1), :], mv[:, 0:1], rstd[:, 0:1],
                                ALU.subtract, ALU.mult).then_inc(y_ok, 1)
                w.take_off()
            dve.wait_ge(stored, 16 * 8)
            dve.sem_inc(stored, -16 * 8)


def build(nc, io, out):
    ks = nc.dram_tensor("ctx_parts", [B, 2 * HD, NG, TP], F32).ap()
    qs = nc.dram_tensor("query_parts", [B, 2, 2, HD, NR, 4, S], F32).ap()
    rows = nc.dram_tensor("rows", [B, S, ROW], F32).ap()
    x4 = nc.dram_tensor("x4", [B, S, D], F32).ap()
    io = dict(io, ks=ks, qs=qs, rows=rows, x4=x4, out=out)

    def stage(fn, *args):
        with ExitStack() as ctx:
            used = []

            def sem(name):
                used.append(ctx.enter_context(nc.semaphore(name)))
                return used[-1]

            fn(*args, sem)
            with nc.Block() as block:
                @block.gpsimd
                def _(pool):
                    for one in used:
                        pool.sem_clear(one)

    stage(token_stage, nc, 0, io)
    stage(self_attention, nc, io)
    stage(token_stage, nc, 1, io)


def layouts(a):
    def rows(v, n=P):
        return np.broadcast_to(np.reshape(v, (1, -1)), (n, np.size(v)))

    lr = np.reshape(a["L0_ffn_log_rel"], (1, -1))
    r = np.arange(P) % 32
    allowed = (r[:, None] // 16 == np.arange(32)[None] // 16) & (np.arange(32)[None] % 16 <= r[:, None] % 16)
    return {
        "x": a["x"], "xT": np.transpose(np.reshape(a["x"], (B, S, KT, P)), (0, 3, 2, 1)),
        "ctx": a["ctx_1024"], "ctxT": np.transpose(np.reshape(a["ctx_1024"], (B, T, 2, P)), (0, 3, 2, 1)),
        "mask": a["mask_SxS2_ff0"],
        "bmaskT": np.transpose(a["L0_attn_mask"]), "w0T": np.transpose(a["L0_attn_weight"]),
        "b0": rows(a["L0_attn_bias"]),
        "wu1T": np.transpose(a["L0_ffn_Wu1"]), "bu1": rows(a["L0_ffn_bu1"]),
        "wu2": rows(a["L0_ffn_Wu2"]), "bu2": rows(a["L0_ffn_bu2"]),
        "wqT": np.transpose(a["L0_ffn_Wq"]), "wr": a["L0_ffn_Wr"], "wrT": np.transpose(a["L0_ffn_Wr"]),
        "keysT": np.transpose(a["L0_ffn_aux_keys"]), "valuesT": np.transpose(a["L0_ffn_aux_values"]),
        "log_rel": np.concatenate([lr, lr], axis=1),
        "wvdT": np.transpose(a["L0_ffn_Wvd"]), "wvuT": np.transpose(a["L0_ffn_Wvu"]),
        "gate_w1": rows(a["L0_ffn_gate_w1"]), "gate_bias": rows(a["L0_ffn_gate_bias"]),
        "wqkvU": np.reshape(np.transpose(np.reshape(a["L1_attn_weight_qkv"], (8, 6, P, KT, P)), (0, 1, 4, 3, 2)),
                            (8, 6, P, D)),
        "wprojU": np.reshape(np.transpose(a["L1_attn_weight_proj"]), (8, 4, P, D)),
        "awT": np.transpose(a["L1_ffn_A_w"]), "bwT": np.transpose(a["L1_ffn_B_w"]),
        "rq": a["L1_ffn_Wq_w"], "rkeysT": np.transpose(a["L1_ffn_keys"]),
        "ident": np.eye(P, dtype=np.float32),
        "ones": np.ones((P, P), np.float32),
        "blocks": np.kron(np.eye(4, dtype=np.float32), np.ones((32, 32), np.float32)),
        "causal": np.where(allowed, 0.0, -HUGE).astype(np.float32),
    }


def kernel(**inputs):
    import concourse.bacc as _bacc
    from concourse.bass_utils import run_bass_kernel_spmd as _run

    nc = _bacc.Bacc("TRN2", target_bir_lowering=False, num_devices=1, dynamic_dma_scratch_size=1024)
    arrays, args = {}, {}
    for name, a in layouts({k: np.asarray(v) for k, v in inputs.items()}).items():
        a = np.ascontiguousarray(a)
        arrays[f"in_{name}_dram"] = a
        args[name] = nc.dram_tensor(f"in_{name}_dram", a.shape, mybir.dt.from_np(a.dtype), kind="ExternalInput").ap()
    out = nc.dram_tensor("out_0_dram", (B, S, D), F32, kind="ExternalOutput").ap()
    build(nc, args, out)
    r = _run(nc, [arrays], core_ids=[0])
    return r.results[0]["out_0_dram"]
```
